# Optimizing a Trainium2 kernel written in Bass

```python
import numpy as np
import jax
import jax.numpy as jnp

def _softmax(x, axis=-1):
    return jax.nn.softmax(x, axis=axis)

def _gelu(x):
    return jax.nn.gelu(x, approximate=True)

def _silu(x):
    return jax.nn.silu(x)

def _sigmoid(x):
    return jax.nn.sigmoid(x)

def _layernorm(x, axis=-1, eps=1e-05):
    m = jnp.mean(x, axis=axis, keepdims=True)
    v = jnp.var(x, axis=axis, keepdims=True)
    return (x - m) / jnp.sqrt(v + eps)

def _scatter_add(tgt, idx, src, axis=0):
    return tgt.at[idx].add(src)

def _segment_sum(src, seg, n):
    return jax.ops.segment_sum(src, seg, n)
kernel_name = 'mk_early_fusion_embed_d1_tok_img768_r4_24fd2d'

def setup_inputs(seed: int=0):
    np.random.seed(seed)
    _w = jnp.asarray

    def _rec_inputs():
        import jax
        import jax.numpy as jnp
        _rk = jax.random.key(seed)
        x = -9.30917e-05 + 1.0002 * jax.random.normal(jax.random.fold_in(_rk, 1), (64, 3, 84, 84), jnp.float32)
        x_txt = jax.random.randint(jax.random.fold_in(_rk, 51), (64, 32), 0, 12564, jnp.int32)
        return (x, x_txt)
    x, x_txt = _rec_inputs()

    def _L0_tok_setup():
        import jax, jax.numpy as jnp
        import numpy as np
        DN = ('NCHW', 'OIHW', 'NCHW')
        G = 7

        def conv(x, w, stride, pad, groups=1):
            return jax.lax.conv_general_dilated(x, w, (stride, stride), [(pad, pad), (pad, pad)], feature_group_count=groups, dimension_numbers=DN)

        def gelu(x):
            return jax.nn.gelu(x, approximate=False)

        def bn(x, s, b):
            return x * s[None, :, None, None] + b[None, :, None, None]

        def region_layer_dw(x, wdw, sdw, bdw, wpw, spw, bpw):
            B, C, H, W = x.shape
            h, w = (H // G, W // G)
            xr = x.reshape(B, C, G, h, G, w).transpose(0, 2, 4, 1, 3, 5).reshape(B, G * G * C, h, w)
            y = gelu(bn(conv(xr, wdw, 1, 1, groups=G * G * C), sdw, bdw))
            y = bn(conv(y, wpw, 1, 0, groups=G * G), spw, bpw)
            xr = y + xr
            return xr.reshape(B, G, G, C, h, w).transpose(0, 3, 1, 4, 2, 5).reshape(B, C, H, W)
        key = jax.random.key(seed)
        ks = jax.random.split(key, 8)
        B, C0, H, W = (32, 3, 224, 224)
        E = 192
        C1 = E // 16
        C2 = E // 4
        R = G * G
        rn = lambda k, shp, sc: jax.random.normal(k, shp, jnp.float32) * sc
        return {'x': rn(ks[0], (B, C0, H, W), 1.0), 'w0': rn(ks[1], (C1, C0, 3, 3), 0.2), 's0': jnp.ones((C1,), jnp.float32), 'b0': jnp.zeros((C1,), jnp.float32), 'wdw': rn(ks[2], (R * C1, 1, 3, 3), 0.2), 'sdw': jnp.ones((R * C1,), jnp.float32), 'bdw': jnp.zeros((R * C1,), jnp.float32), 'wpw': rn(ks[3], (R * C1, C1, 1, 1), 0.1), 'spw': jnp.ones((R * C1,), jnp.float32), 'bpw': jnp.zeros((R * C1,), jnp.float32), 'w1': rn(ks[4], (C2, C1, 4, 4), 0.05), 's1': jnp.ones((C2,), jnp.float32), 'b1': jnp.zeros((C2,), jnp.float32), 'w2': rn(ks[5], (C2, C2, 2, 2), 0.05), 's2': jnp.ones((C2,), jnp.float32), 'b2': jnp.zeros((C2,), jnp.float32), 'w3': rn(ks[6], (E, C2, 2, 2), 0.05), 's3': jnp.ones((E,), jnp.float32), 'b3': jnp.zeros((E,), jnp.float32)}
    _L0_tok_all = _L0_tok_setup()
    _L0_tok_in = {k: v for k, v in _L0_tok_all.items() if k in ('w0', 's0', 'b0', 'wdw', 'sdw', 'bdw', 'wpw', 'spw', 'bpw', 'w1', 's1', 'b1', 'w2', 's2', 'b2', 'w3', 's3', 'b3')}
    del _L0_tok_all

    def _L0_txt_setup():
        import jax, jax.numpy as jnp
        import numpy as np
        D = 192
        DI = 288
        NUM_LAYERS = 4
        VOCAB = 50257
        MAX_POS = 512
        EPS = 1e-05

        def _layer_norm(x, g, b):
            mu = jnp.mean(x, axis=-1, keepdims=True)
            var = jnp.mean(jnp.square(x - mu), axis=-1, keepdims=True)
            return (x - mu) * jax.lax.rsqrt(var + EPS) * g + b

        def _mamba_block(x, ln_g, ln_b, in_w, conv_w, dt_w, dt_b, out_w, layer_scale):
            residual = x
            xn = _layer_norm(x, ln_g, ln_b)
            xp = jnp.einsum('bld,ed->ble', xn, in_w)
            x1, x2 = (xp[..., :DI], xp[..., DI:])
            x1_ncl = jnp.swapaxes(x1, 1, 2)
            x1_conv = jax.lax.conv_general_dilated(x1_ncl, conv_w, window_strides=(1,), padding=[(1, 1)], dimension_numbers=('NCL', 'OIL', 'NCL'), feature_group_count=DI)
            x1_conv = jnp.swapaxes(x1_conv, 1, 2)
            x1_ssm = jax.nn.silu(x1_conv)
            dt = jax.nn.softplus(jnp.einsum('ble,fe->blf', x1_ssm, dt_w) + dt_b)
            x_gated = x1_ssm * jax.nn.sigmoid(dt) * jax.nn.sigmoid(x2)
            out = jnp.einsum('ble,de->bld', x_gated, out_w) * layer_scale
            return out + residual
        key = jax.random.key(seed)
        ks = jax.random.split(key, 12)
        B, L = (32, 512)
        tokens = jax.random.randint(ks[0], (B, L), 0, VOCAB)
        s_d = 1.0 / np.sqrt(D)
        s_di = 1.0 / np.sqrt(DI)
        return {'tokens': tokens, 'embedding': jax.random.normal(ks[1], (VOCAB, D), jnp.float32) * 0.02, 'pos_encoding': jax.random.normal(ks[2], (1, MAX_POS, D), jnp.float32) * 0.02, 'ln_g': jnp.ones((NUM_LAYERS, D), jnp.float32), 'ln_b': jnp.zeros((NUM_LAYERS, D), jnp.float32), 'in_w': jax.random.uniform(ks[3], (NUM_LAYERS, 2 * DI, D), jnp.float32, -s_d, s_d), 'conv_w': jax.random.uniform(ks[4], (NUM_LAYERS, DI, 1, 3), jnp.float32, -0.577, 0.577), 'dt_w': jax.random.uniform(ks[5], (NUM_LAYERS, DI, DI), jnp.float32, -s_di, s_di), 'dt_b': jax.random.uniform(ks[6], (NUM_LAYERS, DI), jnp.float32, -s_di, s_di), 'out_w': jax.random.uniform(ks[7], (NUM_LAYERS, D, DI), jnp.float32, -s_di, s_di), 'layer_scale': jnp.full((NUM_LAYERS, D), 0.1, jnp.float32), 'final_g': jnp.ones((D,), jnp.float32), 'final_b': jnp.zeros((D,), jnp.float32)}
    _L0_txt_all = _L0_txt_setup()
    _L0_txt_in = {k: v for k, v in _L0_txt_all.items() if k in ('embedding', 'pos_encoding', 'ln_g', 'ln_b', 'in_w', 'conv_w', 'dt_w', 'dt_b', 'out_w', 'layer_scale', 'final_g', 'final_b')}
    del _L0_txt_all

    def _L0_attn_setup():
        import jax, jax.numpy as jnp
        import numpy as np
        HIDDEN = 192
        HEADS = 8
        key = jax.random.key(seed)
        ks = jax.random.split(key, 5)
        b, n = (2, 256)
        x = jax.random.normal(ks[0], (b, n, HIDDEN), dtype=jnp.float32)
        W_qkv = jax.random.normal(ks[1], (HIDDEN, 3 * HIDDEN * HEADS), dtype=jnp.float32) * 0.02
        b_qkv = jnp.zeros((3 * HIDDEN * HEADS,), dtype=jnp.float32)
        W_proj = jax.random.normal(ks[2], (HEADS * HIDDEN, HIDDEN), dtype=jnp.float32) * 0.02
        b_proj = jnp.zeros((HIDDEN,), dtype=jnp.float32)
        return {'x': x, 'W_qkv': W_qkv, 'b_qkv': b_qkv, 'W_proj': W_proj, 'b_proj': b_proj}
    _L0_attn_all = _L0_attn_setup()
    _L0_attn_in = {k: v for k, v in _L0_attn_all.items() if k in ('W_qkv', 'b_qkv', 'W_proj', 'b_proj')}
    del _L0_attn_all

    def _L0_ffn_setup():
        import jax, jax.numpy as jnp
        import numpy as np
        B, S, H, F, E, TOP_K = (4, 512, 192, 768, 8, 2)
        key = jax.random.key(seed)
        ks = jax.random.split(key, 6)
        x = jax.random.normal(ks[0], (B, S, H), dtype=jnp.float32)
        Wr = jax.random.normal(ks[1], (E, H), dtype=jnp.float32) * 0.02
        Wi = jax.random.normal(ks[2], (E, F, H), dtype=jnp.float32) * 0.02
        bi = jnp.zeros((E, F), dtype=jnp.float32)
        Wo = jax.random.normal(ks[3], (E, H, F), dtype=jnp.float32) * 0.02
        bo = jnp.zeros((E, H), dtype=jnp.float32)
        return {'x': x, 'Wr': Wr, 'Wi': Wi, 'bi': bi, 'Wo': Wo, 'bo': bo}
    _L0_ffn_all = _L0_ffn_setup()
    _L0_ffn_in = {k: v for k, v in _L0_ffn_all.items() if k in ('Wr', 'Wi', 'bi', 'Wo', 'bo')}
    del _L0_ffn_all
    return {'x': x, 'x_txt': x_txt, 'L0_tok_w0': _L0_tok_in['w0'], 'L0_tok_s0': _L0_tok_in['s0'], 'L0_tok_b0': _L0_tok_in['b0'], 'L0_tok_wdw': _L0_tok_in['wdw'], 'L0_tok_sdw': _L0_tok_in['sdw'], 'L0_tok_bdw': _L0_tok_in['bdw'], 'L0_tok_wpw': _L0_tok_in['wpw'], 'L0_tok_spw': _L0_tok_in['spw'], 'L0_tok_bpw': _L0_tok_in['bpw'], 'L0_tok_w1': _L0_tok_in['w1'], 'L0_tok_s1': _L0_tok_in['s1'], 'L0_tok_b1': _L0_tok_in['b1'], 'L0_tok_w2': _L0_tok_in['w2'], 'L0_tok_s2': _L0_tok_in['s2'], 'L0_tok_b2': _L0_tok_in['b2'], 'L0_tok_w3': _L0_tok_in['w3'], 'L0_tok_s3': _L0_tok_in['s3'], 'L0_tok_b3': _L0_tok_in['b3'], 'L0_txt_embedding': _L0_txt_in['embedding'], 'L0_txt_pos_encoding': _L0_txt_in['pos_encoding'], 'L0_txt_ln_g': _L0_txt_in['ln_g'], 'L0_txt_ln_b': _L0_txt_in['ln_b'], 'L0_txt_in_w': _L0_txt_in['in_w'], 'L0_txt_conv_w': _L0_txt_in['conv_w'], 'L0_txt_dt_w': _L0_txt_in['dt_w'], 'L0_txt_dt_b': _L0_txt_in['dt_b'], 'L0_txt_out_w': _L0_txt_in['out_w'], 'L0_txt_layer_scale': _L0_txt_in['layer_scale'], 'L0_txt_final_g': _L0_txt_in['final_g'], 'L0_txt_final_b': _L0_txt_in['final_b'], 'L0_attn_W_qkv': _L0_attn_in['W_qkv'], 'L0_attn_b_qkv': _L0_attn_in['b_qkv'], 'L0_attn_W_proj': _L0_attn_in['W_proj'], 'L0_attn_b_proj': _L0_attn_in['b_proj'], 'L0_ffn_Wr': _L0_ffn_in['Wr'], 'L0_ffn_Wi': _L0_ffn_in['Wi'], 'L0_ffn_bi': _L0_ffn_in['bi'], 'L0_ffn_Wo': _L0_ffn_in['Wo'], 'L0_ffn_bo': _L0_ffn_in['bo']}

def reference(x, x_txt, L0_tok_w0, L0_tok_s0, L0_tok_b0, L0_tok_wdw, L0_tok_sdw, L0_tok_bdw, L0_tok_wpw, L0_tok_spw, L0_tok_bpw, L0_tok_w1, L0_tok_s1, L0_tok_b1, L0_tok_w2, L0_tok_s2, L0_tok_b2, L0_tok_w3, L0_tok_s3, L0_tok_b3, L0_txt_embedding, L0_txt_pos_encoding, L0_txt_ln_g, L0_txt_ln_b, L0_txt_in_w, L0_txt_conv_w, L0_txt_dt_w, L0_txt_dt_b, L0_txt_out_w, L0_txt_layer_scale, L0_txt_final_g, L0_txt_final_b, L0_attn_W_qkv, L0_attn_b_qkv, L0_attn_W_proj, L0_attn_b_proj, L0_ffn_Wr, L0_ffn_Wi, L0_ffn_bi, L0_ffn_Wo, L0_ffn_bo):
    import jax
    import jax.numpy as jnp

    def _L0_tok_ref(x, w0, s0, b0, wdw, sdw, bdw, wpw, spw, bpw, w1, s1, b1, w2, s2, b2, w3, s3, b3):
        import jax, jax.numpy as jnp
        import numpy as np
        DN = ('NCHW', 'OIHW', 'NCHW')
        G = 7

        def conv(x, w, stride, pad, groups=1):
            return jax.lax.conv_general_dilated(x, w, (stride, stride), [(pad, pad), (pad, pad)], feature_group_count=groups, dimension_numbers=DN)

        def gelu(x):
            return jax.nn.gelu(x, approximate=False)

        def bn(x, s, b):
            return x * s[None, :, None, None] + b[None, :, None, None]

        def region_layer_dw(x, wdw, sdw, bdw, wpw, spw, bpw):
            B, C, H, W = x.shape
            h, w = (H // G, W // G)
            xr = x.reshape(B, C, G, h, G, w).transpose(0, 2, 4, 1, 3, 5).reshape(B, G * G * C, h, w)
            y = gelu(bn(conv(xr, wdw, 1, 1, groups=G * G * C), sdw, bdw))
            y = bn(conv(y, wpw, 1, 0, groups=G * G), spw, bpw)
            xr = y + xr
            return xr.reshape(B, G, G, C, h, w).transpose(0, 3, 1, 4, 2, 5).reshape(B, C, H, W)
        x = gelu(bn(conv(x, w0, 1, 1), s0, b0))
        x = region_layer_dw(x, wdw, sdw, bdw, wpw, spw, bpw)
        x = gelu(x)
        x = gelu(bn(conv(x, w1, 4, 0), s1, b1))
        x = gelu(bn(conv(x, w2, 2, 0), s2, b2))
        x = bn(conv(x, w3, 2, 0), s3, b3)
        B, E, Hp, Wp = x.shape
        return x.reshape(B, E, Hp * Wp).transpose(0, 2, 1)

    def _L0_txt_ref(tokens, embedding, pos_encoding, ln_g, ln_b, in_w, conv_w, dt_w, dt_b, out_w, layer_scale, final_g, final_b):
        import jax, jax.numpy as jnp
        import numpy as np
        D = 192
        DI = 288
        NUM_LAYERS = 4
        VOCAB = 50257
        MAX_POS = 512
        EPS = 1e-05

        def _layer_norm(x, g, b):
            mu = jnp.mean(x, axis=-1, keepdims=True)
            var = jnp.mean(jnp.square(x - mu), axis=-1, keepdims=True)
            return (x - mu) * jax.lax.rsqrt(var + EPS) * g + b

        def _mamba_block(x, ln_g, ln_b, in_w, conv_w, dt_w, dt_b, out_w, layer_scale):
            residual = x
            xn = _layer_norm(x, ln_g, ln_b)
            xp = jnp.einsum('bld,ed->ble', xn, in_w)
            x1, x2 = (xp[..., :DI], xp[..., DI:])
            x1_ncl = jnp.swapaxes(x1, 1, 2)
            x1_conv = jax.lax.conv_general_dilated(x1_ncl, conv_w, window_strides=(1,), padding=[(1, 1)], dimension_numbers=('NCL', 'OIL', 'NCL'), feature_group_count=DI)
            x1_conv = jnp.swapaxes(x1_conv, 1, 2)
            x1_ssm = jax.nn.silu(x1_conv)
            dt = jax.nn.softplus(jnp.einsum('ble,fe->blf', x1_ssm, dt_w) + dt_b)
            x_gated = x1_ssm * jax.nn.sigmoid(dt) * jax.nn.sigmoid(x2)
            out = jnp.einsum('ble,de->bld', x_gated, out_w) * layer_scale
            return out + residual
        B, L = tokens.shape
        x = embedding[tokens] + pos_encoding[:, :L, :]
        for i in range(NUM_LAYERS):
            x = _mamba_block(x, ln_g[i], ln_b[i], in_w[i], conv_w[i], dt_w[i], dt_b[i], out_w[i], layer_scale[i])
        return _layer_norm(x, final_g, final_b)

    def _L0_attn_ref(x, W_qkv, b_qkv, W_proj, b_proj):
        import jax, jax.numpy as jnp
        import numpy as np
        HIDDEN = 192
        HEADS = 8
        b, n, c = x.shape
        qkv = x @ W_qkv + b_qkv
        q, k, v = jnp.split(qkv, 3, axis=-1)
        q = q.reshape(b, HEADS, n, HIDDEN)
        k = k.reshape(b, HEADS, n, HIDDEN)
        v = v.reshape(b, HEADS, n, HIDDEN)
        energy = jnp.einsum('bhqd,bhkd->bhqk', q, k)
        scaling = jnp.float32(HIDDEN ** 0.5)
        attn = jax.nn.softmax(energy, axis=-1) / scaling
        out = jnp.einsum('bhal,bhlv->bhav', attn, v)
        out = out.reshape(b, n, HEADS * HIDDEN)
        return out @ W_proj + b_proj

    def _L0_ffn_ref(x, Wr, Wi, bi, Wo, bo):
        import jax, jax.numpy as jnp
        import numpy as np
        B, S, H, F, E, TOP_K = (4, 512, 192, 768, 8, 2)
        xf = x.reshape(-1, x.shape[-1])
        router_logits = jnp.einsum('th,eh->te', xf, Wr)
        topk_vals, topk_idx = jax.lax.top_k(router_logits, TOP_K)
        routing_weights = jax.nn.softmax(topk_vals, axis=-1)
        h = jnp.einsum('th,efh->etf', xf, Wi) + bi[:, None, :]
        h = jax.nn.gelu(h, approximate=False)
        expert_out = jnp.einsum('etf,ehf->eth', h, Wo) + bo[:, None, :]
        expert_out = jnp.transpose(expert_out, (1, 0, 2))
        gathered = jnp.take_along_axis(expert_out, topk_idx[:, :, None], axis=1)
        out = jnp.einsum('tk,tkh->th', routing_weights, gathered)
        return out.reshape(x.shape)
    h = _L0_tok_ref(x, L0_tok_w0, L0_tok_s0, L0_tok_b0, L0_tok_wdw, L0_tok_sdw, L0_tok_bdw, L0_tok_wpw, L0_tok_spw, L0_tok_bpw, L0_tok_w1, L0_tok_s1, L0_tok_b1, L0_tok_w2, L0_tok_s2, L0_tok_b2, L0_tok_w3, L0_tok_s3, L0_tok_b3)
    h = jnp.concatenate([h, _L0_txt_ref(x_txt, L0_txt_embedding, L0_txt_pos_encoding, L0_txt_ln_g, L0_txt_ln_b, L0_txt_in_w, L0_txt_conv_w, L0_txt_dt_w, L0_txt_dt_b, L0_txt_out_w, L0_txt_layer_scale, L0_txt_final_g, L0_txt_final_b)], axis=1)
    h = h + _L0_attn_ref(_layernorm(h, axis=-1), L0_attn_W_qkv, L0_attn_b_qkv, L0_attn_W_proj, L0_attn_b_proj)
    h = h + _L0_ffn_ref(_layernorm(h, axis=-1), L0_ffn_Wr, L0_ffn_Wi, L0_ffn_bi, L0_ffn_Wo, L0_ffn_bo)
    return h

_drawn_inputs = setup_inputs


def setup_inputs(seed=0):
    import zlib

    import numpy as np

    out = dict(_drawn_inputs(seed))
    spreads = {'L0_tok_s0': (1.0, 0.2),
     'L0_tok_b0': (0.0, 0.383),
     'L0_tok_sdw': (1.0, 0.6),
     'L0_tok_bdw': (0.0, 0.8),
     'L0_tok_spw': (1.0, 0.6),
     'L0_tok_bpw': (0.0, 0.349),
     'L0_tok_s1': (1.0, 0.2),
     'L0_tok_b1': (0.0, 0.268),
     'L0_tok_s2': (1.0, 0.2),
     'L0_tok_b2': (0.0, 0.1),
     'L0_tok_s3': (1.0, 0.2),
     'L0_tok_b3': (0.0, 0.1),
     'L0_txt_ln_g': (1.0, 0.2),
     'L0_txt_ln_b': (0.0, 0.1),
     'L0_txt_layer_scale': (0.10000000149011612, 0.2),
     'L0_txt_final_g': (1.0, 0.2),
     'L0_txt_final_b': (0.0, 0.1),
     'L0_attn_b_qkv': (0.0, 0.581),
     'L0_attn_b_proj': (0.0, 0.1),
     'L0_ffn_bi': (0.0, 0.317),
     'L0_ffn_bo': (0.0, 0.1)}
    factors = {'L0_tok_wdw': 2.991,
     'L0_tok_wpw': 2.753,
     'L0_txt_dt_w': 8.0,
     'L0_txt_dt_b': 25.51,
     'L0_attn_W_qkv': 3.389,
     'L0_attn_W_proj': 3.529}
    for name, (base, spread) in spreads.items():
        noise = np.random.default_rng([zlib.crc32(name.encode()), seed]).standard_normal(out[name].shape)
        drawn = base * np.exp(spread * noise) if base else spread * noise
        out[name] = jnp.asarray(drawn.astype(out[name].dtype))
    for name, factor in factors.items():
        out[name] = (out[name] * factor).astype(out[name].dtype)
    return out
```

```python
from contextlib import ExitStack

import concourse.bass as bass
from concourse import mybir

F32 = mybir.dt.float32
BF16 = mybir.dt.bfloat16
I32 = mybir.dt.int32
U32 = mybir.dt.uint32
ALU = mybir.AluOpType
ACT = mybir.ActivationFunctionType
AX_X = mybir.AxisListType.X

BATCH = 64
D = 192
HALF = D // 2
TEXT_LEN = 32
IMG_LEN = 25
SEQ = IMG_LEN + TEXT_LEN
TOKENS = BATCH * SEQ
EPS = 1e-5
LN2 = 0.6931471805599453

LAYERS = 4
DI = 288
DI_CHUNKS = DI // HALF


def reached(step, n):
    return not isinstance(step, int) or step >= n


def text_stage(nc, io):
    T = TEXT_LEN
    seqs_per_tile = 128 // T
    tiles = BATCH * T // 128
    TG = 4
    groups = tiles // TG
    N = 128 * TG
    steps = LAYERS * groups
    IN, C = 2 * DI_CHUNKS, DI_CHUNKS

    with ExitStack() as ctx:
        def sb(name, shape, dt=F32):
            return ctx.enter_context(nc.sbuf_tensor("txt_sb_" + name, shape, dt))

        def ps(name, shape):
            return ctx.enter_context(nc.psum_tensor("txt_ps_" + name, shape, F32))

        def sem(name):
            return ctx.enter_context(nc.semaphore("txt_" + name))

        idx = sb("idx", [128, tiles], I32)
        pos = sb("pos", [128, D])
        x = sb("x", [128, tiles, D])
        ident = sb("ident", [128, 128])
        final_g = sb("final_g", [128, D])
        final_b = sb("final_b", [128, D])
        ln_gb = sb("ln_gb", [HALF, LAYERS, 2, 2])
        taps = sb("taps", [HALF, LAYERS, C, 3])
        dt_b = sb("dt_b", [HALF, LAYERS, C])
        dt_bias = sb("dt_bias", [HALF, LAYERS, C])
        in_w = sb("in_w", [HALF, 2, 2 * DI])
        dt_w = sb("dt_w", [HALF, C, DI])
        out_raw = sb("out_raw", [HALF, C + 1, D])
        half_scale = sb("half_scale", [HALF, D])
        out_w = sb("out_w", [HALF, C, D])
        minus_half = sb("minus_half", [128, TG])
        stats = sb("stats", [128, TG, 6])
        mv = sb("mv", [128, 2, TG, 2])
        var_eps = sb("var_eps", [128, TG])
        rstd = sb("rstd", [128, 2, TG])
        xn = sb("xn", [128, TG, D])
        xnT = sb("xnT", [HALF, 2, N])
        conv = sb("conv", [HALF, C, N])
        conv_sg = sb("conv_sg", [HALF, C, N])
        ssm = sb("ssm", [HALF, 2, C, N])
        x2_sg = sb("x2_sg", [HALF, 2, C, N])
        dt_sg = sb("dt_sg", [HALF, C, N])
        gate = sb("gate", [HALF, C, N])
        xg = sb("xg", [HALF, C, N])
        turn_ps = ps("turn_ps", [HALF, 2, 512])
        ring_ps = ps("ring_ps", [HALF, 4, 512])
        out_ps = ps("out_ps", [128, TG, 256])

        idx_loaded = sem("idx_loaded")
        const_loaded = sem("const_loaded")
        wait_carrier = sem("wait_carrier")
        gathered = sem("gathered")
        embedded = sem("embedded")
        consts_set = sem("consts_set")
        dt_bias_set = sem("dt_bias_set")
        in_w_loaded = sem("in_w_loaded")
        dt_w_loaded = sem("dt_w_loaded")
        out_raw_loaded = sem("out_raw_loaded")
        scale_halved = sem("scale_halved")
        out_w_ready = sem("out_w_ready")
        stats_done = sem("stats_done")
        var_ready = sem("var_ready")
        eps_added = sem("eps_added")
        rstd_ready = sem("rstd_ready")
        normed = sem("normed")
        turned = sem("turned")
        xnT_ready = sem("xnT_ready")
        in_done = sem("in_done")
        conv_tap = sem("conv_tap")
        conv_done = sem("conv_done")
        conv_sg_done = sem("conv_sg_done")
        x2_sg_done = sem("x2_sg_done")
        ssm_ready = sem("ssm_ready")
        dt_done = sem("dt_done")
        dt_sg_done = sem("dt_sg_done")
        gate_done = sem("gate_done")
        xg_ready = sem("xg_ready")
        out_done = sem("out_done")
        added = sem("added")
        scaled = sem("scaled")
        final_ready = sem("final_ready")
        h_stored = sem("h_stored")

        def over_steps(eng, body):
            for g in range(groups):
                body(g, 0, g)
            with eng.Fori(1, LAYERS - 1) as layer:
                for g in range(groups):
                    body(layer * groups + g, layer, g)
            for g in range(groups):
                body((LAYERS - 1) * groups + g, LAYERS - 1, g)

        def next_layer(layer, g):
            return layer + 1 if g == groups - 1 else layer

        block = ctx.enter_context(nc.Block())

        @block.sync
        def _(sp):
            sp.dma_start(idx[:], io["txt_idx"]).then_inc(idx_loaded, 16)
            for dst, name in ((pos, "txt_pos"), (ident, "ident"), (final_g, "txt_final_g"), (final_b, "txt_final_b"),
                              (ln_gb, "txt_ln_gb"), (taps, "txt_taps"), (dt_b, "txt_dt_b")):
                sp.dma_start(dst[:], io[name]).then_inc(const_loaded, 16)

            def load_layer(layer):
                if reached(layer, 1):
                    sp.wait_ge(in_done, layer * (groups * IN))
                    sp.sem_inc(wait_carrier, 1)
                sp.dma_start(in_w[:], io["txt_in_w"][layer]).then_inc(in_w_loaded, 16)
                if reached(layer, 1):
                    sp.wait_ge(out_w_ready, layer)
                    sp.sem_inc(wait_carrier, 1)
                sp.dma_start(out_raw[:], io["txt_out_w"][layer]).then_inc(out_raw_loaded, 16)
                if reached(layer, 1):
                    sp.wait_ge(dt_done, layer * (groups * C))
                    sp.sem_inc(wait_carrier, 1)
                sp.dma_start(dt_w[:], io["txt_dt_w"][layer]).then_inc(dt_w_loaded, 16)

            load_layer(0)
            with sp.Fori(1, LAYERS) as layer:
                load_layer(layer)
            with sp.Fori(0, groups) as g:
                sp.wait_ge(final_ready, g + 1)
                sp.sem_inc(wait_carrier, 1)
                for t in range(TG):
                    for b in range(seqs_per_tile):
                        seq = (g * TG + t) * seqs_per_tile + b
                        sp.dma_start(io["h"][bass.ds(seq * SEQ + IMG_LEN, T), :],
                                     x[b * T:(b + 1) * T, g * TG + t, :]).then_inc(h_stored, 16)
            sp.wait_ge(h_stored, 16 * BATCH)

        @block.gpsimd
        def _(pool):
            pool.wait_ge(idx_loaded, 16)
            for t in range(tiles):
                pool.indirect_dma_start(
                    out=x[:, t, :], out_offset=None, in_=io["embedding"],
                    in_offset=bass.IndirectOffsetOnAxis(ap=idx[:, t:t + 1].bitcast(U32), axis=0),
                ).then_inc(gathered, 16)
            pool.memset(minus_half[:], -0.5).then_inc(consts_set, 1)
            pool.wait_ge(consts_set, 1)
            pool.wait_ge(const_loaded, 16 * 7)
            pool.tensor_scalar(dt_bias[:], dt_b[:], -LN2, None, ALU.add).then_inc(dt_bias_set, 1)

            def inverse_deviation(n, par):
                pool.wait_ge(var_ready, n + 1)
                pool.sem_inc(wait_carrier, 1)
                pool.tensor_scalar(var_eps[:], mv[:, par, :, 1], EPS, None, ALU.add).then_inc(eps_added, 1)
                pool.wait_ge(eps_added, n + 1)
                pool.tensor_tensor(rstd[:, par, :], var_eps[:], minus_half[:], ALU.pow).then_inc(rstd_ready, 1)

            def scale_out_weights(layer):
                pool.wait_ge(out_raw_loaded, (layer + 1) * 16)
                pool.sem_inc(wait_carrier, 1)
                pool.tensor_scalar(half_scale[:], out_raw[:, C, :], 0.5, None, ALU.mult).then_inc(scale_halved, 1)
                pool.wait_ge(scale_halved, layer + 1)
                if reached(layer, 1):
                    pool.wait_ge(out_done, layer * groups)
                for c in range(C):
                    last = pool.tensor_tensor(out_w[:, c, :], out_raw[:, c, :], half_scale[:], ALU.mult)
                last.then_inc(out_w_ready, 1)

            inverse_deviation(0, 0)
            scale_out_weights(0)

            def step(i, layer, g):
                if not (isinstance(i, int) and i == steps - 1):
                    inverse_deviation(i + 1, (g + 1) % 2)
                if g == 1 and reached(layer, 1):
                    scale_out_weights(layer)

            over_steps(pool, step)
            for g in range(groups):
                inverse_deviation(steps + g, g % 2)

        @block.tensor
        def _(pe):
            def turn(i, g):
                pe.wait_ge(normed, i + 1)
                if reached(i, 1):
                    pe.wait_ge(xnT_ready, i * 2)
                for h in range(2):
                    for t in range(TG):
                        last = pe.transpose(turn_ps[:, h, t * 128:(t + 1) * 128],
                                            xn[:, t, h * HALF:(h + 1) * HALF], ident[:])
                    last.then_inc(turned, 1)

            def ring_free(i, k):
                if k == 0:
                    if reached(i, 1):
                        pe.wait_ge(x2_sg_done, i * C)
                elif k < 4:
                    if reached(i, 2):
                        pe.wait_ge(dt_sg_done, (i - 2) * C + k)
                elif k < 7:
                    pe.wait_ge(conv_done, i * C + (k - 3))
                else:
                    pe.wait_ge(x2_sg_done, i * C + (k - 6))

            def in_projection(i, layer, g):
                if g == 0:
                    pe.wait_ge(in_w_loaded, (layer + 1) * 16)
                pe.wait_ge(xnT_ready, (i + 1) * 2)
                for k in range(IN):
                    ring_free(i, k)
                    for h in range(2):
                        mm = pe.matmul(ring_ps[:, (g * (IN + C) + k) % 4, :], in_w[:, h, k * HALF:(k + 1) * HALF],
                                       xnT[:, h, :], start=(h == 0), stop=(h == 1))
                    mm.then_inc(in_done, 1)

            def dt_product(i, g_now, layer, g, free):
                if g == 0:
                    pe.wait_ge(dt_w_loaded, (layer + 1) * 16)
                pe.wait_ge(ssm_ready, (i + 1) * C)
                for m in range(C):
                    free(m)
                    for c in range(C):
                        mm = pe.matmul(ring_ps[:, (g_now * (IN + C) + IN + m) % 4, :], dt_w[:, c, m * HALF:(m + 1) * HALF],
                                       ssm[:, g % 2, c, :], start=(c == 0), stop=(c == C - 1))
                    mm.then_inc(dt_done, 1)

            def out_product(i, layer, g):
                if g == 0:
                    pe.wait_ge(out_w_ready, layer + 1)
                pe.wait_ge(xg_ready, (i + 1) * C)
                if reached(i, 1):
                    pe.wait_ge(added, i)
                for t in range(TG):
                    for c in range(C):
                        mm = pe.matmul(out_ps[:, t, 0:D], xg[:, c, t * 128:(t + 1) * 128], out_w[:, c, :],
                                       start=(c == 0), stop=(c == C - 1))
                mm.then_inc(out_done, 1)

            pe.wait_ge(const_loaded, 16 * 7)
            turn(0, 0)

            def step(i, layer, g):
                in_projection(i, layer, g)
                if reached(i, 2):
                    out_product(i - 2, layer if g >= 2 else layer - 1, (g - 2) % groups)
                if not (isinstance(i, int) and i == steps - 1):
                    turn(i + 1, (g + 1) % groups)
                if reached(i, 1):
                    dt_product(i - 1, g, layer if g >= 1 else layer - 1, (g - 1) % groups,
                               lambda m: ring_free(i, IN + m))

            over_steps(pe, step)
            out_product(steps - 2, LAYERS - 1, groups - 2)
            pe.wait_ge(conv_done, steps * C)
            pe.wait_ge(x2_sg_done, steps * C)
            pe.wait_ge(dt_sg_done, (steps - 1) * C)
            dt_product(steps - 1, 0, LAYERS - 1, groups - 1, lambda m: None)
            out_product(steps - 1, LAYERS - 1, groups - 1)

        @block.scalar
        def _(act):
            def take_turned(i, layer):
                if reached(i, 1):
                    act.wait_ge(in_done, i * IN)
                for h in range(2):
                    act.wait_ge(turned, i * 2 + (h + 1))
                    act.sem_inc(wait_carrier, 1)
                    act.activation(xnT[:, h, :], turn_ps[:, h, :], ACT.Identity, scale=ln_gb[:, layer, 0, h:h + 1],
                                   bias=ln_gb[:, layer, 1, h:h + 1]).then_inc(xnT_ready, 1)

            def gate_sigmoids(i, layer, g, slot_g):
                for m in range(C):
                    act.wait_ge(dt_done, i * C + (m + 1))
                    if m == 0 and reached(i, 1):
                        act.wait_ge(gate_done, i * C)
                    act.sem_inc(wait_carrier, 1)
                    act.activation(dt_sg[:, m, :], ring_ps[:, (slot_g * (IN + C) + IN + m) % 4, :], ACT.Sigmoid,
                                   bias=dt_bias[:, layer, m:m + 1]).then_inc(dt_sg_done, 1)

            act.wait_ge(const_loaded, 16 * 7)
            act.wait_ge(dt_bias_set, 1)
            take_turned(0, 0)

            def step(i, layer, g):
                for c in range(C):
                    act.wait_ge(in_done, i * IN + (C + c + 1))
                    if c == 0 and reached(i, 2):
                        act.wait_ge(xg_ready, (i - 1) * C)
                    act.activation(x2_sg[:, g % 2, c, :], ring_ps[:, (g * (IN + C) + C + c) % 4, :],
                                   ACT.Sigmoid).then_inc(x2_sg_done, 1)
                for c in range(C):
                    act.wait_ge(conv_done, i * C + (c + 1))
                    if c == 0 and reached(i, 1):
                        act.wait_ge(ssm_ready, i * C)
                    act.activation(conv_sg[:, c, :], conv[:, c, :], ACT.Sigmoid).then_inc(conv_sg_done, 1)
                if not (isinstance(i, int) and i == steps - 1):
                    take_turned(i + 1, next_layer(layer, g))
                if reached(i, 1):
                    gate_sigmoids(i - 1, layer if g >= 1 else layer - 1, (g - 1) % groups, g)

            over_steps(act, step)
            gate_sigmoids(steps - 1, LAYERS - 1, groups - 1, 0)

        @block.vector
        def _(dve):
            def statistics(n, g, par):
                for t in range(TG):
                    s = dve.bn_stats(stats[:, t, :], x[:, g * TG + t, :])
                s.then_inc(stats_done, 1)
                dve.wait_ge(stats_done, n + 1)
                dve.sem_inc(wait_carrier, 1)
                for t in range(TG):
                    s = dve.bn_aggr(mv[:, par, t, :], stats[:, t, :])
                s.then_inc(var_ready, 1)

            def normalise(n, g, par):
                dve.wait_ge(rstd_ready, n + 1)
                if reached(n, 1):
                    dve.wait_ge(turned, n * 2)
                for t in range(TG):
                    s = dve.tensor_scalar(xn[:, t, :], x[:, g * TG + t, :], mv[:, par, t, 0:1], rstd[:, par, t:t + 1],
                                          ALU.subtract, ALU.mult)
                s.then_inc(normed, 1)

            def convolve(i, layer, g):
                for c in range(C):
                    seq = ring_ps[:, (g * (IN + C) + c) % 4, :].rearrange("p (s l) -> p s l", l=T)
                    out = conv[:, c, :].rearrange("p (s l) -> p s l", l=T)
                    dve.wait_ge(in_done, i * IN + (c + 1))
                    dve.tensor_scalar(out, seq, taps[:, layer, c, 1:2], None, ALU.mult).then_inc(conv_tap, 1)
                    dve.wait_ge(conv_tap, i * (2 * C) + (2 * c + 1))
                    dve.scalar_tensor_tensor(out[:, :, 1:T], seq[:, :, 0:T - 1], taps[:, layer, c, 0:1], out[:, :, 1:T],
                                             ALU.mult, ALU.add).then_inc(conv_tap, 1)
                    dve.wait_ge(conv_tap, i * (2 * C) + (2 * c + 2))
                    dve.scalar_tensor_tensor(out[:, :, 0:T - 1], seq[:, :, 1:T], taps[:, layer, c, 2:3], out[:, :, 0:T - 1],
                                             ALU.mult, ALU.add).then_inc(conv_done, 1)

            def silu(i, g):
                if reached(i, 2):
                    dve.wait_ge(dt_done, (i - 1) * C)
                for c in range(C):
                    dve.wait_ge(conv_sg_done, i * C + (c + 1))
                    dve.tensor_tensor(ssm[:, g % 2, c, :], conv[:, c, :], conv_sg[:, c, :],
                                      ALU.mult).then_inc(ssm_ready, 1)

            def apply_gate(i, g):
                if reached(i, 1):
                    dve.wait_ge(out_done, i)
                for c in range(C):
                    dve.wait_ge(dt_sg_done, i * C + (c + 1))
                    dve.scalar_tensor_tensor(gate[:, c, :], dt_sg[:, c, :], 1.0, x2_sg[:, g % 2, c, :],
                                             ALU.add, ALU.mult).then_inc(gate_done, 1)
                for c in range(C):
                    dve.wait_ge(gate_done, i * C + (c + 1))
                    dve.tensor_tensor(xg[:, c, :], gate[:, c, :], ssm[:, g % 2, c, :], ALU.mult).then_inc(xg_ready, 1)

            def add_residual(i, g):
                dve.wait_ge(out_done, i + 1)
                dve.tensor_tensor(x[:, g * TG:(g + 1) * TG, :], x[:, g * TG:(g + 1) * TG, :], out_ps[:, :, 0:D],
                                  ALU.add).then_inc(added, 1)

            dve.wait_ge(const_loaded, 16 * 7)
            for t in range(tiles):
                dve.wait_ge(gathered, 16 * tiles)
                dve.tensor_tensor(x[:, t, :], x[:, t, :], pos[:], ALU.add).then_inc(embedded, 1)
            dve.wait_ge(embedded, tiles)
            statistics(0, 0, 0)
            normalise(0, 0, 0)

            def step(i, layer, g):
                more = not (isinstance(i, int) and i == steps - 1)
                if more:
                    if reached(i, 3):
                        dve.wait_ge(added, i - 2)
                    statistics(i + 1, (g + 1) % groups, (g + 1) % 2)
                convolve(i, layer, g)
                if reached(i, 2):
                    add_residual(i - 2, (g - 2) % groups)
                if more:
                    normalise(i + 1, (g + 1) % groups, (g + 1) % 2)
                silu(i, g)
                if reached(i, 1):
                    apply_gate(i - 1, (g - 1) % groups)

            over_steps(dve, step)
            add_residual(steps - 2, groups - 2)
            apply_gate(steps - 1, groups - 1)
            add_residual(steps - 1, groups - 1)

            for g in range(groups):
                dve.wait_ge(added, steps)
                statistics(steps + g, g, g % 2)
                dve.wait_ge(rstd_ready, steps + g + 1)
                if g == 0:
                    dve.wait_ge(turned, 2 * steps)
                else:
                    dve.wait_ge(scaled, g)
                for t in range(TG):
                    s = dve.tensor_scalar(xn[:, t, :], x[:, g * TG + t, :], mv[:, g % 2, t, 0:1],
                                          rstd[:, g % 2, t:t + 1], ALU.subtract, ALU.mult)
                s.then_inc(normed, 1)
                dve.wait_ge(normed, steps + g + 1)
                for t in range(TG):
                    s = dve.tensor_tensor(x[:, g * TG + t, :], xn[:, t, :], final_g[:], ALU.mult)
                s.then_inc(scaled, 1)
                dve.wait_ge(scaled, g + 1)
                for t in range(TG):
                    s = dve.tensor_tensor(x[:, g * TG + t, :], x[:, g * TG + t, :], final_b[:], ALU.add)
                s.then_inc(final_ready, 1)


PAIR = 2 * SEQ
HEADS = 8
TILES = TOKENS // PAIR
SCALING = float(D) ** 0.5


def attention_stage(nc, io, h1):
    GB = 4
    GT = GB * SEQ
    groups = BATCH // GB
    ROWS = SEQ * HEADS
    PAIRS = ROWS // PAIR
    BLOCKS = 3 * HEADS // 2 * 3
    SLOTS = BLOCKS + 1
    BPS = BLOCKS // GB
    BIG, SMALL = 128, D - 128

    with ExitStack() as ctx:
        def sb(name, shape, dt=F32):
            return ctx.enter_context(nc.sbuf_tensor("att_sb_" + name, shape, dt))

        def ps(name, shape):
            return ctx.enter_context(nc.psum_tensor("att_ps_" + name, shape, F32))

        def sem(name):
            return ctx.enter_context(nc.semaphore("att_" + name))

        ident = sb("ident", [128, 128])
        qkv_w = sb("qkv_w", [HALF, 2, BLOCKS, 128])
        qkv_b = sb("qkv_b", [128, BLOCKS])
        proj_w = sb("proj_w", [HALF, 2 * HEADS, D])
        proj_b = sb("proj_b", [PAIR, D])
        mask_f = sb("mask_f", [2, 2, PAIR])
        mask = sb("mask", [2, 2, PAIR], BF16)
        h_in = sb("h_in", [PAIR, 2, 2, D])
        minus_half = sb("minus_half", [PAIR, 2])
        stats = sb("stats", [PAIR, 2, 6])
        mv = sb("mv", [PAIR, 2, 2])
        var_eps = sb("var_eps", [PAIR, 2])
        rstd = sb("rstd", [PAIR, 2])
        xn = sb("xn", [PAIR, 2, D])
        xnT = sb("xnT", [HALF, 2, GT])
        big = sb("big", [BIG, 2, 3, GT * HEADS])
        small = sb("small", [SMALL, 2, 3, GT * HEADS])
        v_rows = sb("v_rows", [PAIR, PAIRS, D])
        row_max = sb("row_max", [PAIR, PAIRS])
        row_sum = sb("row_sum", [PAIR, PAIRS])
        sum_scaled = sb("sum_scaled", [PAIR, PAIRS])
        inv_sum = sb("inv_sum", [PAIR, PAIRS])
        probs = sb("probs", [PAIR, 2, PAIRS, PAIR])
        probsT = sb("probsT", [PAIR, PAIRS, PAIR])
        outT = sb("outT", [HALF, 2, 2, 2 * ROWS])
        ring_ps = ps("ring_ps", [128, 2, 512])
        score_ps = ps("score_ps", [PAIR, 512])
        v_ps = ps("v_ps", [PAIR, 2, 256])
        probsT_ps = ps("probsT_ps", [PAIR, 512])
        out_ps = ps("out_ps", [HALF, 2, 512])
        proj_ps = ps("proj_ps", [PAIR, 512])

        const_loaded = sem("const_loaded")
        wait_carrier = sem("wait_carrier")
        qkv_w_loaded = sem("qkv_w_loaded")
        h_loaded = [sem("h_loaded_even"), sem("h_loaded_odd")]
        half_set = sem("half_set")
        mask_ready = sem("mask_ready")
        stats_done = sem("stats_done")
        var_ready = sem("var_ready")
        eps_added = sem("eps_added")
        rstd_ready = sem("rstd_ready")
        normed = sem("normed")
        h_biased = sem("h_biased")
        ring_done = sem("ring_done")
        ring_read = sem("ring_read")
        scored = sem("scored")
        max_done = sem("max_done")
        shifted = sem("shifted")
        exp_done = sem("exp_done")
        sum_step = sem("sum_step")
        probs_ready = sem("probs_ready")
        probs_turned = sem("probs_turned")
        probsT_ready = sem("probsT_ready")
        v_turned = sem("v_turned")
        v_ready = sem("v_ready")
        out_done = sem("out_done")
        outT_ready = sem("outT_ready")
        proj_done = sem("proj_done")
        h1_ready = sem("h1_ready")

        def over_groups(eng, body):
            body(0, 0)
            body(1, 1)
            with eng.Fori(1, groups // 2 - 1) as k:
                body(k * 2, 0)
                body(k * 2 + 1, 1)
            body(groups - 2, 0)
            body(groups - 1, 1)

        def exists(group, ahead):
            return not (isinstance(group, int) and group + ahead >= groups)

        block = ctx.enter_context(nc.Block())

        @block.sync
        def _(sp):
            def load(group, par):
                if reached(group, 2):
                    sp.wait_ge(h_biased, group - 1)
                    sp.wait_ge(normed, group - 1)
                    sp.sem_inc(wait_carrier, 1)
                sp.dma_start(h_in[:, par], io["h"][bass.ds(group * GT, GT), :].rearrange("(t p) d -> p t d", p=PAIR)
                             ).then_inc(h_loaded[par], 16)

            load(0, 0)
            load(1, 1)
            for dst, name in ((ident, "ident"), (qkv_b, "qkv_b"), (proj_b, "proj_b"), (mask_f, "mask"),
                              (proj_w, "proj_w")):
                sp.dma_start(dst[:], io[name]).then_inc(const_loaded, 16)
            sp.dma_start(qkv_w[:], io["qkv_w"]).then_inc(qkv_w_loaded, 16)
            with sp.Fori(1, groups // 2) as k:
                load(k * 2, 0)
                load(k * 2 + 1, 1)

        @block.gpsimd
        def _(pool):
            pool.memset(minus_half[:], -0.5).then_inc(half_set, 1)
            pool.wait_ge(half_set, 1)
            pool.wait_ge(const_loaded, 16 * 5)

            def body(group, par, turn_of_loop):
                pool.wait_ge(var_ready, group + 1)
                pool.sem_inc(wait_carrier, 1)
                pool.tensor_scalar(var_eps[:], mv[:, :, 1], EPS, None, ALU.add).then_inc(eps_added, 1)
                pool.wait_ge(eps_added, group + 1)
                if reached(group, 1):
                    pool.wait_ge(normed, group)
                pool.tensor_tensor(rstd[:], var_eps[:], minus_half[:], ALU.pow).then_inc(rstd_ready, 1)
                pool.wait_ge(h_loaded[par], (turn_of_loop + 1) * 16)
                for t in range(2):
                    last = pool.tensor_tensor(h1[:, group * 2 + t, :], h_in[:, par, t, :], proj_b[:], ALU.add)
                last.then_inc(h_biased, 1)

            with pool.Fori(0, groups // 2) as k:
                body(k * 2, 0, k)
                body(k * 2 + 1, 1, k)

        @block.tensor
        def _(pe):
            def ring_slot(group, par, s):
                n = group * SLOTS + s
                if not (isinstance(n, int) and n < 2):
                    pe.wait_ge(ring_read, n - 1)
                return ring_ps[:, (par * SLOTS + s) % 2, :]

            def turn(group, par):
                pe.wait_ge(normed, group + 1)
                slot = ring_slot(group, par, 0)
                for h in range(2):
                    for t in range(2):
                        last = pe.transpose(slot[0:HALF, h * GT + t * PAIR:h * GT + (t + 1) * PAIR],
                                            xn[:, t, h * HALF:(h + 1) * HALF], ident[0:PAIR, 0:PAIR])
                last.then_inc(ring_done, 1)

            def project_in(group, par, blocks):
                for blk in blocks:
                    slot = ring_slot(group, par, 1 + blk)
                    if blk == 0:
                        pe.wait_ge(ring_read, group * SLOTS + 1)
                    for h in range(2):
                        mm = pe.matmul(slot[:, 0:GT], qkv_w[:, h, blk, :], xnT[:, h, :], start=(h == 0), stop=(h == 1))
                    mm.then_inc(ring_done, 1)

            def scores(b, par, j):
                if reached(b, 1):
                    pe.wait_ge(shifted, b)
                for p in range(PAIRS):
                    r = slice(j * ROWS + p * PAIR, j * ROWS + (p + 1) * PAIR)
                    out = score_ps[:, p * PAIR:(p + 1) * PAIR]
                    pe.matmul(out, mask[:, 0, :], mask[:, 1, :], start=True, stop=False)
                    pe.matmul(out, big[:, par, 0, r], big[:, par, 1, r], start=False, stop=False)
                    mm = pe.matmul(out, small[:, par, 0, r], small[:, par, 1, r], start=False, stop=True)
                mm.then_inc(scored, 1)

            def turn_probs(b, j):
                pe.wait_ge(probs_ready, b + 1)
                if reached(b, 1):
                    pe.wait_ge(probsT_ready, b)
                for p in range(PAIRS):
                    last = pe.transpose(probsT_ps[:, p * PAIR:(p + 1) * PAIR], probs[:, j % 2, p, :],
                                        ident[0:PAIR, 0:PAIR])
                last.then_inc(probs_turned, 1)

            def turn_values(b, par, j):
                for rnd in range(2):
                    if reached(b, 1) or rnd:
                        pe.wait_ge(v_ready, b * 2 + rnd)
                    for p in range(2):
                        at = j * ROWS + (2 * rnd + p) * PAIR
                        pe.transpose(v_ps[:, p, 0:BIG], big[:, par, 2, at:at + PAIR], ident[:])
                        last = pe.transpose(v_ps[:, p, BIG:D], small[:, par, 2, at:at + PAIR], ident[0:SMALL, 0:SMALL])
                    last.then_inc(v_turned, 1)

            def mix_values(b, j):
                pe.wait_ge(probsT_ready, b + 1)
                pe.wait_ge(v_ready, b * 2 + 2)
                if reached(b, 1):
                    pe.wait_ge(outT_ready, b)
                for h in range(2):
                    for p in range(PAIRS):
                        mm = pe.matmul(out_ps[:, h, p * PAIR:(p + 1) * PAIR], v_rows[:, p, h * HALF:(h + 1) * HALF],
                                       probsT[:, p, :], start=True, stop=True)
                mm.then_inc(out_done, 1)

            def project_out(pair, pair_par):
                pe.wait_ge(outT_ready, pair * 2 + 2)
                if reached(pair, 1):
                    pe.wait_ge(h1_ready, pair)
                rows = outT[:, pair_par].rearrange("p h (n c) -> p h c n", c=HEADS)
                for c in range(HEADS):
                    for h in range(2):
                        mm = pe.matmul(proj_ps[:, 0:D], rows[:, h, c, :], proj_w[:, 2 * c + h, :],
                                       start=(c + h == 0), stop=(c == HEADS - 1 and h == 1))
                mm.then_inc(proj_done, 1)

            def body(group, par):
                for j in range(GB):
                    b = group * GB + j
                    if j == 0:
                        if exists(group, 1):
                            turn(group + 1, 1 - par)
                        pe.wait_ge(ring_read, (group + 1) * SLOTS)
                    scores(b, par, j)
                    if j % 2 == 0 and reached(b, 2):
                        project_out(group * 2 + (j // 2 - 1), (j // 2 + 1) % 2)
                    if exists(group, 1):
                        project_in(group + 1, 1 - par, range(j * BPS, j * BPS + 5))
                    turn_probs(b, j)
                    turn_values(b, par, j)
                    if exists(group, 1):
                        project_in(group + 1, 1 - par, range(j * BPS + 5, (j + 1) * BPS))
                    mix_values(b, j)

            pe.wait_ge(const_loaded, 16 * 5)
            turn(0, 0)
            pe.wait_ge(mask_ready, 1)
            pe.wait_ge(qkv_w_loaded, 16)
            project_in(0, 0, range(BLOCKS))
            over_groups(pe, body)
            project_out(TILES - 1, 1)

        @block.scalar
        def _(act):
            def take_turned(group, par):
                act.wait_ge(ring_done, group * SLOTS + 1)
                act.activation(xnT[:].rearrange("p h n -> p (h n)"), ring_ps[0:HALF, (par * SLOTS) % 2, 0:2 * GT],
                               ACT.Copy).then_inc(ring_read, 1)

            def take_blocks(group, par, blocks):
                for blk in blocks:
                    kind, rest = divmod(blk, BLOCKS // 3)
                    cp, third = divmod(rest, 3)
                    slot = ring_ps[:, (par * SLOTS + 1 + blk) % 2, 0:GT]
                    wide = big[:, par, kind, :].rearrange("p (n c) -> p c n", c=HEADS)
                    narrow = small[:, par, kind, :].rearrange("p (n c) -> p c n", c=HEADS)
                    act.wait_ge(ring_done, group * SLOTS + (2 + blk))
                    if blk == 0 and reached(group, 2):
                        act.wait_ge(scored, (group - 1) * GB)
                        act.wait_ge(v_turned, (group - 1) * (2 * GB))
                    if third < 2:
                        act.activation(wide[:, 2 * cp + third, :], slot, ACT.Identity,
                                       bias=qkv_b[:, blk:blk + 1]).then_inc(ring_read, 1)
                    else:
                        act.activation(narrow[:, 2 * cp, :], slot[0:SMALL, :], ACT.Identity,
                                       bias=qkv_b[0:SMALL, blk:blk + 1])
                        act.activation(narrow[:, 2 * cp + 1, :], slot[SMALL:128, :], ACT.Identity,
                                       bias=qkv_b[SMALL:128, blk:blk + 1]).then_inc(ring_read, 1)

            def body(group, par):
                for j in range(GB):
                    b = group * GB + j
                    more = exists(group, 1)
                    if j == 0 and more:
                        take_turned(group + 1, 1 - par)
                    if more:
                        take_blocks(group + 1, 1 - par, range(j * BPS, j * BPS + 2))
                    act.wait_ge(shifted, b + 1)
                    act.activation(probs[:, j % 2], probs[:, j % 2], ACT.Exp).then_inc(exp_done, 1)
                    if more:
                        take_blocks(group + 1, 1 - par, range(j * BPS + 2, (j + 1) * BPS))
                    act.wait_ge(out_done, b + 1)
                    pair = group * 2 + j // 2
                    if j % 2 == 0 and reached(pair, 2):
                        act.wait_ge(proj_done, pair - 1)
                    act.activation(outT[:, (j // 2) % 2, :, (j % 2) * ROWS:(j % 2 + 1) * ROWS], out_ps[:, :, 0:ROWS],
                                   ACT.Copy).then_inc(outT_ready, 1)

            act.wait_ge(const_loaded, 16 * 5)
            take_turned(0, 0)
            take_blocks(0, 0, range(BLOCKS))
            over_groups(act, body)

        @block.vector
        def _(dve):
            def statistics(group, par, count):
                dve.wait_ge(h_loaded[par], count * 16)
                for t in range(2):
                    s = dve.bn_stats(stats[:, t, :], h_in[:, par, t, :])
                s.then_inc(stats_done, 1)
                dve.wait_ge(stats_done, group + 1)
                if reached(group, 1):
                    dve.wait_ge(rstd_ready, group)
                dve.sem_inc(wait_carrier, 1)
                for t in range(2):
                    s = dve.bn_aggr(mv[:, t, :], stats[:, t, :])
                s.then_inc(var_ready, 1)

            def normalise(group, par):
                dve.wait_ge(rstd_ready, group + 1)
                if reached(group, 1):
                    dve.wait_ge(ring_done, (group - 1) * SLOTS + 1)
                for t in range(2):
                    s = dve.tensor_scalar(xn[:, t, :], h_in[:, par, t, :], mv[:, t, 0:1], rstd[:, t:t + 1],
                                          ALU.subtract, ALU.mult)
                s.then_inc(normed, 1)

            def add_residual(pair):
                dve.wait_ge(proj_done, pair + 1)
                dve.tensor_tensor(h1[:, pair, :], h1[:, pair, :], proj_ps[:, 0:D], ALU.add).then_inc(h1_ready, 1)

            def wide(small_tile):
                return small_tile[:].unsqueeze(2).to_broadcast([PAIR, PAIRS, PAIR])

            def body(group, par, k):
                for j in range(GB):
                    b = group * GB + j
                    p = probs[:, j % 2]
                    score = score_ps[:, 0:ROWS].rearrange("q (p k) -> q p k", k=PAIR)
                    dve.wait_ge(scored, b + 1)
                    dve.tensor_reduce(row_max[:], score, AX_X, ALU.max).then_inc(max_done, 1)
                    dve.wait_ge(max_done, b + 1)
                    if reached(b, 2):
                        dve.wait_ge(probs_turned, b - 1)
                    dve.tensor_tensor(p, score, wide(row_max), ALU.subtract).then_inc(shifted, 1)
                    if j % 2 == 0 and reached(b, 2):
                        if j == 0:
                            dve.wait_ge(h_biased, group)
                        else:
                            dve.wait_ge(h_biased, group + 1)
                        add_residual(group * 2 + (j // 2 - 1))
                    dve.wait_ge(exp_done, b + 1)
                    dve.tensor_reduce(row_sum[:], p, AX_X, ALU.add).then_inc(sum_step, 1)
                    dve.wait_ge(sum_step, b * 3 + 1)
                    dve.tensor_scalar(sum_scaled[:], row_sum[:], SCALING, None, ALU.mult).then_inc(sum_step, 1)
                    dve.wait_ge(sum_step, b * 3 + 2)
                    dve.reciprocal(inv_sum[:], sum_scaled[:]).then_inc(sum_step, 1)
                    dve.wait_ge(sum_step, b * 3 + 3)
                    dve.tensor_tensor(p, p, wide(inv_sum), ALU.mult).then_inc(probs_ready, 1)
                    if j == 2 and exists(group, 2):
                        statistics(group + 2, par, k + 2)
                    if j == 3 and exists(group, 2):
                        normalise(group + 2, par)
                    dve.wait_ge(probs_turned, b + 1)
                    if reached(b, 1):
                        dve.wait_ge(out_done, b)
                    dve.tensor_copy(probsT[:], probsT_ps[:, 0:ROWS].rearrange("q (p k) -> q p k", k=PAIR)
                                    ).then_inc(probsT_ready, 1)
                    for rnd in range(2):
                        dve.wait_ge(v_turned, b * 2 + rnd + 1)
                        dve.tensor_copy(v_rows[:, 2 * rnd:2 * rnd + 2, :], v_ps[:, :, 0:D]).then_inc(v_ready, 1)

            dve.wait_ge(const_loaded, 16 * 5)
            dve.tensor_copy(mask[:], mask_f[:]).then_inc(mask_ready, 1)
            statistics(0, 0, 1)
            normalise(0, 0)
            statistics(1, 1, 1)
            normalise(1, 1)
            body(0, 0, 0)
            body(1, 1, 0)
            with dve.Fori(1, groups // 2 - 1) as k:
                body(k * 2, 0, k)
                body(k * 2 + 1, 1, k)
            body(groups - 2, 0, groups // 2 - 1)
            body(groups - 1, 1, groups // 2 - 1)
            dve.wait_ge(h_biased, groups)
            add_residual(TILES - 1)
            dve.wait_ge(h1_ready, TILES)


IMG = 84
GRID = 7
REG = IMG // GRID
C0, C1, C2 = 3, 12, 48


def image_stage(nc, io):
    B8, G4 = 8, 4
    CH = B8 * C1
    XW = IMG + 2
    XP = REG * XW
    PITCH = REG + 1
    GP = PITCH * PITCH
    LEAD = PITCH + 1
    RP = LEAD + G4 * GP + 2
    WROWS = G4 * PITCH - 1
    RPX = REG * REG
    PIECES = 2 * G4
    PROWS = REG // 2
    OY, OX = REG // 4, 20
    TAPS = 16
    RUN = G4 * OY * OX
    PAIRED = [(0, 1), (2, 3), (4, 5), (6,)]
    units = 2 * GRID
    P_PW, P_SC = 0, GRID * CH
    P_DW = 2 * GRID * CH
    P_SDW = P_DW + 9 * GRID
    P_BDW, P_BPW, P_LEN = P_SDW + GRID, P_SDW + 2 * GRID, P_SDW + 3 * GRID

    with ExitStack() as ctx:
        def sb(name, shape, dt=F32):
            return ctx.enter_context(nc.sbuf_tensor("img_sb_" + name, shape, dt))

        def ps(name, shape):
            return ctx.enter_context(nc.psum_tensor("img_ps_" + name, shape, F32))

        def sem(name):
            return ctx.enter_context(nc.semaphore("img_" + name))

        w0 = sb("w0", [B8 * C0 * 3, 3, CH])
        sb0 = sb("sb0", [CH, 2])
        w1 = sb("w1", [CH, 2, 64])
        sb1 = sb("sb1", [128, 2])
        w2 = sb("w2", [128, 4, 128])
        sb2 = sb("sb2", [128, 2])
        w3 = sb("w3", [128, 4, D])
        sb3 = sb("sb3", [128, 2, D])
        x = sb("x", [B8 * C0 * 3, 2, G4, XP])
        y0 = sb("y0", [CH, 2, GRID, RP])
        par = sb("par", [CH, 2, P_LEN])
        acc = sb("acc", [CH, 2, G4 * GP])
        y1 = sb("y1", [CH, 2, G4 * RPX])
        y2 = sb("y2", [CH, 2, G4 * RPX])
        taps = sb("taps", [128, TAPS * RUN])
        cols = sb("cols", [CH, 2, B8, RUN])
        z1 = sb("z1", [128, 4, 2 * G4, GRID * OY * OX])
        tok = sb("tok", [4 * IMG_LEN, 4, D])
        c0_ps = ps("c0_ps", [128, 2, 512])
        pw_ps = ps("pw_ps", [128, 2, G4, 256])
        c1_ps = ps("c1_ps", [128, 2, 512])
        z2 = taps[:, 0:4 * 32 * IMG_LEN].rearrange("p (t n) -> p t n", t=4)

        const_loaded = sem("const_loaded")
        wait_carrier = sem("wait_carrier")
        x_loaded = [sem("x_loaded_half0"), sem("x_loaded_half1")]
        par_loaded = [sem("par_loaded_even"), sem("par_loaded_odd")]
        pads_set = sem("pads_set")
        pw_scaled = sem("pw_scaled")
        conv0_done = sem("conv0_done")
        y0_ready = sem("y0_ready")
        dw_tap = sem("dw_tap")
        dw_done = sem("dw_done")
        y1_ready = sem("y1_ready")
        pw_done = sem("pw_done")
        y2_ready = sem("y2_ready")
        taps_ready = sem("taps_ready")
        taps_stored = sem("taps_stored")
        cols_loaded = sem("cols_loaded")
        conv1_done = sem("conv1_done")
        z1_ready = sem("z1_ready")
        conv2_done = sem("conv2_done")
        z2_ready = sem("z2_ready")
        conv3_done = sem("conv3_done")
        tok_scaled = sem("tok_scaled")
        tok_ready = sem("tok_ready")
        h_stored = [sem(f"h_stored_{i}") for i in range(4)]

        def over_units(eng, body):
            for hf in range(2):
                body(0, 0, 0, hf)
            with eng.Fori(0, 2) as k:
                for hf in range(2):
                    body(k * 2 + 1, k, 1, hf)
                for hf in range(2):
                    body(k * 2 + 2, k + 1, 0, hf)
            for s in (GRID - 2, GRID - 1):
                for hf in range(2):
                    body(s, s // 2, s % 2, hf)

        def is_last(s):
            return isinstance(s, int) and s == GRID - 1

        def has_next(s, hf):
            return not (is_last(s) and hf == 1)

        def window(half, gx, ky, kx):
            at = LEAD + (ky - 1) * PITCH + (kx - 1)
            return y0[:, half, gx, at:at + WROWS * PITCH].rearrange("p (r c) -> p r c", c=PITCH)[:, :, 0:REG]

        def pixels(tile):
            return tile.rearrange("p (g r c) -> p g r c", r=PITCH, c=PITCH)[:, :, 0:REG, 0:REG]

        block = ctx.enter_context(nc.Block())

        @block.sync
        def _(sp):
            def load_x(s, half):
                for dy in range(3):
                    src = io["img_x"][:, half * G4:(half + 1) * G4, bass.ds((s * REG + dy) * XW, XP)]
                    sp.dma_start(x[dy * B8 * C0:(dy + 1) * B8 * C0, half], src).then_inc(x_loaded[half], 16)

            def load_par(s, parity):
                sp.dma_start(par[:, parity], io["img_par"][s]).then_inc(par_loaded[parity], 16)

            def regroup(u, half):
                sp.wait_ge(taps_ready, (u + 1) * GRID)
                sp.dma_start(io["img_taps"][half], taps[0:CH, :]).then_inc(taps_stored, 16)
                sp.wait_ge(taps_stored, (u + 1) * 16)
                sp.sem_inc(wait_carrier, 1)
                if reached(u, 1):
                    sp.wait_ge(conv1_done, u)
                src = io["img_taps"][half].rearrange("(b k c) (t n) -> k c t b n", k=2, c=C1 // 2, n=RUN)
                for k in range(2):
                    sp.dma_start(cols[:, k], src[k].rearrange("c t b n -> (c t) b n")).then_inc(cols_loaded, 16)

            load_x(0, 0)
            consts = ((w0, "img_w0"), (sb0, "img_sb0"), (w1, "img_w1"), (sb1, "img_sb1"), (w2, "img_w2"),
                      (sb2, "img_sb2"), (w3, "img_w3"), (sb3, "img_sb3"))
            for dst, name in consts:
                sp.dma_start(dst[:], io[name]).then_inc(const_loaded, 16)
            load_par(0, 0)
            load_x(0, 1)

            def body(s, sc, parity, hf):
                u = s * 2 + hf
                if not is_last(s):
                    sp.wait_ge(conv0_done, (u + 1) * PIECES)
                    sp.sem_inc(wait_carrier, 1)
                    load_x(s + 1, hf)
                    if hf == 0:
                        if reached(s, 1):
                            sp.wait_ge(taps_ready, u * GRID)
                            sp.sem_inc(wait_carrier, 1)
                        load_par(s + 1, 1 - parity)
                if reached(u, 1):
                    regroup(u - 1, 1 - hf)

            over_units(sp, body)
            regroup(units - 1, 1)

            def store(n):
                h, i = divmod(n, 8)
                b8 = h * 4 + i // 2
                sp.wait_ge(tok_ready, n + 1)
                rows = io["h"].rearrange("(g b t) d -> b g t d", b=B8, t=SEQ)
                for g in range(4):
                    sp.dma_start(rows[b8, (i % 2) * 4 + g, 0:IMG_LEN, :],
                                 tok[g * IMG_LEN:(g + 1) * IMG_LEN, n % 4, :]).then_inc(h_stored[n % 4], 16)

            for n in range(16):
                store(n)
            for done in h_stored:
                sp.wait_ge(done, 4 * 64)

        @block.gpsimd
        def _(pool):
            def scale_pointwise(s, sc, parity, hf):
                if hf == 0:
                    pool.wait_ge(par_loaded[parity], (sc + 1) * 16)
                    pool.tensor_tensor(par[:, parity, P_PW:P_PW + GRID * CH], par[:, parity, P_PW:P_PW + GRID * CH],
                                       par[:, parity, P_SC:P_SC + GRID * CH], ALU.mult).then_inc(pw_scaled, 1)

            over_units(pool, scale_pointwise)

        @block.tensor
        def _(pe):
            def conv0(u, half, x_count, pieces):
                for piece in pieces:
                    g, part = divmod(piece, 2)
                    if piece == 0:
                        pe.wait_ge(x_loaded[half], x_count)
                    if piece >= 2 or reached(u, 1):
                        pe.wait_ge(y0_ready, u * PIECES + (piece - 1))
                    rows = x[:, half, g, :].rearrange("p (r c) -> p r c", c=XW)[:, part * PROWS:(part + 1) * PROWS, :]
                    out = c0_ps[0:CH, piece % 2, 0:PROWS * IMG]
                    for dx in range(3):
                        mm = pe.matmul(out, w0[:, dx, :], rows[:, :, dx:dx + IMG], start=(dx == 0), stop=(dx == 2))
                    mm.then_inc(conv0_done, 1)

            def pointwise(u, s, hf, parity, gx):
                r, rp = u * GRID + gx, (hf + gx) % 2
                if hf == 0 and gx == 0:
                    pe.wait_ge(pw_scaled, s + 1)
                pe.wait_ge(y1_ready, r + 1)
                if reached(r, 2):
                    pe.wait_ge(y2_ready, r - 1)
                for q in range(2):
                    mm = pe.matmul(pw_ps[0:CH, rp, 2 * q:2 * q + 2, 0:RPX],
                                   par[:, parity, P_PW + gx * CH:P_PW + (gx + 1) * CH],
                                   y1[:, rp, 2 * q * RPX:(2 * q + 2) * RPX].rearrange("p (g n) -> p g n", n=RPX),
                                   start=True, stop=True)
                mm.then_inc(pw_done, 1)

            def conv1(u):
                pe.wait_ge(cols_loaded, (u + 1) * 32)
                if reached(u, 1):
                    pe.wait_ge(z1_ready, u)
                for m in range(4):
                    for k in range(2):
                        mm = pe.matmul(c1_ps[64 * (m // 2):64 * (m // 2) + 64, m % 2, 0:2 * RUN], w1[:, k, :],
                                       cols[:, k, 2 * m:2 * m + 2, :], start=(k == 0), stop=(k == 1))
                mm.then_inc(conv1_done, 1)

            pe.wait_ge(const_loaded, 16 * 8)
            conv0(0, 0, 48, range(PIECES))

            def body(s, sc, parity, hf):
                u = s * 2 + hf
                for q, regions in enumerate(PAIRED):
                    if has_next(s, hf):
                        conv0(u + 1, 1 - hf, (s + (1 + hf)) * 48, (2 * q, 2 * q + 1))
                    for gx in regions:
                        pointwise(u, s, hf, parity, gx)
                if reached(u, 1):
                    conv1(u - 1)

            over_units(pe, body)
            conv1(units - 1)

            z = z1[:].rearrange("p b g (y x) -> p (b g) y x", x=OX)
            pe.wait_ge(z1_ready, units)
            for i in range(8):
                """2x2 with stride 2, both b8 halves by a block-diagonal weight."""
                if i >= 4:
                    pe.wait_ge(z2_ready, i - 3)
                for t in range(4):
                    mm = pe.matmul(pw_ps[:, i % 4 // 2, (i % 2) * 2:(i % 2) * 2 + 2, :].rearrange(
                                       "p a n -> p (a n)")[:, 0:400],
                                   w2[:, t, :], z[:, 4 * i:4 * i + 4, t // 2:t // 2 + 19:2, t % 2:t % 2 + 19:2],
                                   start=(t == 0), stop=(t == 3))
                mm.then_inc(conv2_done, 1)
            for n in range(16):
                """2x2 with stride 2, tokens on partitions: four batches of 25 tokens."""
                h, i = divmod(n, 8)
                if h == 0:
                    pe.wait_ge(z2_ready, i + 1)
                if n >= 2:
                    pe.wait_ge(tok_scaled, n - 1)
                for t in range(4):
                    mm = pe.matmul(c0_ps[0:4 * IMG_LEN, n % 2, 0:D],
                                   z2[64 * h:64 * h + 64, t, 4 * i * IMG_LEN:(4 * i + 4) * IMG_LEN],
                                   w3[64 * h:64 * h + 64, t, :], start=(t == 0), stop=(t == 3))
                mm.then_inc(conv3_done, 1)

        @block.scalar
        def _(act):
            def take_conv0(u, half, pieces):
                for piece in pieces:
                    g, part = divmod(piece, 2)
                    act.wait_ge(conv0_done, u * PIECES + (piece + 1))
                    if piece == 0 and reached(u, 2):
                        act.wait_ge(y2_ready, (u - 1) * GRID)
                    at = LEAD + g * GP + part * PROWS * PITCH
                    dst = y0[:, half, :, at:at + PROWS * PITCH].rearrange("p r (y c) -> p y r c", c=PITCH)[:, :, :, 0:REG]
                    src = c0_ps[0:CH, piece % 2, 0:PROWS * IMG].rearrange("p (y r c) -> p y r c", r=GRID, c=REG)
                    act.activation(dst, src, ACT.Gelu, scale=sb0[:, 0:1], bias=sb0[:, 1:2]).then_inc(y0_ready, 1)

            def take_depthwise(u, hf, parity, gx):
                r, rp = u * GRID + gx, (hf + gx) % 2
                act.wait_ge(dw_done, r + 1)
                if reached(r, 2):
                    act.wait_ge(pw_done, r - 1)
                act.activation(y1[:, rp, :].rearrange("p (g y c) -> p g y c", y=REG, c=REG), pixels(acc[:, rp, :]), ACT.Gelu,
                               scale=par[:, parity, P_SDW + gx:P_SDW + gx + 1],
                               bias=par[:, parity, P_BDW + gx:P_BDW + gx + 1]).then_inc(y1_ready, 1)

            def take_region(u, hf, parity, gx):
                r, rp = u * GRID + gx, (hf + gx) % 2
                n = min(OY, OX - gx * OY)
                act.wait_ge(y2_ready, r + 1)
                if gx == 0 and reached(u, 1):
                    act.wait_ge(taps_stored, u * 16)
                src = y2[:, rp, :].rearrange("p (a d b e) -> p d a b e", d=4, b=OY, e=4)
                dst = taps[0:CH, :].rearrange("p (d e a x) -> p d a x e", d=4, e=4, x=OX)
                for dy in range(4):
                    last = act.activation(dst[:, dy, :, gx * OY:gx * OY + n, :], src[:, dy, :, 0:n, :], ACT.Gelu,
                                          bias=par[:, parity, P_BPW + gx:P_BPW + gx + 1])
                last.then_inc(taps_ready, 1)

            def take_conv1(u, s, hf):
                act.wait_ge(conv1_done, u + 1)
                act.sem_inc(wait_carrier, 1)
                for m in range(2):
                    last = act.activation(z1[:, 2 * m:2 * m + 2, hf * G4:(hf + 1) * G4, bass.ds(s * (OY * OX), OY * OX)],
                                          c1_ps[:, m, 0:2 * RUN].rearrange("p (b g n) -> p b g n", b=2, g=G4), ACT.Gelu,
                                          scale=sb1[:, 0:1], bias=sb1[:, 1:2])
                last.then_inc(z1_ready, 1)

            act.wait_ge(const_loaded, 16 * 8)
            act.wait_ge(pads_set, 1)
            take_conv0(0, 0, range(PIECES))

            def body(s, sc, parity, hf):
                u = s * 2 + hf
                if hf == 0:
                    act.wait_ge(par_loaded[parity], (sc + 1) * 16)
                for q, regions in enumerate(PAIRED):
                    for gx in regions:
                        take_depthwise(u, hf, parity, gx)
                    if q == 0:
                        if reached(u, 1):
                            take_region(u - 1, 1 - hf, parity if hf else 1 - parity, GRID - 1)
                    else:
                        for gx in PAIRED[q - 1]:
                            take_region(u, hf, parity, gx)
                    if has_next(s, hf):
                        take_conv0(u + 1, 1 - hf, (2 * q, 2 * q + 1))
                if reached(u, 1):
                    take_conv1(u - 1, s if hf else s - 1, 1 - hf)

            over_units(act, body)
            take_region(units - 1, 1, (GRID - 1) % 2, GRID - 1)
            take_conv1(units - 1, GRID - 1, 1)
            act.wait_ge(taps_stored, units * 16)
            for i in range(8):
                act.wait_ge(conv2_done, i + 1)
                src = pw_ps[:, i % 4 // 2, (i % 2) * 2:(i % 2) * 2 + 2, :].rearrange("p a n -> p (a n)")[:, 0:400]
                src = src.rearrange("p (a d x e) -> p d a x e", d=2, x=5, e=2)
                dst = z2[:, :, 4 * i * IMG_LEN:(4 * i + 4) * IMG_LEN].rearrange("p (d e) (a x) -> p d a x e", d=2, x=5)
                for dy in range(2):
                    last = act.activation(dst[:, dy], src[:, dy], ACT.Gelu, scale=sb2[:, 0:1], bias=sb2[:, 1:2])
                last.then_inc(z2_ready, 1)

        @block.vector
        def _(dve):
            dve.memset(y0[:], 0.0).then_inc(pads_set, 1)

            def depthwise(u, hf, parity, regions):
                n = len(regions)
                first = u * (8 * GRID) + 8 * regions[0]
                for k, (ky, kx) in enumerate([(1, 1)] + [(i // 3, i % 3) for i in range(9) if i != 4]):
                    for a, gx in enumerate(regions):
                        r, rp = u * GRID + gx, (hf + gx) % 2
                        out = acc[:, rp, 0:WROWS * PITCH].rearrange("p (r c) -> p r c", c=PITCH)[:, :, 0:REG]
                        at = P_DW + gx * 9 + ky * 3 + kx
                        w = par[:, parity, at:at + 1]
                        if k == 0:
                            if reached(r, 2):
                                dve.wait_ge(y1_ready, r - 1)
                            s = dve.tensor_scalar(out, window(hf, gx, ky, kx), w, None, ALU.mult)
                        else:
                            dve.wait_ge(dw_tap, first + (n * (k - 1) + a + 1))
                            s = dve.scalar_tensor_tensor(out, window(hf, gx, ky, kx), w, out, ALU.mult, ALU.add)
                        s.then_inc(dw_tap if k < 8 else dw_done, 1)

            def add_input(u, hf, gx):
                r, rp = u * GRID + gx, (hf + gx) % 2
                dve.wait_ge(pw_done, r + 1)
                if reached(r, 2):
                    dve.wait_ge(taps_ready, r - 1)
                dve.tensor_tensor(y2[:, rp, :].rearrange("p (g y c) -> p g y c", y=REG, c=REG),
                                  pw_ps[0:CH, rp, :, 0:RPX].rearrange("p g (y c) -> p g y c", c=REG),
                                  pixels(y0[:, hf, gx, LEAD:LEAD + G4 * GP]), ALU.add).then_inc(y2_ready, 1)

            def body(s, sc, parity, hf):
                u = s * 2 + hf
                if hf == 0:
                    dve.wait_ge(par_loaded[parity], (sc + 1) * 16)
                dve.wait_ge(y0_ready, (u + 1) * PIECES)
                for q, regions in enumerate(PAIRED):
                    depthwise(u, hf, parity, regions)
                    if q:
                        for gx in PAIRED[q - 1]:
                            add_input(u, hf, gx)
                    elif reached(u, 1):
                        add_input(u - 1, 1 - hf, GRID - 1)

            over_units(dve, body)
            add_input(units - 1, 1, GRID - 1)

            for n in range(16):
                dve.wait_ge(conv3_done, n + 1)
                if n >= 4:
                    dve.wait_ge(h_stored[n % 4], 64 * (n // 4))
                rows = slice(0, 4 * IMG_LEN)
                dve.tensor_tensor(tok[:, n % 4, :], c0_ps[rows, n % 2, 0:D], sb3[rows, 0, :], ALU.mult).then_inc(tok_scaled, 1)
                dve.wait_ge(tok_scaled, n + 1)
                dve.tensor_tensor(tok[:, n % 4, :], tok[:, n % 4, :], sb3[rows, 1, :], ALU.add).then_inc(tok_ready, 1)


EXPERTS = 8
F = 768


def expert_stage(nc, io, h1):
    FB = F // 128
    BT = 4
    BN = BT * PAIR
    NB = TILES // BT

    with ExitStack() as ctx:
        def sb(name, shape, dt=F32):
            return ctx.enter_context(nc.sbuf_tensor("moe_sb_" + name, shape, dt))

        def ps(name, shape):
            return ctx.enter_context(nc.psum_tensor("moe_ps_" + name, shape, F32))

        def sem(name):
            return ctx.enter_context(nc.semaphore("moe_" + name))

        ident = sb("ident", [128, 128])
        router_w = sb("router_w", [HALF, 2, EXPERTS])
        up_b = sb("up_b", [128, EXPERTS, FB])
        down_b = sb("down_b", [EXPERTS, D])
        up_w = sb("up_w", [HALF, 2, 2, F])
        down_w = sb("down_w", [128, 2, FB, D])
        minus_half = sb("minus_half", [PAIR, TILES])
        number = sb("number", [PAIR, EXPERTS])
        stats = sb("stats", [PAIR, TILES, 6])
        mv = sb("mv", [PAIR, TILES, 2])
        var_eps = sb("var_eps", [PAIR, TILES])
        rstd = sb("rstd", [PAIR, TILES])
        xn = sb("xn", [PAIR, 4, D])
        xnT = sb("xnT", [HALF, 2, TOKENS])
        logits = sb("logits", [PAIR, TILES, EXPERTS])
        top = sb("top", [PAIR, TILES, 8])
        top_at = sb("top_at", [PAIR, TILES, 8], U32)
        top_atf = sb("top_atf", [PAIR, TILES, 8])
        gap = sb("gap", [PAIR, TILES])
        ratio = sb("ratio", [PAIR, TILES])
        one_plus = sb("one_plus", [PAIR, TILES])
        share = sb("share", [PAIR, 2, TILES])
        picked = sb("picked", [PAIR, 2, TILES, EXPERTS])
        mix = sb("mix", [PAIR, TILES, EXPERTS])
        mixT = sb("mixT", [EXPERTS, 2, PAIR])
        hidden = sb("hidden", [128, 2, FB, BN])
        ring_ps = ps("ring_ps", [128, 4, 512])
        down_ps = ps("down_ps", [128, BT, 512])

        const_loaded = sem("const_loaded")
        wait_carrier = sem("wait_carrier")
        weights_loaded = [sem("weights_loaded_even"), sem("weights_loaded_odd")]
        consts_set = sem("consts_set")
        stats_done = sem("stats_done")
        var_ready = sem("var_ready")
        eps_added = sem("eps_added")
        rstd_ready = sem("rstd_ready")
        normed = sem("normed")
        turned = sem("turned")
        xnT_ready = sem("xnT_ready")
        logits_done = sem("logits_done")
        logits_ready = sem("logits_ready")
        top_step = sem("top_step")
        ratio_ready = sem("ratio_ready")
        gap_ready = sem("gap_ready")
        mix_ready = sem("mix_ready")
        mix_turned = sem("mix_turned")
        mixT_ready = sem("mixT_ready")
        bias_done = sem("bias_done")
        bias_added = sem("bias_added")
        up_done = sem("up_done")
        hidden_ready = sem("hidden_ready")
        down_done = sem("down_done")
        added = sem("added")
        out_stored = sem("out_stored")

        def over_steps(eng, body):
            def expert(e, par):
                body(e, par, 0, 0)
                body(e, par, 1, 1)
                with eng.Fori(1, NB // 2) as i:
                    body(e, par, i * 2, 0)
                    body(e, par, i * 2 + 1, 1)
            expert(0, 0)
            expert(1, 1)
            with eng.Fori(1, EXPERTS // 2) as k:
                expert(k * 2, 0)
                expert(k * 2 + 1, 1)

        def logits_of(pe, t):
            pe.wait_ge(xnT_ready, t + 1)
            if t >= 2:
                pe.wait_ge(logits_ready, t - 1)
            for h in range(2):
                mm = pe.matmul(ring_ps[0:PAIR, 2 + t % 2, 0:EXPERTS], xnT[:, h, t * PAIR:(t + 1) * PAIR],
                               router_w[:, h, :], start=(h == 0), stop=(h == 1))
            mm.then_inc(logits_done, 1)

        def take_logits(dve, t):
            dve.wait_ge(logits_done, t + 1)
            dve.tensor_copy(logits[:, t, :], ring_ps[0:PAIR, 2 + t % 2, 0:EXPERTS]).then_inc(logits_ready, 1)

        block = ctx.enter_context(nc.Block())

        @block.sync
        def _(sp):
            for dst, name in ((ident, "ident"), (router_w, "router_w"), (up_b, "up_b"), (down_b, "down_b")):
                sp.dma_start(dst[:], io[name]).then_inc(const_loaded, 16)

            def load(e, par):
                if reached(e, 2):
                    sp.wait_ge(up_done, (e - 1) * (NB * FB))
                    sp.sem_inc(wait_carrier, 1)
                    sp.wait_ge(down_done, (e - 1) * TILES)
                    sp.sem_inc(wait_carrier, 1)
                sp.dma_start(up_w[:, par], io["up_w"][e]).then_inc(weights_loaded[par], 16)
                sp.dma_start(down_w[:, par], io["down_w"][e]).then_inc(weights_loaded[par], 16)

            load(0, 0)
            load(1, 1)
            with sp.Fori(1, EXPERTS // 2) as k:
                load(k * 2, 0)
                load(k * 2 + 1, 1)
            out = io["out"].rearrange("(t p) d -> p t d", p=PAIR)
            for j in range(NB):
                sp.wait_ge(added, (EXPERTS - 1) * TILES + (j + 1) * BT)
                sp.dma_start(out[:, j * BT:(j + 1) * BT, :], h1[:, j * BT:(j + 1) * BT, :]).then_inc(out_stored, 16)
            sp.wait_ge(out_stored, NB * 16)

        @block.gpsimd
        def _(pool):
            pool.memset(minus_half[:], -0.5).then_inc(consts_set, 1)
            pool.iota(number[:], pattern=[[1, EXPERTS]], base=0, channel_multiplier=0,
                      allow_small_or_imprecise_dtypes=True).then_inc(consts_set, 1)
            pool.wait_ge(consts_set, 2)
            pool.wait_ge(var_ready, 1)
            pool.tensor_scalar(var_eps[:], mv[:, :, 1], EPS, None, ALU.add).then_inc(eps_added, 1)
            pool.wait_ge(eps_added, 1)
            pool.tensor_tensor(rstd[:], var_eps[:], minus_half[:], ALU.pow).then_inc(rstd_ready, 1)

        @block.tensor
        def _(pe):
            pe.wait_ge(const_loaded, 16 * 4)
            for t in range(TILES):
                pe.wait_ge(normed, t + 1)
                if t >= 2:
                    pe.wait_ge(xnT_ready, t - 1)
                for h in range(2):
                    last = pe.transpose(ring_ps[0:HALF, t % 2, h * PAIR:(h + 1) * PAIR],
                                        xn[:, t % 4, h * HALF:(h + 1) * HALF], ident[0:PAIR, 0:PAIR])
                last.then_inc(turned, 1)
                if t >= 1:
                    logits_of(pe, t - 1)
            logits_of(pe, TILES - 1)
            pe.wait_ge(mix_ready, 1)
            for t in range(TILES):
                if t >= 2:
                    pe.wait_ge(mixT_ready, t - 1)
                pe.transpose(ring_ps[0:EXPERTS, t % 2, 0:PAIR], mix[:, t, :], ident[0:PAIR, 0:PAIR]
                             ).then_inc(mix_turned, 1)
                pe.wait_ge(mixT_ready, t + 1)
                if t >= 2:
                    pe.wait_ge(bias_added, t - 1)
                pe.matmul(ring_ps[0:PAIR, 2 + t % 2, 0:D], mixT[:, t % 2, :], down_b[:], start=True, stop=True
                          ).then_inc(bias_done, 1)

            def up(e, par, j, jp):
                n = e * NB + j
                if jp == 0 and isinstance(j, int) and j == 0:
                    pe.wait_ge(weights_loaded[par], (e // 2 + 1) * 32 if isinstance(e, int) else e * 16 + (32 - 16 * par))
                for m in range(FB):
                    if m >= 4 or reached(n, 1):
                        pe.wait_ge(hidden_ready, n * FB + (m - 3))
                    for h in range(2):
                        mm = pe.matmul(ring_ps[:, (jp * FB + m) % 4, 0:BN], up_w[:, par, h, m * 128:(m + 1) * 128],
                                       xnT[:, h, bass.ds(j * BN, BN)], start=(h == 0), stop=(h == 1))
                    mm.then_inc(up_done, 1)

            def down(n, par, jp):
                pe.wait_ge(hidden_ready, (n + 1) * FB)
                for t in range(BT):
                    if reached(n, 1):
                        pe.wait_ge(added, n * BT + (t + 1 - BT))
                    for m in range(FB):
                        mm = pe.matmul(down_ps[0:PAIR, t, 0:D], hidden[:, jp, m, t * PAIR:(t + 1) * PAIR],
                                       down_w[:, par, m, :], start=(m == 0), stop=(m == FB - 1))
                    mm.then_inc(down_done, 1)

            pe.wait_ge(bias_added, TILES)
            def step(e, par, j, jp):
                n = e * NB + j
                up(e, par, j, jp)
                first = isinstance(j, int) and j == 0
                if reached(n, 1):
                    down(n - 1, 1 - par if first else par, 1 - jp)

            over_steps(pe, step)
            down(EXPERTS * NB - 1, 1, 1)

        @block.scalar
        def _(act):
            act.wait_ge(const_loaded, 16 * 4)
            for t in range(TILES):
                act.wait_ge(turned, t + 1)
                act.activation(xnT[:, :, t * PAIR:(t + 1) * PAIR],
                               ring_ps[0:HALF, t % 2, 0:2 * PAIR].rearrange("p (h n) -> p h n", h=2),
                               ACT.Copy).then_inc(xnT_ready, 1)
            act.wait_ge(gap_ready, 1)
            act.activation(ratio[:], gap[:], ACT.Exp).then_inc(ratio_ready, 1)

            def gelu(e, par, j, jp):
                n = e * NB + j
                for m in range(FB):
                    act.wait_ge(up_done, n * FB + (m + 1))
                    if m == 0 and reached(n, 2):
                        act.wait_ge(down_done, (n - 1) * BT)
                    act.sem_inc(wait_carrier, 1)
                    act.activation(hidden[:, jp, m, :], ring_ps[:, (jp * FB + m) % 4, 0:BN], ACT.Gelu,
                                   bias=up_b[:, e, m:m + 1]).then_inc(hidden_ready, 1)

            over_steps(act, gelu)

        @block.vector
        def _(dve):
            for t in range(TILES):
                s = dve.bn_stats(stats[:, t, :], h1[:, t, :])
            s.then_inc(stats_done, 1)
            dve.wait_ge(stats_done, 1)
            for t in range(TILES):
                s = dve.bn_aggr(mv[:, t, :], stats[:, t, :])
            s.then_inc(var_ready, 1)
            dve.wait_ge(rstd_ready, 1)
            for t in range(TILES):
                if t >= 4:
                    dve.wait_ge(turned, t - 3)
                dve.tensor_scalar(xn[:, t % 4, :], h1[:, t, :], mv[:, t, 0:1], rstd[:, t:t + 1],
                                  ALU.subtract, ALU.mult).then_inc(normed, 1)
                if t >= 2:
                    take_logits(dve, t - 2)
            take_logits(dve, TILES - 2)
            take_logits(dve, TILES - 1)

            steps = 0

            def chained(s):
                nonlocal steps
                steps += 1
                s.then_inc(top_step, 1)
                dve.wait_ge(top_step, steps)

            dve.wait_ge(consts_set, 2)
            dve.wait_ge(logits_ready, TILES)
            for t in range(TILES):
                s = dve.max(top[:, t, :], logits[:, t, :])
            chained(s)
            for t in range(TILES):
                s = dve.max_index(top_at[:, t, :], top[:, t, :], logits[:, t, :])
            chained(s)
            dve.tensor_tensor(gap[:], top[:, :, 1], top[:, :, 0], ALU.subtract).then_inc(gap_ready, 1)
            chained(dve.tensor_copy(top_atf[:], top_at[:]))
            for k in range(2):
                s = dve.tensor_tensor(picked[:, k], number[:].unsqueeze(1).to_broadcast([PAIR, TILES, EXPERTS]),
                                      top_atf[:, :, k:k + 1].to_broadcast([PAIR, TILES, EXPERTS]), ALU.is_equal)
            chained(s)
            dve.wait_ge(ratio_ready, 1)
            chained(dve.tensor_scalar(one_plus[:], ratio[:], 1.0, None, ALU.add))
            chained(dve.reciprocal(share[:, 0], one_plus[:]))
            chained(dve.tensor_tensor(share[:, 1], share[:, 0], ratio[:], ALU.mult))
            for k in range(2):
                s = dve.tensor_tensor(picked[:, k], picked[:, k],
                                      share[:, k].unsqueeze(2).to_broadcast([PAIR, TILES, EXPERTS]), ALU.mult)
            chained(s)
            dve.tensor_tensor(mix[:], picked[:, 0], picked[:, 1], ALU.add).then_inc(mix_ready, 1)
            dve.wait_ge(mix_ready, 1)
            for t in range(TILES):
                dve.wait_ge(mix_turned, t + 1)
                if t >= 2:
                    dve.wait_ge(bias_done, t - 1)
                dve.tensor_copy(mixT[:, t % 2, :], ring_ps[0:EXPERTS, t % 2, 0:PAIR]).then_inc(mixT_ready, 1)
                dve.wait_ge(bias_done, t + 1)
                dve.tensor_tensor(h1[:, t, :], h1[:, t, :], ring_ps[0:PAIR, 2 + t % 2, 0:D], ALU.add
                                  ).then_inc(bias_added, 1)
            dve.wait_ge(bias_added, TILES)

            def add_expert(e, par, j, jp):
                n = e * NB + j
                for t in range(BT):
                    tile = j * BT + t
                    dve.wait_ge(down_done, n * BT + (t + 1))
                    if reached(e, 1):
                        dve.wait_ge(added, n * BT + (t + 1 - TILES))
                    dve.scalar_tensor_tensor(h1[:, tile, :], down_ps[0:PAIR, t, 0:D], mix[:, tile, bass.ds(e, 1)],
                                             h1[:, tile, :], ALU.mult, ALU.add).then_inc(added, 1)

            over_steps(dve, add_expert)





def build_program(nc, io):
    image_stage(nc, io)
    text_stage(nc, io)
    with nc.sbuf_tensor("h1", [PAIR, TILES, D], F32) as h1:
        attention_stage(nc, io, h1)
        expert_stage(nc, io, h1)


def _layouts(a):
    import numpy as np
    P = 128
    out = {}
    out["txt_idx"] = a["x_txt"].reshape(-1, P).T
    out["txt_pos"] = np.tile(a["L0_txt_pos_encoding"][0, :TEXT_LEN], (P // TEXT_LEN, 1))
    out["embedding"] = a["L0_txt_embedding"]
    out["ident"] = np.eye(P, dtype=np.float32)
    out["txt_final_g"] = np.broadcast_to(a["L0_txt_final_g"], (P, D))
    out["txt_final_b"] = np.broadcast_to(a["L0_txt_final_b"], (P, D))
    gb = np.stack([a["L0_txt_ln_g"], a["L0_txt_ln_b"]], 1)
    out["txt_ln_gb"] = gb.reshape(LAYERS, 2, 2, HALF).transpose(3, 0, 1, 2)
    out["txt_taps"] = a["L0_txt_conv_w"].reshape(LAYERS, DI_CHUNKS, HALF, 3).transpose(2, 0, 1, 3)
    out["txt_dt_b"] = a["L0_txt_dt_b"].reshape(LAYERS, DI_CHUNKS, HALF).transpose(2, 0, 1)
    out["txt_in_w"] = a["L0_txt_in_w"].reshape(LAYERS, 2 * DI, 2, HALF).transpose(0, 3, 2, 1)
    out["txt_dt_w"] = a["L0_txt_dt_w"].reshape(LAYERS, DI, DI_CHUNKS, HALF).transpose(0, 3, 2, 1)
    ow = a["L0_txt_out_w"].reshape(LAYERS, D, DI_CHUNKS, HALF).transpose(0, 3, 2, 1)
    ls = np.broadcast_to(a["L0_txt_layer_scale"][:, None, None, :], (LAYERS, HALF, 1, D))
    out["txt_out_w"] = np.concatenate([ow, ls], 2)
    def blocks(w):
        w = w.reshape(-1, 3, HEADS // 2, 2, D)
        tail = w[..., 128:].reshape(w.shape[0], 3, HEADS // 2, 1, 128)
        return np.concatenate([w[..., :128], tail], 3).reshape(w.shape[0], -1, 128)
    out["qkv_w"] = blocks(a["L0_attn_W_qkv"]).reshape(2, HALF, -1, 128).transpose(1, 0, 2, 3)
    out["qkv_b"] = blocks(a["L0_attn_b_qkv"][None])[0].T
    out["proj_w"] = a["L0_attn_W_proj"].reshape(2 * HEADS, HALF, D).transpose(1, 0, 2)
    out["proj_b"] = np.broadcast_to(a["L0_attn_b_proj"], (PAIR, D))
    first = np.repeat([1.0, 0.0], SEQ)
    out["mask"] = np.stack([np.stack([first, 1 - first]), np.stack([1 - first, first]) * -1e30], 1).astype(np.float32)
    f = np.float32
    xp = np.pad(a["x"], ((0, 0), (0, 0), (1, 1), (1, 1)))
    out["img_x"] = xp.reshape(8, 8 * C0, -1).transpose(1, 0, 2)
    w0 = np.zeros((3, 8, C0, 3, 8, C1), f)
    for b in range(8):
        w0[:, b, :, :, b, :] = a["L0_tok_w0"].transpose(2, 1, 3, 0)
    out["img_w0"] = w0.reshape(72, 3, 96)
    out["img_sb0"] = np.tile(np.stack([a["L0_tok_s0"], a["L0_tok_b0"]], 1), (8, 1))
    pw = a["L0_tok_wpw"].reshape(GRID, GRID, C1, C1).transpose(0, 3, 1, 2)
    pwd = np.zeros((GRID, 8, C1, GRID, 8, C1), f)
    for b in range(8):
        pwd[:, b, :, :, b, :] = pw
    spw = np.broadcast_to(a["L0_tok_spw"].reshape(GRID, 1, GRID, 1, C1), (GRID, 96, GRID, 8, C1))
    def by_channel(v):
        return np.tile(v.reshape(GRID, GRID, C1, -1).transpose(0, 2, 1, 3), (1, 8, 1, 1)).reshape(GRID, 96, -1)
    out["img_par"] = np.concatenate([pwd.reshape(GRID, 96, -1), spw.reshape(GRID, 96, -1), by_channel(a["L0_tok_wdw"]),
                                     by_channel(a["L0_tok_sdw"]), by_channel(a["L0_tok_bdw"]),
                                     by_channel(a["L0_tok_bpw"])], 2)
    w1 = a["L0_tok_w1"].transpose(1, 2, 3, 0).reshape(2, 96, C2).transpose(1, 0, 2)
    out["img_w1"] = np.pad(w1, ((0, 0), (0, 0), (0, 64 - C2)))
    def padded_pair(s, b):
        return np.tile(np.pad(np.stack([s, b], 1), ((0, 64 - C2), (0, 0))), (2, 1))
    out["img_sb1"] = padded_pair(a["L0_tok_s1"], a["L0_tok_b1"])
    out["img_sb2"] = padded_pair(a["L0_tok_s2"], a["L0_tok_b2"])
    w2 = np.zeros((2, 64, 4, 2, 64), f)
    for k in range(2):
        w2[k, :C2, :, k, :C2] = a["L0_tok_w2"].transpose(1, 2, 3, 0).reshape(C2, 4, C2)
    out["img_w2"] = w2.reshape(128, 4, 128)
    w3 = np.pad(a["L0_tok_w3"].transpose(1, 2, 3, 0).reshape(C2, 4, D), ((0, 64 - C2), (0, 0), (0, 0)))
    out["img_w3"] = np.tile(w3, (2, 1, 1))
    out["img_sb3"] = np.broadcast_to(np.stack([a["L0_tok_s3"], a["L0_tok_b3"]])[None], (128, 2, D))
    out["router_w"] = a["L0_ffn_Wr"].reshape(EXPERTS, 2, HALF).transpose(2, 1, 0)
    out["up_w"] = a["L0_ffn_Wi"].reshape(EXPERTS, F, 2, HALF).transpose(0, 3, 2, 1)
    out["up_b"] = a["L0_ffn_bi"].reshape(EXPERTS, F // P, P).transpose(2, 0, 1)
    out["down_w"] = a["L0_ffn_Wo"].reshape(EXPERTS, D, F // P, P).transpose(0, 3, 2, 1)
    out["down_b"] = a["L0_ffn_bo"]
    return {name: np.ascontiguousarray(v) for name, v in out.items()}


def kernel(**inputs):
    import numpy as np
    import concourse.bacc as bacc
    from concourse.bass_utils import run_bass_kernel_spmd

    nc = bacc.Bacc("TRN2", target_bir_lowering=False, num_devices=1)
    arrays = _layouts({name: np.asarray(v) for name, v in inputs.items()})
    io = {name: nc.dram_tensor("in_" + name, v.shape, mybir.dt.from_np(v.dtype), kind="ExternalInput").ap()
          for name, v in arrays.items()}
    io["out"] = nc.dram_tensor("out_dram", (TOKENS, D), F32, kind="ExternalOutput").ap()
    io["h"] = nc.dram_tensor("h_dram", (TOKENS, D), F32).ap()
    io["img_taps"] = nc.dram_tensor("img_taps_dram", (2, 96, 3840), F32).ap()
    build_program(nc, io)
    r = run_bass_kernel_spmd(nc, [{"in_" + name: v for name, v in arrays.items()}], core_ids=[0])
    return r.results[0]["out_dram"].reshape(BATCH, SEQ, D)
```

```python
from contextlib import ExitStack

import concourse.bass as bass
from concourse import mybir

F32 = mybir.dt.float32
F32R = mybir.dt.float32r
BF16 = mybir.dt.bfloat16
I32 = mybir.dt.int32
U32 = mybir.dt.uint32
ALU = mybir.AluOpType
ACT = mybir.ActivationFunctionType
AX_X = mybir.AxisListType.X

BATCH = 64
D = 192
HALF = D // 2
TEXT_LEN = 32
IMG_LEN = 25
SEQ = IMG_LEN + TEXT_LEN
TOKENS = BATCH * SEQ
EPS = 1e-5
LN2 = 0.6931471805599453

LAYERS = 4
DI = 288
DI_CHUNKS = DI // HALF


def reached(step, n):
    return not isinstance(step, int) or step >= n


def text_stage(nc, io):
    T = TEXT_LEN
    seqs_per_tile = 128 // T
    tiles = BATCH * T // 128
    TG = 4
    groups = tiles // TG
    N = 128 * TG
    steps = LAYERS * groups
    IN, C = 2 * DI_CHUNKS, DI_CHUNKS

    with ExitStack() as ctx:
        def sb(name, shape, dt=F32):
            return ctx.enter_context(nc.sbuf_tensor("txt_sb_" + name, shape, dt))

        def ps(name, shape):
            return ctx.enter_context(nc.psum_tensor("txt_ps_" + name, shape, F32))

        def sem(name):
            return ctx.enter_context(nc.semaphore("txt_" + name))

        idx = sb("idx", [128, tiles], I32)
        pos = sb("pos", [128, D])
        x = sb("x", [128, tiles, D])
        ident = sb("ident", [128, 128])
        final_g = sb("final_g", [128, D])
        final_b = sb("final_b", [128, D])
        ln_gb = sb("ln_gb", [HALF, LAYERS, 2, 2])
        taps = sb("taps", [HALF, LAYERS, C, 3])
        dt_b = sb("dt_b", [HALF, LAYERS, C])
        dt_bias = sb("dt_bias", [HALF, LAYERS, C])
        in_w = sb("in_w", [HALF, 2, 2 * DI])
        dt_w = sb("dt_w", [HALF, C, DI])
        out_raw = sb("out_raw", [HALF, C + 1, D])
        half_scale = sb("half_scale", [HALF, D])
        out_w = sb("out_w", [HALF, C, D])
        minus_half = sb("minus_half", [128, TG])
        stats = sb("stats", [128, TG, 6])
        mv = sb("mv", [128, 2, TG, 2])
        var_eps = sb("var_eps", [128, TG])
        rstd = sb("rstd", [128, 2, TG])
        xn = sb("xn", [128, TG, D])
        xnT = sb("xnT", [HALF, 2, N])
        conv = sb("conv", [HALF, C, N])
        conv_sg = sb("conv_sg", [HALF, C, N])
        ssm = sb("ssm", [HALF, 2, C, N])
        x2_sg = sb("x2_sg", [HALF, 2, C, N])
        dt_sg = sb("dt_sg", [HALF, C, N])
        gate = sb("gate", [HALF, C, N])
        xg = sb("xg", [HALF, C, N])
        turn_ps = ps("turn_ps", [HALF, 2, 512])
        ring_ps = ps("ring_ps", [HALF, 4, 512])
        out_ps = ps("out_ps", [128, TG, 256])

        idx_loaded = sem("idx_loaded")
        const_loaded = sem("const_loaded")
        wait_carrier = sem("wait_carrier")
        gathered = sem("gathered")
        embedded = sem("embedded")
        consts_set = sem("consts_set")
        dt_bias_set = sem("dt_bias_set")
        in_w_loaded = sem("in_w_loaded")
        dt_w_loaded = sem("dt_w_loaded")
        out_raw_loaded = sem("out_raw_loaded")
        scale_halved = sem("scale_halved")
        out_w_ready = sem("out_w_ready")
        stats_done = sem("stats_done")
        var_ready = sem("var_ready")
        eps_added = sem("eps_added")
        rstd_ready = sem("rstd_ready")
        normed = sem("normed")
        turned = sem("turned")
        xnT_ready = sem("xnT_ready")
        in_done = sem("in_done")
        conv_tap = sem("conv_tap")
        conv_done = sem("conv_done")
        conv_sg_done = sem("conv_sg_done")
        x2_sg_done = sem("x2_sg_done")
        ssm_ready = sem("ssm_ready")
        dt_done = sem("dt_done")
        dt_sg_done = sem("dt_sg_done")
        gate_done = sem("gate_done")
        xg_ready = sem("xg_ready")
        out_done = sem("out_done")
        added = sem("added")
        scaled = sem("scaled")
        final_ready = sem("final_ready")
        h_stored = sem("h_stored")

        def over_steps(eng, body):
            for g in range(groups):
                body(g, 0, g)
            with eng.Fori(1, LAYERS - 1) as layer:
                for g in range(groups):
                    body(layer * groups + g, layer, g)
            for g in range(groups):
                body((LAYERS - 1) * groups + g, LAYERS - 1, g)

        def next_layer(layer, g):
            return layer + 1 if g == groups - 1 else layer

        block = ctx.enter_context(nc.Block())

        @block.sync
        def _(sp):
            sp.dma_start(idx[:], io["txt_idx"]).then_inc(idx_loaded, 16)
            for dst, name in ((pos, "txt_pos"), (ident, "ident"), (final_g, "txt_final_g"), (final_b, "txt_final_b"),
                              (ln_gb, "txt_ln_gb"), (taps, "txt_taps"), (dt_b, "txt_dt_b")):
                sp.dma_start(dst[:], io[name]).then_inc(const_loaded, 16)

            def load_layer(layer):
                if reached(layer, 1):
                    sp.wait_ge(in_done, layer * (groups * IN))
                    sp.sem_inc(wait_carrier, 1)
                sp.dma_start(in_w[:], io["txt_in_w"][layer]).then_inc(in_w_loaded, 16)
                if reached(layer, 1):
                    sp.wait_ge(out_w_ready, layer)
                    sp.sem_inc(wait_carrier, 1)
                sp.dma_start(out_raw[:], io["txt_out_w"][layer]).then_inc(out_raw_loaded, 16)
                if reached(layer, 1):
                    sp.wait_ge(dt_done, layer * (groups * C))
                    sp.sem_inc(wait_carrier, 1)
                sp.dma_start(dt_w[:], io["txt_dt_w"][layer]).then_inc(dt_w_loaded, 16)

            load_layer(0)
            with sp.Fori(1, LAYERS) as layer:
                load_layer(layer)
            with sp.Fori(0, groups) as g:
                sp.wait_ge(final_ready, g + 1)
                sp.sem_inc(wait_carrier, 1)
                for t in range(TG):
                    for b in range(seqs_per_tile):
                        seq = (g * TG + t) * seqs_per_tile + b
                        sp.dma_start(io["h"][bass.ds(seq * SEQ + IMG_LEN, T), :],
                                     x[b * T:(b + 1) * T, g * TG + t, :]).then_inc(h_stored, 16)
            sp.wait_ge(h_stored, 16 * BATCH)

        @block.gpsimd
        def _(pool):
            pool.wait_ge(idx_loaded, 16)
            for t in range(tiles):
                pool.indirect_dma_start(
                    out=x[:, t, :], out_offset=None, in_=io["embedding"],
                    in_offset=bass.IndirectOffsetOnAxis(ap=idx[:, t:t + 1].bitcast(U32), axis=0),
                ).then_inc(gathered, 16)
            pool.memset(minus_half[:], -0.5).then_inc(consts_set, 1)
            pool.wait_ge(consts_set, 1)
            pool.wait_ge(const_loaded, 16 * 7)
            pool.tensor_scalar(dt_bias[:], dt_b[:], -LN2, None, ALU.add).then_inc(dt_bias_set, 1)

            def inverse_deviation(n, par):
                pool.wait_ge(var_ready, n + 1)
                pool.sem_inc(wait_carrier, 1)
                pool.tensor_scalar(var_eps[:], mv[:, par, :, 1], EPS, None, ALU.add).then_inc(eps_added, 1)
                pool.wait_ge(eps_added, n + 1)
                pool.tensor_tensor(rstd[:, par, :], var_eps[:], minus_half[:], ALU.pow).then_inc(rstd_ready, 1)

            def scale_out_weights(layer):
                pool.wait_ge(out_raw_loaded, (layer + 1) * 16)
                pool.sem_inc(wait_carrier, 1)
                pool.tensor_scalar(half_scale[:], out_raw[:, C, :], 0.5, None, ALU.mult).then_inc(scale_halved, 1)
                pool.wait_ge(scale_halved, layer + 1)
                if reached(layer, 1):
                    pool.wait_ge(out_done, layer * groups)
                for c in range(C):
                    last = pool.tensor_tensor(out_w[:, c, :], out_raw[:, c, :], half_scale[:], ALU.mult)
                last.then_inc(out_w_ready, 1)

            inverse_deviation(0, 0)
            scale_out_weights(0)

            def step(i, layer, g):
                if not (isinstance(i, int) and i == steps - 1):
                    inverse_deviation(i + 1, (g + 1) % 2)
                if g == 1 and reached(layer, 1):
                    scale_out_weights(layer)

            over_steps(pool, step)
            for g in range(groups):
                inverse_deviation(steps + g, g % 2)

        @block.tensor
        def _(pe):
            def turn(i, g):
                pe.wait_ge(normed, i + 1)
                if reached(i, 1):
                    pe.wait_ge(xnT_ready, i * 2)
                for h in range(2):
                    for t in range(TG):
                        last = pe.transpose(turn_ps[:, h, t * 128:(t + 1) * 128],
                                            xn[:, t, h * HALF:(h + 1) * HALF], ident[:])
                    last.then_inc(turned, 1)

            def ring_free(i, k):
                if k == 0:
                    if reached(i, 1):
                        pe.wait_ge(x2_sg_done, i * C)
                elif k < 4:
                    if reached(i, 2):
                        pe.wait_ge(dt_sg_done, (i - 2) * C + k)
                elif k < 7:
                    pe.wait_ge(conv_done, i * C + (k - 3))
                else:
                    pe.wait_ge(x2_sg_done, i * C + (k - 6))

            def in_projection(i, layer, g):
                if g == 0:
                    pe.wait_ge(in_w_loaded, (layer + 1) * 16)
                pe.wait_ge(xnT_ready, (i + 1) * 2)
                for k in range(IN):
                    ring_free(i, k)
                    for h in range(2):
                        mm = pe.matmul(ring_ps[:, (g * (IN + C) + k) % 4, :], in_w[:, h, k * HALF:(k + 1) * HALF],
                                       xnT[:, h, :], start=(h == 0), stop=(h == 1))
                    mm.then_inc(in_done, 1)

            def dt_product(i, g_now, layer, g, free):
                if g == 0:
                    pe.wait_ge(dt_w_loaded, (layer + 1) * 16)
                pe.wait_ge(ssm_ready, (i + 1) * C)
                for m in range(C):
                    free(m)
                    for c in range(C):
                        mm = pe.matmul(ring_ps[:, (g_now * (IN + C) + IN + m) % 4, :], dt_w[:, c, m * HALF:(m + 1) * HALF],
                                       ssm[:, g % 2, c, :], start=(c == 0), stop=(c == C - 1))
                    mm.then_inc(dt_done, 1)

            def out_product(i, layer, g):
                if g == 0:
                    pe.wait_ge(out_w_ready, layer + 1)
                pe.wait_ge(xg_ready, (i + 1) * C)
                if reached(i, 1):
                    pe.wait_ge(added, i)
                for t in range(TG):
                    for c in range(C):
                        mm = pe.matmul(out_ps[:, t, 0:D], xg[:, c, t * 128:(t + 1) * 128], out_w[:, c, :],
                                       start=(c == 0), stop=(c == C - 1))
                mm.then_inc(out_done, 1)

            pe.wait_ge(const_loaded, 16 * 7)
            turn(0, 0)

            def step(i, layer, g):
                in_projection(i, layer, g)
                if reached(i, 2):
                    out_product(i - 2, layer if g >= 2 else layer - 1, (g - 2) % groups)
                if not (isinstance(i, int) and i == steps - 1):
                    turn(i + 1, (g + 1) % groups)
                if reached(i, 1):
                    dt_product(i - 1, g, layer if g >= 1 else layer - 1, (g - 1) % groups,
                               lambda m: ring_free(i, IN + m))

            over_steps(pe, step)
            out_product(steps - 2, LAYERS - 1, groups - 2)
            pe.wait_ge(conv_done, steps * C)
            pe.wait_ge(x2_sg_done, steps * C)
            pe.wait_ge(dt_sg_done, (steps - 1) * C)
            dt_product(steps - 1, 0, LAYERS - 1, groups - 1, lambda m: None)
            out_product(steps - 1, LAYERS - 1, groups - 1)

        @block.scalar
        def _(act):
            def take_turned(i, layer):
                if reached(i, 1):
                    act.wait_ge(in_done, i * IN)
                for h in range(2):
                    act.wait_ge(turned, i * 2 + (h + 1))
                    act.sem_inc(wait_carrier, 1)
                    act.activation(xnT[:, h, :], turn_ps[:, h, :], ACT.Identity, scale=ln_gb[:, layer, 0, h:h + 1],
                                   bias=ln_gb[:, layer, 1, h:h + 1]).then_inc(xnT_ready, 1)

            def gate_sigmoids(i, layer, g, slot_g):
                for m in range(C):
                    act.wait_ge(dt_done, i * C + (m + 1))
                    if m == 0 and reached(i, 1):
                        act.wait_ge(gate_done, i * C)
                    act.sem_inc(wait_carrier, 1)
                    act.activation(dt_sg[:, m, :], ring_ps[:, (slot_g * (IN + C) + IN + m) % 4, :], ACT.Sigmoid,
                                   bias=dt_bias[:, layer, m:m + 1]).then_inc(dt_sg_done, 1)

            act.wait_ge(const_loaded, 16 * 7)
            act.wait_ge(dt_bias_set, 1)
            take_turned(0, 0)

            def step(i, layer, g):
                for c in range(C):
                    act.wait_ge(in_done, i * IN + (C + c + 1))
                    if c == 0 and reached(i, 2):
                        act.wait_ge(xg_ready, (i - 1) * C)
                    act.activation(x2_sg[:, g % 2, c, :], ring_ps[:, (g * (IN + C) + C + c) % 4, :],
                                   ACT.Sigmoid).then_inc(x2_sg_done, 1)
                for c in range(C):
                    act.wait_ge(conv_done, i * C + (c + 1))
                    if c == 0 and reached(i, 1):
                        act.wait_ge(ssm_ready, i * C)
                    act.activation(conv_sg[:, c, :], conv[:, c, :], ACT.Sigmoid).then_inc(conv_sg_done, 1)
                if not (isinstance(i, int) and i == steps - 1):
                    take_turned(i + 1, next_layer(layer, g))
                if reached(i, 1):
                    gate_sigmoids(i - 1, layer if g >= 1 else layer - 1, (g - 1) % groups, g)

            over_steps(act, step)
            gate_sigmoids(steps - 1, LAYERS - 1, groups - 1, 0)

        @block.vector
        def _(dve):
            def statistics(n, g, par):
                for t in range(TG):
                    s = dve.bn_stats(stats[:, t, :], x[:, g * TG + t, :])
                s.then_inc(stats_done, 1)
                dve.wait_ge(stats_done, n + 1)
                dve.sem_inc(wait_carrier, 1)
                for t in range(TG):
                    s = dve.bn_aggr(mv[:, par, t, :], stats[:, t, :])
                s.then_inc(var_ready, 1)

            def normalise(n, g, par):
                dve.wait_ge(rstd_ready, n + 1)
                if reached(n, 1):
                    dve.wait_ge(turned, n * 2)
                for t in range(TG):
                    s = dve.tensor_scalar(xn[:, t, :], x[:, g * TG + t, :], mv[:, par, t, 0:1], rstd[:, par, t:t + 1],
                                          ALU.subtract, ALU.mult)
                s.then_inc(normed, 1)

            def convolve(i, layer, g):
                for c in range(C):
                    seq = ring_ps[:, (g * (IN + C) + c) % 4, :].rearrange("p (s l) -> p s l", l=T)
                    out = conv[:, c, :].rearrange("p (s l) -> p s l", l=T)
                    dve.wait_ge(in_done, i * IN + (c + 1))
                    dve.tensor_scalar(out, seq, taps[:, layer, c, 1:2], None, ALU.mult).then_inc(conv_tap, 1)
                    dve.wait_ge(conv_tap, i * (2 * C) + (2 * c + 1))
                    dve.scalar_tensor_tensor(out[:, :, 1:T], seq[:, :, 0:T - 1], taps[:, layer, c, 0:1], out[:, :, 1:T],
                                             ALU.mult, ALU.add).then_inc(conv_tap, 1)
                    dve.wait_ge(conv_tap, i * (2 * C) + (2 * c + 2))
                    dve.scalar_tensor_tensor(out[:, :, 0:T - 1], seq[:, :, 1:T], taps[:, layer, c, 2:3], out[:, :, 0:T - 1],
                                             ALU.mult, ALU.add).then_inc(conv_done, 1)

            def silu(i, g):
                if reached(i, 2):
                    dve.wait_ge(dt_done, (i - 1) * C)
                for c in range(C):
                    dve.wait_ge(conv_sg_done, i * C + (c + 1))
                    dve.tensor_tensor(ssm[:, g % 2, c, :], conv[:, c, :], conv_sg[:, c, :],
                                      ALU.mult).then_inc(ssm_ready, 1)

            def apply_gate(i, g):
                if reached(i, 1):
                    dve.wait_ge(out_done, i)
                for c in range(C):
                    dve.wait_ge(dt_sg_done, i * C + (c + 1))
                    dve.scalar_tensor_tensor(gate[:, c, :], dt_sg[:, c, :], 1.0, x2_sg[:, g % 2, c, :],
                                             ALU.add, ALU.mult).then_inc(gate_done, 1)
                for c in range(C):
                    dve.wait_ge(gate_done, i * C + (c + 1))
                    dve.tensor_tensor(xg[:, c, :], gate[:, c, :], ssm[:, g % 2, c, :], ALU.mult).then_inc(xg_ready, 1)

            def add_residual(i, g):
                dve.wait_ge(out_done, i + 1)
                dve.tensor_tensor(x[:, g * TG:(g + 1) * TG, :], x[:, g * TG:(g + 1) * TG, :], out_ps[:, :, 0:D],
                                  ALU.add).then_inc(added, 1)

            dve.wait_ge(const_loaded, 16 * 7)
            for t in range(tiles):
                dve.wait_ge(gathered, 16 * tiles)
                dve.tensor_tensor(x[:, t, :], x[:, t, :], pos[:], ALU.add).then_inc(embedded, 1)
            dve.wait_ge(embedded, tiles)
            statistics(0, 0, 0)
            normalise(0, 0, 0)

            def step(i, layer, g):
                more = not (isinstance(i, int) and i == steps - 1)
                if more:
                    if reached(i, 3):
                        dve.wait_ge(added, i - 2)
                    statistics(i + 1, (g + 1) % groups, (g + 1) % 2)
                convolve(i, layer, g)
                if reached(i, 2):
                    add_residual(i - 2, (g - 2) % groups)
                if more:
                    normalise(i + 1, (g + 1) % groups, (g + 1) % 2)
                silu(i, g)
                if reached(i, 1):
                    apply_gate(i - 1, (g - 1) % groups)

            over_steps(dve, step)
            add_residual(steps - 2, groups - 2)
            apply_gate(steps - 1, groups - 1)
            add_residual(steps - 1, groups - 1)

            for g in range(groups):
                dve.wait_ge(added, steps)
                statistics(steps + g, g, g % 2)
                dve.wait_ge(rstd_ready, steps + g + 1)
                if g == 0:
                    dve.wait_ge(turned, 2 * steps)
                else:
                    dve.wait_ge(scaled, g)
                for t in range(TG):
                    s = dve.tensor_scalar(xn[:, t, :], x[:, g * TG + t, :], mv[:, g % 2, t, 0:1],
                                          rstd[:, g % 2, t:t + 1], ALU.subtract, ALU.mult)
                s.then_inc(normed, 1)
                dve.wait_ge(normed, steps + g + 1)
                for t in range(TG):
                    s = dve.tensor_tensor(x[:, g * TG + t, :], xn[:, t, :], final_g[:], ALU.mult)
                s.then_inc(scaled, 1)
                dve.wait_ge(scaled, g + 1)
                for t in range(TG):
                    s = dve.tensor_tensor(x[:, g * TG + t, :], x[:, g * TG + t, :], final_b[:], ALU.add)
                s.then_inc(final_ready, 1)


PAIR = 2 * SEQ
HEADS = 8
TILES = TOKENS // PAIR
SCALING = float(D) ** 0.5


def attention_stage(nc, io):
    GB = 4
    GT = GB * SEQ
    groups = BATCH // GB
    ROWS = SEQ * HEADS
    PAIRS = ROWS // PAIR
    BLOCKS = 3 * HEADS // 2 * 3
    SLOTS = BLOCKS + 1
    BPS = BLOCKS // GB
    STAGES = 3
    PART = 6
    PARTS = BLOCKS // PART
    BIG, SMALL = 128, D - 128

    with ExitStack() as ctx:
        def sb(name, shape, dt=F32):
            return ctx.enter_context(nc.sbuf_tensor("att_sb_" + name, shape, dt))

        def ps(name, shape):
            return ctx.enter_context(nc.psum_tensor("att_ps_" + name, shape, F32))

        def sem(name):
            return ctx.enter_context(nc.semaphore("att_" + name))

        ident = sb("ident", [128, 128])
        qkv_w_high = sb("qkv_w_high", [HALF, 2, BLOCKS, 128], F32R)
        qkv_w_low = sb("qkv_w_low", [HALF, 2, BLOCKS, 128], F32R)
        qkv_b = sb("qkv_b", [128, BLOCKS])
        proj_w = sb("proj_w", [HALF, 2 * HEADS, D])
        proj_b = sb("proj_b", [PAIR, D])
        mask_f = sb("mask_f", [2, 2, PAIR])
        mask = sb("mask", [2, 2, PAIR], BF16)
        h_in = sb("h_in", [PAIR, 2, 2, D])
        minus_half = sb("minus_half", [PAIR, 2])
        stats = sb("stats", [PAIR, 2, 6])
        mv = sb("mv", [PAIR, 2, 2])
        var_eps = sb("var_eps", [PAIR, 2])
        rstd = sb("rstd", [PAIR, 2])
        xn = sb("xn", [PAIR, 2, D])
        xnT_high = sb("xnT_high", [HALF, 2, GT], F32R)
        xnT_low = sb("xnT_low", [HALF, 2, GT], F32R)
        big = sb("big", [BIG, 2, 3, GT * HEADS])
        small = sb("small", [2 * SMALL, 3, GT * HEADS])
        h1 = sb("h1", [PAIR, 2, 2, D])
        v_rows = sb("v_rows", [PAIR, PAIRS, D])
        row_max = sb("row_max", [PAIR, PAIRS])
        row_sum = sb("row_sum", [PAIR, PAIRS])
        sum_scaled = sb("sum_scaled", [PAIR, PAIRS])
        inv_sum = sb("inv_sum", [PAIR, PAIRS])
        probs = sb("probs", [PAIR, 2, PAIRS, PAIR])
        probsT = sb("probsT", [PAIR, PAIRS, PAIR])
        outT = sb("outT", [HALF, 2, 2, 2 * ROWS])
        ring_ps = ps("ring_ps", [128, 2, 512])
        score_ps = ps("score_ps", [PAIR, 512])
        v_ps = ps("v_ps", [PAIR, 2, 256])
        probsT_ps = ps("probsT_ps", [PAIR, 512])
        out_ps = ps("out_ps", [HALF, 2, 512])
        proj_ps = ps("proj_ps", [PAIR, 512])

        const_loaded = sem("const_loaded")
        wait_carrier = sem("wait_carrier")
        qkv_w_loaded = [sem("qkv_w_loaded_%d" % i) for i in range(STAGES)]
        qkv_w_high_ready = sem("qkv_w_high_ready")
        qkv_w_ready = sem("qkv_w_ready")
        xnT_low_ready = sem("xnT_low_ready")
        proj_w_loaded = sem("proj_w_loaded")
        h_loaded = [sem("h_loaded_even"), sem("h_loaded_odd")]
        half_set = sem("half_set")
        mask_ready = sem("mask_ready")
        stats_done = sem("stats_done")
        var_ready = sem("var_ready")
        eps_added = sem("eps_added")
        rstd_ready = sem("rstd_ready")
        normed = sem("normed")
        h_biased = sem("h_biased")
        ring_done = sem("ring_done")
        ring_read = sem("ring_read")
        scored = sem("scored")
        max_done = sem("max_done")
        shifted = sem("shifted")
        exp_done = sem("exp_done")
        sum_step = sem("sum_step")
        probs_ready = sem("probs_ready")
        probs_turned = sem("probs_turned")
        probsT_ready = sem("probsT_ready")
        v_turned = sem("v_turned")
        v_ready = sem("v_ready")
        out_done = sem("out_done")
        outT_ready = sem("outT_ready")
        proj_done = sem("proj_done")
        h1_ready = sem("h1_ready")
        h1_stored = [sem("h1_stored_even"), sem("h1_stored_odd")]

        def over_groups(eng, body):
            body(0, 0)
            body(1, 1)
            with eng.Fori(1, groups // 2 - 1) as k:
                body(k * 2, 0)
                body(k * 2 + 1, 1)
            body(groups - 2, 0)
            body(groups - 1, 1)

        def exists(group, ahead):
            return not (isinstance(group, int) and group + ahead >= groups)

        block = ctx.enter_context(nc.Block())

        def staged(part):
            size = 2 * PART * 128
            at = (part % STAGES) * size
            return (big[0:HALF, 1].rearrange("p k n -> p (k n)")[:, at:at + size]
                    .rearrange("p (h b f) -> p h b f", h=2, b=PART))

        def small_at(par, kind):
            return small[par * SMALL:(par + 1) * SMALL, kind, :]

        @block.sync
        def _(sp):
            def store(group, par):
                sp.wait_ge(h1_ready, group * 2 + 2)
                sp.sem_inc(wait_carrier, 1)
                sp.dma_start(io["out"][bass.ds(group * GT, GT), :].rearrange("(t p) d -> p t d", p=PAIR), h1[:, par]
                             ).then_inc(h1_stored[par], 16)

            def load(group, par):
                if reached(group, 2):
                    sp.wait_ge(h_biased, group - 1)
                    sp.wait_ge(normed, group - 1)
                    sp.sem_inc(wait_carrier, 1)
                sp.dma_start(h_in[:, par], io["h"][bass.ds(group * GT, GT), :].rearrange("(t p) d -> p t d", p=PAIR)
                             ).then_inc(h_loaded[par], 16)

            load(0, 0)
            load(1, 1)
            for dst, name in ((ident, "ident"), (qkv_b, "qkv_b"), (proj_b, "proj_b"), (mask_f, "mask")):
                sp.dma_start(dst[:], io[name]).then_inc(const_loaded, 16)
            for part in range(PARTS):
                if part >= STAGES:
                    sp.wait_ge(qkv_w_ready, part - STAGES + 1)
                sp.dma_start(staged(part), io["qkv_w"][:, :, part * PART:(part + 1) * PART, :]
                             ).then_inc(qkv_w_loaded[part % STAGES], 16)
            sp.dma_start(proj_w[:], io["proj_w"]).then_inc(proj_w_loaded, 16)
            load(2, 0)
            store(0, 0)
            load(3, 1)
            with sp.Fori(2, groups // 2) as k:
                store(k * 2 - 3, 1)
                load(k * 2, 0)
                store(k * 2 - 2, 0)
                load(k * 2 + 1, 1)
            store(groups - 3, 1)
            store(groups - 2, 0)
            store(groups - 1, 1)
            for par in range(2):
                sp.wait_ge(h1_stored[par], 16 * (groups // 2))

        @block.gpsimd
        def _(pool):
            pool.memset(minus_half[:], -0.5).then_inc(half_set, 1)
            pool.wait_ge(half_set, 1)
            pool.wait_ge(const_loaded, 16 * 4)

            def rstd_of(group):
                pool.wait_ge(var_ready, group + 1)
                pool.sem_inc(wait_carrier, 1)
                pool.tensor_scalar(var_eps[:], mv[:, :, 1], EPS, None, ALU.add).then_inc(eps_added, 1)
                pool.wait_ge(eps_added, group + 1)
                if reached(group, 1):
                    pool.wait_ge(normed, group)
                pool.tensor_tensor(rstd[:], var_eps[:], minus_half[:], ALU.pow).then_inc(rstd_ready, 1)

            def add_bias(group, par, k):
                pool.wait_ge(h_loaded[par], (k + 1) * 16)
                if reached(group, 2):
                    pool.wait_ge(h1_stored[par], k * 16)
                for t in range(2):
                    last = pool.tensor_tensor(h1[:, par, t, :], h_in[:, par, t, :], proj_b[:], ALU.add)
                last.then_inc(h_biased, 1)

            rstd_of(0)
            rstd_of(1)
            add_bias(0, 0, 0)
            rstd_of(2)
            add_bias(1, 1, 0)
            rstd_of(3)
            add_bias(2, 0, 1)
            with pool.Fori(2, groups // 2) as k:
                rstd_of(k * 2)
                add_bias(k * 2 - 1, 1, k - 1)
                rstd_of(k * 2 + 1)
                add_bias(k * 2, 0, k)
            add_bias(groups - 1, 1, groups // 2 - 1)

        @block.tensor
        def _(pe):
            def ring_slot(group, par, s):
                n = group * SLOTS + s
                if not (isinstance(n, int) and n < 2):
                    pe.wait_ge(ring_read, n - 1)
                return ring_ps[:, (par * SLOTS + s) % 2, :]

            def turn(group, par):
                pe.wait_ge(normed, group + 1)
                slot = ring_slot(group, par, 0)
                for h in range(2):
                    for t in range(2):
                        last = pe.transpose(slot[0:HALF, h * GT + t * PAIR:h * GT + (t + 1) * PAIR],
                                            xn[:, t, h * HALF:(h + 1) * HALF], ident[0:PAIR, 0:PAIR])
                last.then_inc(ring_done, 1)

            def project_in(group, par, blocks):
                for blk in blocks:
                    slot = ring_slot(group, par, 1 + blk)
                    if blk == 0:
                        pe.wait_ge(ring_read, group * SLOTS + 1)
                        pe.wait_ge(xnT_low_ready, group + 1)
                    parts = [(w, x, h) for w, x in ((qkv_w_low, xnT_high), (qkv_w_high, xnT_low),
                                                    (qkv_w_high, xnT_high)) for h in range(2)]
                    for n, (w, x, h) in enumerate(parts):
                        mm = pe.matmul(slot[:, 0:GT], w[:, h, blk, :], x[:, h, :], start=(n == 0),
                                       stop=(n == len(parts) - 1))
                    mm.then_inc(ring_done, 1)

            def scores(b, par, j):
                if reached(b, 1):
                    pe.wait_ge(shifted, b)
                for p in range(PAIRS):
                    r = slice(j * ROWS + p * PAIR, j * ROWS + (p + 1) * PAIR)
                    out = score_ps[:, p * PAIR:(p + 1) * PAIR]
                    pe.matmul(out, mask[:, 0, :], mask[:, 1, :], start=True, stop=False)
                    pe.matmul(out, big[:, par, 0, r], big[:, par, 1, r], start=False, stop=False)
                    mm = pe.matmul(out, small_at(par, 0)[:, r], small_at(par, 1)[:, r], start=False, stop=True)
                mm.then_inc(scored, 1)

            def turn_probs(b, j):
                pe.wait_ge(probs_ready, b + 1)
                if reached(b, 1):
                    pe.wait_ge(probsT_ready, b)
                for p in range(PAIRS):
                    last = pe.transpose(probsT_ps[:, p * PAIR:(p + 1) * PAIR], probs[:, j % 2, p, :],
                                        ident[0:PAIR, 0:PAIR])
                last.then_inc(probs_turned, 1)

            def turn_values(b, par, j, rnd):
                if reached(b, 1) or rnd:
                    pe.wait_ge(v_ready, b * 2 + rnd)
                for p in range(2):
                    at = j * ROWS + (2 * rnd + p) * PAIR
                    pe.transpose(v_ps[:, p, 0:BIG], big[:, par, 2, at:at + PAIR], ident[:])
                    half = slice(par * SMALL, (par + 1) * SMALL)
                    last = pe.transpose(v_ps[:, p, BIG:D], small[half, 2, at:at + PAIR], ident[half, half])
                last.then_inc(v_turned, 1)

            def mix_values(b):
                pe.wait_ge(probsT_ready, b + 1)
                pe.wait_ge(v_ready, b * 2 + 2)
                if reached(b, 1):
                    pe.wait_ge(outT_ready, b)
                for h in range(2):
                    for p in range(PAIRS):
                        mm = pe.matmul(out_ps[:, h, p * PAIR:(p + 1) * PAIR], v_rows[:, p, h * HALF:(h + 1) * HALF],
                                       probsT[:, p, :], start=True, stop=True)
                mm.then_inc(out_done, 1)

            def project_out(pair, pair_par):
                pe.wait_ge(outT_ready, pair * 2 + 2)
                if reached(pair, 1):
                    pe.wait_ge(h1_ready, pair)
                rows = outT[:, pair_par].rearrange("p h (n c) -> p h c n", c=HEADS)
                for c in range(HEADS):
                    for h in range(2):
                        mm = pe.matmul(proj_ps[:, 0:D], rows[:, h, c, :], proj_w[:, 2 * c + h, :],
                                       start=(c + h == 0), stop=(c == HEADS - 1 and h == 1))
                mm.then_inc(proj_done, 1)

            def body(group, par):
                for j in range(GB):
                    b = group * GB + j
                    last_par = par if j else 1 - par
                    last_j = (j - 1) % GB
                    if j == 0:
                        if exists(group, 1):
                            turn(group + 1, 1 - par)
                        pe.wait_ge(ring_read, (group + 1) * SLOTS)
                    scores(b, par, j)
                    if j % 2 == 1 and reached(b, 3):
                        project_out(group * 2 + (j // 2 - 1), (j // 2 + 1) % 2)
                    if reached(b, 1):
                        turn_probs(b - 1, last_j)
                    for part in range(3):
                        if exists(group, 1):
                            project_in(group + 1, 1 - par, range(j * BPS + 3 * part, j * BPS + 3 * part + 3))
                        if part < 2 and reached(b, 1):
                            turn_values(b - 1, last_par, last_j, part)
                    if reached(b, 1):
                        mix_values(b - 1)

            pe.wait_ge(const_loaded, 16 * 4)
            turn(0, 0)
            pe.wait_ge(mask_ready, 1)
            for part in range(PARTS):
                pe.wait_ge(qkv_w_ready, part + 1)
                project_in(0, 0, range(part * PART, (part + 1) * PART))
            pe.wait_ge(proj_w_loaded, 16)
            over_groups(pe, body)
            turn_probs(BATCH - 1, GB - 1)
            for rnd in range(2):
                turn_values(BATCH - 1, 1, GB - 1, rnd)
            mix_values(BATCH - 1)
            project_out(TILES - 1, 1)

        @block.scalar
        def _(act):
            def take_turned(group, par):
                act.wait_ge(ring_done, group * SLOTS + 1)
                act.activation(xnT_high[:].rearrange("p h n -> p (h n)"), ring_ps[0:HALF, (par * SLOTS) % 2, 0:2 * GT],
                               ACT.Copy).then_inc(ring_read, 1)

            def take_blocks(group, par, blocks):
                for blk in blocks:
                    kind, rest = divmod(blk, BLOCKS // 3)
                    cp, third = divmod(rest, 3)
                    slot = ring_ps[:, (par * SLOTS + 1 + blk) % 2, 0:GT]
                    wide = big[:, par, kind, :].rearrange("p (n c) -> p c n", c=HEADS)
                    narrow = small_at(par, kind).rearrange("p (n c) -> p c n", c=HEADS)
                    act.wait_ge(ring_done, group * SLOTS + (2 + blk))
                    if blk == 0 and reached(group, 2):
                        act.wait_ge(scored, (group - 1) * GB)
                    if blk == 2 * BLOCKS // 3 and reached(group, 2):
                        act.wait_ge(v_turned, (group - 1) * (2 * GB))
                    if third < 2:
                        act.activation(wide[:, 2 * cp + third, :], slot, ACT.Identity,
                                       bias=qkv_b[:, blk:blk + 1]).then_inc(ring_read, 1)
                    else:
                        act.activation(narrow[:, 2 * cp, :], slot[0:SMALL, :], ACT.Identity,
                                       bias=qkv_b[0:SMALL, blk:blk + 1])
                        act.activation(narrow[:, 2 * cp + 1, :], slot[SMALL:128, :], ACT.Identity,
                                       bias=qkv_b[SMALL:128, blk:blk + 1]).then_inc(ring_read, 1)

            def take_mixed(b, pair, j):
                act.wait_ge(out_done, b + 1)
                if j % 2 == 0 and reached(pair, 2):
                    act.wait_ge(proj_done, pair - 1)
                act.activation(outT[:, (j // 2) % 2, :, (j % 2) * ROWS:(j % 2 + 1) * ROWS], out_ps[:, :, 0:ROWS],
                               ACT.Copy).then_inc(outT_ready, 1)

            def body(group, par):
                for j in range(GB):
                    b = group * GB + j
                    if j == 0 and exists(group, 1):
                        take_turned(group + 1, 1 - par)
                    first = 1 - j % 2
                    if exists(group, 1):
                        take_blocks(group + 1, 1 - par, range(j * BPS, j * BPS + first))
                    act.wait_ge(shifted, b + 1)
                    act.activation(probs[:, j % 2], probs[:, j % 2], ACT.Exp).then_inc(exp_done, 1)
                    if exists(group, 1):
                        take_blocks(group + 1, 1 - par, range(j * BPS + first, (j + 1) * BPS))
                    if reached(b, 1):
                        take_mixed(b - 1, group * 2 + ((j + 1) // 2 - 1), (j - 1) % GB)

            act.wait_ge(const_loaded, 16 * 4)
            take_turned(0, 0)
            for part in range(PARTS):
                act.wait_ge(qkv_w_loaded[part % STAGES], (part // STAGES + 1) * 16)
                act.activation(qkv_w_high[:, :, part * PART:(part + 1) * PART, :], staged(part), ACT.Copy
                               ).then_inc(qkv_w_high_ready, 1)
            take_blocks(0, 0, range(BLOCKS))
            over_groups(act, body)
            take_mixed(BATCH - 1, TILES - 1, GB - 1)

        @block.vector
        def _(dve):
            def statistics(group, par, count):
                dve.wait_ge(h_loaded[par], count * 16)
                for t in range(2):
                    s = dve.bn_stats(stats[:, t, :], h_in[:, par, t, :])
                s.then_inc(stats_done, 1)
                dve.wait_ge(stats_done, group + 1)
                if reached(group, 1):
                    dve.wait_ge(rstd_ready, group)
                dve.sem_inc(wait_carrier, 1)
                for t in range(2):
                    s = dve.bn_aggr(mv[:, t, :], stats[:, t, :])
                s.then_inc(var_ready, 1)

            def normalise(group, par):
                dve.wait_ge(rstd_ready, group + 1)
                if reached(group, 1):
                    dve.wait_ge(ring_done, (group - 1) * SLOTS + 1)
                for t in range(2):
                    s = dve.tensor_scalar(xn[:, t, :], h_in[:, par, t, :], mv[:, t, 0:1], rstd[:, t:t + 1],
                                          ALU.subtract, ALU.mult)
                s.then_inc(normed, 1)

            def take_turned(group, par):
                dve.wait_ge(ring_read, group * SLOTS + 1)
                dve.sem_inc(wait_carrier, 1)
                dve.tensor_tensor(xnT_low[:].rearrange("p h n -> p (h n)"), ring_ps[0:HALF, (par * SLOTS) % 2, 0:2 * GT],
                                  xnT_high[:].rearrange("p h n -> p (h n)"), ALU.subtract).then_inc(xnT_low_ready, 1)

            def add_residual(pair, par, t):
                dve.wait_ge(proj_done, pair + 1)
                dve.tensor_tensor(h1[:, par, t, :], h1[:, par, t, :], proj_ps[:, 0:D], ALU.add).then_inc(h1_ready, 1)

            def wide(small_tile):
                return small_tile[:].unsqueeze(2).to_broadcast([PAIR, PAIRS, PAIR])

            def take_turned_probs(b):
                dve.wait_ge(probs_turned, b + 1)
                if reached(b, 1):
                    dve.wait_ge(out_done, b)
                dve.tensor_copy(probsT[:], probsT_ps[:, 0:ROWS].rearrange("q (p k) -> q p k", k=PAIR)
                                ).then_inc(probsT_ready, 1)

            def take_values(b, rnd):
                dve.wait_ge(v_turned, b * 2 + rnd + 1)
                dve.tensor_copy(v_rows[:, 2 * rnd:2 * rnd + 2, :], v_ps[:, :, 0:D]).then_inc(v_ready, 1)

            def body(group, par, k):
                for j in range(GB):
                    b = group * GB + j
                    if j == 0 and exists(group, 1):
                        take_turned(group + 1, 1 - par)
                    p = probs[:, j % 2]
                    score = score_ps[:, 0:ROWS].rearrange("q (p k) -> q p k", k=PAIR)
                    dve.wait_ge(scored, b + 1)
                    dve.tensor_reduce(row_max[:], score, AX_X, ALU.max).then_inc(max_done, 1)
                    dve.wait_ge(max_done, b + 1)
                    if reached(b, 2):
                        dve.wait_ge(probs_turned, b - 1)
                    dve.tensor_tensor(p, score, wide(row_max), ALU.subtract).then_inc(shifted, 1)
                    if j % 2 == 1 and reached(b, 3):
                        if j == 1:
                            dve.wait_ge(h_biased, group)
                            add_residual(group * 2 - 1, 1 - par, 1)
                        else:
                            dve.wait_ge(h_biased, group + 1)
                            add_residual(group * 2, par, 0)
                    if reached(b, 1):
                        take_turned_probs(b - 1)
                    dve.wait_ge(exp_done, b + 1)
                    dve.tensor_reduce(row_sum[:], p, AX_X, ALU.add).then_inc(sum_step, 1)
                    dve.wait_ge(sum_step, b * 3 + 1)
                    dve.tensor_scalar(sum_scaled[:], row_sum[:], SCALING, None, ALU.mult).then_inc(sum_step, 1)
                    dve.wait_ge(sum_step, b * 3 + 2)
                    dve.reciprocal(inv_sum[:], sum_scaled[:]).then_inc(sum_step, 1)
                    dve.wait_ge(sum_step, b * 3 + 3)
                    dve.tensor_tensor(p, p, wide(inv_sum), ALU.mult).then_inc(probs_ready, 1)
                    if reached(b, 1):
                        take_values(b - 1, 0)
                        take_values(b - 1, 1)
                    if j == 2 and exists(group, 2):
                        statistics(group + 2, par, k + 2)
                    if j == 3 and exists(group, 2):
                        normalise(group + 2, par)

            dve.wait_ge(const_loaded, 16 * 4)
            dve.tensor_copy(mask[:], mask_f[:]).then_inc(mask_ready, 1)
            statistics(0, 0, 1)
            normalise(0, 0)
            statistics(1, 1, 1)
            take_turned(0, 0)
            for part in range(PARTS):
                dve.wait_ge(qkv_w_high_ready, part + 1)
                high = qkv_w_high[:, :, part * PART:(part + 1) * PART, :]
                dve.tensor_tensor(qkv_w_low[:, :, part * PART:(part + 1) * PART, :], staged(part), high, ALU.subtract
                                  ).then_inc(qkv_w_ready, 1)
            normalise(1, 1)
            body(0, 0, 0)
            body(1, 1, 0)
            with dve.Fori(1, groups // 2 - 1) as k:
                body(k * 2, 0, k)
                body(k * 2 + 1, 1, k)
            body(groups - 2, 0, groups // 2 - 1)
            body(groups - 1, 1, groups // 2 - 1)
            take_turned_probs(BATCH - 1)
            take_values(BATCH - 1, 0)
            take_values(BATCH - 1, 1)
            dve.wait_ge(h_biased, groups)
            add_residual(TILES - 1, 1, 1)


IMG = 84
GRID = 7
REG = IMG // GRID
C0, C1, C2 = 3, 12, 48


def image_stage(nc, io):
    B8, G4 = 8, 4
    CH = B8 * C1
    XW = IMG + 2
    XP = REG * XW
    PITCH = REG + 1
    GP = PITCH * PITCH
    LEAD = PITCH + 1
    RP = LEAD + G4 * GP + 2
    WROWS = G4 * PITCH - 1
    RPX = REG * REG
    PIECES = 2 * G4
    PROWS = REG // 2
    OY, OX = REG // 4, 20
    TAPS = 16
    RUN = G4 * OY * OX
    PAIRED = [(0, 1), (2, 3), (4, 5), (6,)]
    units = 2 * GRID
    P_PW, P_SC = 0, GRID * CH
    P_DW = 2 * GRID * CH
    P_SDW = P_DW + 9 * GRID
    P_BDW, P_BPW, P_LEN = P_SDW + GRID, P_SDW + 2 * GRID, P_SDW + 3 * GRID

    with ExitStack() as ctx:
        def sb(name, shape, dt=F32):
            return ctx.enter_context(nc.sbuf_tensor("img_sb_" + name, shape, dt))

        def ps(name, shape):
            return ctx.enter_context(nc.psum_tensor("img_ps_" + name, shape, F32))

        def sem(name):
            return ctx.enter_context(nc.semaphore("img_" + name))

        w0 = sb("w0", [B8 * C0 * 3, 3, CH])
        sb0 = sb("sb0", [CH, 2])
        w1 = sb("w1", [CH, 2, 64])
        sb1 = sb("sb1", [128, 2])
        w2 = sb("w2", [128, 4, 128])
        sb2 = sb("sb2", [128, 2])
        w3 = sb("w3", [128, 4, D])
        sb3 = sb("sb3", [128, 2, D])
        x = sb("x", [B8 * C0 * 3, 2, G4, XP])
        y0 = sb("y0", [CH, 2, GRID, RP])
        par = sb("par", [CH, 2, P_LEN])
        acc = sb("acc", [CH, 2, G4 * GP])
        y1 = sb("y1", [CH, 2, G4 * RPX])
        y2 = sb("y2", [CH, 2, G4 * RPX])
        taps = sb("taps", [128, TAPS * RUN])
        cols = sb("cols", [CH, 2, B8, RUN])
        z1 = sb("z1", [128, 4, 2 * G4, GRID * OY * OX])
        tok = sb("tok", [4 * IMG_LEN, 4, D])
        c0_ps = ps("c0_ps", [128, 2, 512])
        pw_ps = ps("pw_ps", [128, 2, G4, 256])
        c1_ps = ps("c1_ps", [128, 2, 512])
        z2 = taps[:, 0:4 * 32 * IMG_LEN].rearrange("p (t n) -> p t n", t=4)

        const_loaded = sem("const_loaded")
        wait_carrier = sem("wait_carrier")
        x_loaded = [sem("x_loaded_half0"), sem("x_loaded_half1")]
        par_loaded = [sem("par_loaded_even"), sem("par_loaded_odd")]
        pads_set = sem("pads_set")
        pw_scaled = sem("pw_scaled")
        conv0_done = sem("conv0_done")
        y0_ready = sem("y0_ready")
        dw_tap = sem("dw_tap")
        dw_done = sem("dw_done")
        y1_ready = sem("y1_ready")
        pw_done = sem("pw_done")
        y2_ready = sem("y2_ready")
        taps_ready = sem("taps_ready")
        taps_stored = sem("taps_stored")
        cols_loaded = sem("cols_loaded")
        conv1_done = sem("conv1_done")
        z1_ready = sem("z1_ready")
        conv2_done = sem("conv2_done")
        z2_ready = sem("z2_ready")
        conv3_done = sem("conv3_done")
        tok_scaled = sem("tok_scaled")
        tok_ready = sem("tok_ready")
        h_stored = [sem(f"h_stored_{i}") for i in range(4)]

        def over_units(eng, body):
            for hf in range(2):
                body(0, 0, 0, hf)
            with eng.Fori(0, 2) as k:
                for hf in range(2):
                    body(k * 2 + 1, k, 1, hf)
                for hf in range(2):
                    body(k * 2 + 2, k + 1, 0, hf)
            for s in (GRID - 2, GRID - 1):
                for hf in range(2):
                    body(s, s // 2, s % 2, hf)

        def is_last(s):
            return isinstance(s, int) and s == GRID - 1

        def has_next(s, hf):
            return not (is_last(s) and hf == 1)

        def window(half, gx, ky, kx):
            at = LEAD + (ky - 1) * PITCH + (kx - 1)
            return y0[:, half, gx, at:at + WROWS * PITCH].rearrange("p (r c) -> p r c", c=PITCH)[:, :, 0:REG]

        def pixels(tile):
            return tile.rearrange("p (g r c) -> p g r c", r=PITCH, c=PITCH)[:, :, 0:REG, 0:REG]

        block = ctx.enter_context(nc.Block())

        @block.sync
        def _(sp):
            def load_x(s, half):
                for dy in range(3):
                    src = io["img_x"][:, half * G4:(half + 1) * G4, bass.ds((s * REG + dy) * XW, XP)]
                    sp.dma_start(x[dy * B8 * C0:(dy + 1) * B8 * C0, half], src).then_inc(x_loaded[half], 16)

            def load_par(s, parity):
                sp.dma_start(par[:, parity], io["img_par"][s]).then_inc(par_loaded[parity], 16)

            def regroup(u, half):
                sp.wait_ge(taps_ready, (u + 1) * GRID)
                sp.dma_start(io["img_taps"][half], taps[0:CH, :]).then_inc(taps_stored, 16)
                sp.wait_ge(taps_stored, (u + 1) * 16)
                sp.sem_inc(wait_carrier, 1)
                if reached(u, 1):
                    sp.wait_ge(conv1_done, u)
                src = io["img_taps"][half].rearrange("(b k c) (t n) -> k c t b n", k=2, c=C1 // 2, n=RUN)
                for k in range(2):
                    sp.dma_start(cols[:, k], src[k].rearrange("c t b n -> (c t) b n")).then_inc(cols_loaded, 16)

            load_x(0, 0)
            consts = ((w0, "img_w0"), (sb0, "img_sb0"), (w1, "img_w1"), (sb1, "img_sb1"), (w2, "img_w2"),
                      (sb2, "img_sb2"), (w3, "img_w3"), (sb3, "img_sb3"))
            for dst, name in consts:
                sp.dma_start(dst[:], io[name]).then_inc(const_loaded, 16)
            load_par(0, 0)
            load_x(0, 1)

            def body(s, sc, parity, hf):
                u = s * 2 + hf
                if not is_last(s):
                    sp.wait_ge(conv0_done, (u + 1) * PIECES)
                    sp.sem_inc(wait_carrier, 1)
                    load_x(s + 1, hf)
                    if hf == 0:
                        if reached(s, 1):
                            sp.wait_ge(taps_ready, u * GRID)
                            sp.sem_inc(wait_carrier, 1)
                        load_par(s + 1, 1 - parity)
                if reached(u, 1):
                    regroup(u - 1, 1 - hf)

            over_units(sp, body)
            regroup(units - 1, 1)

            def store(n):
                h, i = divmod(n, 8)
                b8 = h * 4 + i // 2
                sp.wait_ge(tok_ready, n + 1)
                rows = io["h"].rearrange("(g b t) d -> b g t d", b=B8, t=SEQ)
                for g in range(4):
                    sp.dma_start(rows[b8, (i % 2) * 4 + g, 0:IMG_LEN, :],
                                 tok[g * IMG_LEN:(g + 1) * IMG_LEN, n % 4, :]).then_inc(h_stored[n % 4], 16)

            for n in range(16):
                store(n)
            for done in h_stored:
                sp.wait_ge(done, 4 * 64)

        @block.gpsimd
        def _(pool):
            def scale_pointwise(s, sc, parity, hf):
                if hf == 0:
                    pool.wait_ge(par_loaded[parity], (sc + 1) * 16)
                    pool.tensor_tensor(par[:, parity, P_PW:P_PW + GRID * CH], par[:, parity, P_PW:P_PW + GRID * CH],
                                       par[:, parity, P_SC:P_SC + GRID * CH], ALU.mult).then_inc(pw_scaled, 1)

            over_units(pool, scale_pointwise)

        @block.tensor
        def _(pe):
            def conv0(u, half, x_count, pieces):
                for piece in pieces:
                    g, part = divmod(piece, 2)
                    if piece == 0:
                        pe.wait_ge(x_loaded[half], x_count)
                    if piece >= 2 or reached(u, 1):
                        pe.wait_ge(y0_ready, u * PIECES + (piece - 1))
                    rows = x[:, half, g, :].rearrange("p (r c) -> p r c", c=XW)[:, part * PROWS:(part + 1) * PROWS, :]
                    out = c0_ps[0:CH, piece % 2, 0:PROWS * IMG]
                    for dx in range(3):
                        mm = pe.matmul(out, w0[:, dx, :], rows[:, :, dx:dx + IMG], start=(dx == 0), stop=(dx == 2))
                    mm.then_inc(conv0_done, 1)

            def pointwise(u, s, hf, parity, gx):
                r, rp = u * GRID + gx, (hf + gx) % 2
                if hf == 0 and gx == 0:
                    pe.wait_ge(pw_scaled, s + 1)
                pe.wait_ge(y1_ready, r + 1)
                if reached(r, 2):
                    pe.wait_ge(y2_ready, r - 1)
                for q in range(2):
                    mm = pe.matmul(pw_ps[0:CH, rp, 2 * q:2 * q + 2, 0:RPX],
                                   par[:, parity, P_PW + gx * CH:P_PW + (gx + 1) * CH],
                                   y1[:, rp, 2 * q * RPX:(2 * q + 2) * RPX].rearrange("p (g n) -> p g n", n=RPX),
                                   start=True, stop=True)
                mm.then_inc(pw_done, 1)

            def conv1(u):
                pe.wait_ge(cols_loaded, (u + 1) * 32)
                if reached(u, 1):
                    pe.wait_ge(z1_ready, u)
                for m in range(4):
                    for k in range(2):
                        mm = pe.matmul(c1_ps[64 * (m // 2):64 * (m // 2) + 64, m % 2, 0:2 * RUN], w1[:, k, :],
                                       cols[:, k, 2 * m:2 * m + 2, :], start=(k == 0), stop=(k == 1))
                mm.then_inc(conv1_done, 1)

            pe.wait_ge(const_loaded, 16 * 8)
            conv0(0, 0, 48, range(PIECES))

            def body(s, sc, parity, hf):
                u = s * 2 + hf
                for q, regions in enumerate(PAIRED):
                    if has_next(s, hf):
                        conv0(u + 1, 1 - hf, (s + (1 + hf)) * 48, (2 * q, 2 * q + 1))
                    for gx in regions:
                        pointwise(u, s, hf, parity, gx)
                if reached(u, 1):
                    conv1(u - 1)

            over_units(pe, body)
            conv1(units - 1)

            z = z1[:].rearrange("p b g (y x) -> p (b g) y x", x=OX)
            pe.wait_ge(z1_ready, units)
            for i in range(8):
                """2x2 with stride 2, both b8 halves by a block-diagonal weight."""
                if i >= 4:
                    pe.wait_ge(z2_ready, i - 3)
                for t in range(4):
                    mm = pe.matmul(pw_ps[:, i % 4 // 2, (i % 2) * 2:(i % 2) * 2 + 2, :].rearrange(
                                       "p a n -> p (a n)")[:, 0:400],
                                   w2[:, t, :], z[:, 4 * i:4 * i + 4, t // 2:t // 2 + 19:2, t % 2:t % 2 + 19:2],
                                   start=(t == 0), stop=(t == 3))
                mm.then_inc(conv2_done, 1)
            for n in range(16):
                """2x2 with stride 2, tokens on partitions: four batches of 25 tokens."""
                h, i = divmod(n, 8)
                if h == 0:
                    pe.wait_ge(z2_ready, i + 1)
                if n >= 2:
                    pe.wait_ge(tok_scaled, n - 1)
                for t in range(4):
                    mm = pe.matmul(c0_ps[0:4 * IMG_LEN, n % 2, 0:D],
                                   z2[64 * h:64 * h + 64, t, 4 * i * IMG_LEN:(4 * i + 4) * IMG_LEN],
                                   w3[64 * h:64 * h + 64, t, :], start=(t == 0), stop=(t == 3))
                mm.then_inc(conv3_done, 1)

        @block.scalar
        def _(act):
            def take_conv0(u, half, pieces):
                for piece in pieces:
                    g, part = divmod(piece, 2)
                    act.wait_ge(conv0_done, u * PIECES + (piece + 1))
                    if piece == 0 and reached(u, 2):
                        act.wait_ge(y2_ready, (u - 1) * GRID)
                    at = LEAD + g * GP + part * PROWS * PITCH
                    dst = y0[:, half, :, at:at + PROWS * PITCH].rearrange("p r (y c) -> p y r c", c=PITCH)[:, :, :, 0:REG]
                    src = c0_ps[0:CH, piece % 2, 0:PROWS * IMG].rearrange("p (y r c) -> p y r c", r=GRID, c=REG)
                    act.activation(dst, src, ACT.Gelu, scale=sb0[:, 0:1], bias=sb0[:, 1:2]).then_inc(y0_ready, 1)

            def take_depthwise(u, hf, parity, gx):
                r, rp = u * GRID + gx, (hf + gx) % 2
                act.wait_ge(dw_done, r + 1)
                if reached(r, 2):
                    act.wait_ge(pw_done, r - 1)
                act.activation(y1[:, rp, :].rearrange("p (g y c) -> p g y c", y=REG, c=REG), pixels(acc[:, rp, :]), ACT.Gelu,
                               scale=par[:, parity, P_SDW + gx:P_SDW + gx + 1],
                               bias=par[:, parity, P_BDW + gx:P_BDW + gx + 1]).then_inc(y1_ready, 1)

            def take_region(u, hf, parity, gx):
                r, rp = u * GRID + gx, (hf + gx) % 2
                n = min(OY, OX - gx * OY)
                act.wait_ge(y2_ready, r + 1)
                if gx == 0 and reached(u, 1):
                    act.wait_ge(taps_stored, u * 16)
                src = y2[:, rp, :].rearrange("p (a d b e) -> p d a b e", d=4, b=OY, e=4)
                dst = taps[0:CH, :].rearrange("p (d e a x) -> p d a x e", d=4, e=4, x=OX)
                for dy in range(4):
                    last = act.activation(dst[:, dy, :, gx * OY:gx * OY + n, :], src[:, dy, :, 0:n, :], ACT.Gelu,
                                          bias=par[:, parity, P_BPW + gx:P_BPW + gx + 1])
                last.then_inc(taps_ready, 1)

            def take_conv1(u, s, hf):
                act.wait_ge(conv1_done, u + 1)
                act.sem_inc(wait_carrier, 1)
                for m in range(2):
                    last = act.activation(z1[:, 2 * m:2 * m + 2, hf * G4:(hf + 1) * G4, bass.ds(s * (OY * OX), OY * OX)],
                                          c1_ps[:, m, 0:2 * RUN].rearrange("p (b g n) -> p b g n", b=2, g=G4), ACT.Gelu,
                                          scale=sb1[:, 0:1], bias=sb1[:, 1:2])
                last.then_inc(z1_ready, 1)

            act.wait_ge(const_loaded, 16 * 8)
            act.wait_ge(pads_set, 1)
            take_conv0(0, 0, range(PIECES))

            def body(s, sc, parity, hf):
                u = s * 2 + hf
                if hf == 0:
                    act.wait_ge(par_loaded[parity], (sc + 1) * 16)
                for q, regions in enumerate(PAIRED):
                    for gx in regions:
                        take_depthwise(u, hf, parity, gx)
                    if q == 0:
                        if reached(u, 1):
                            take_region(u - 1, 1 - hf, parity if hf else 1 - parity, GRID - 1)
                    else:
                        for gx in PAIRED[q - 1]:
                            take_region(u, hf, parity, gx)
                    if has_next(s, hf):
                        take_conv0(u + 1, 1 - hf, (2 * q, 2 * q + 1))
                if reached(u, 1):
                    take_conv1(u - 1, s if hf else s - 1, 1 - hf)

            over_units(act, body)
            take_region(units - 1, 1, (GRID - 1) % 2, GRID - 1)
            take_conv1(units - 1, GRID - 1, 1)
            act.wait_ge(taps_stored, units * 16)
            for i in range(8):
                act.wait_ge(conv2_done, i + 1)
                src = pw_ps[:, i % 4 // 2, (i % 2) * 2:(i % 2) * 2 + 2, :].rearrange("p a n -> p (a n)")[:, 0:400]
                src = src.rearrange("p (a d x e) -> p d a x e", d=2, x=5, e=2)
                dst = z2[:, :, 4 * i * IMG_LEN:(4 * i + 4) * IMG_LEN].rearrange("p (d e) (a x) -> p d a x e", d=2, x=5)
                for dy in range(2):
                    last = act.activation(dst[:, dy], src[:, dy], ACT.Gelu, scale=sb2[:, 0:1], bias=sb2[:, 1:2])
                last.then_inc(z2_ready, 1)

        @block.vector
        def _(dve):
            dve.memset(y0[:], 0.0).then_inc(pads_set, 1)

            def depthwise(u, hf, parity, regions):
                n = len(regions)
                first = u * (8 * GRID) + 8 * regions[0]
                for k, (ky, kx) in enumerate([(1, 1)] + [(i // 3, i % 3) for i in range(9) if i != 4]):
                    for a, gx in enumerate(regions):
                        r, rp = u * GRID + gx, (hf + gx) % 2
                        out = acc[:, rp, 0:WROWS * PITCH].rearrange("p (r c) -> p r c", c=PITCH)[:, :, 0:REG]
                        at = P_DW + gx * 9 + ky * 3 + kx
                        w = par[:, parity, at:at + 1]
                        if k == 0:
                            if reached(r, 2):
                                dve.wait_ge(y1_ready, r - 1)
                            s = dve.tensor_scalar(out, window(hf, gx, ky, kx), w, None, ALU.mult)
                        else:
                            dve.wait_ge(dw_tap, first + (n * (k - 1) + a + 1))
                            s = dve.scalar_tensor_tensor(out, window(hf, gx, ky, kx), w, out, ALU.mult, ALU.add)
                        s.then_inc(dw_tap if k < 8 else dw_done, 1)

            def add_input(u, hf, gx):
                r, rp = u * GRID + gx, (hf + gx) % 2
                dve.wait_ge(pw_done, r + 1)
                if reached(r, 2):
                    dve.wait_ge(taps_ready, r - 1)
                dve.tensor_tensor(y2[:, rp, :].rearrange("p (g y c) -> p g y c", y=REG, c=REG),
                                  pw_ps[0:CH, rp, :, 0:RPX].rearrange("p g (y c) -> p g y c", c=REG),
                                  pixels(y0[:, hf, gx, LEAD:LEAD + G4 * GP]), ALU.add).then_inc(y2_ready, 1)

            def body(s, sc, parity, hf):
                u = s * 2 + hf
                if hf == 0:
                    dve.wait_ge(par_loaded[parity], (sc + 1) * 16)
                dve.wait_ge(y0_ready, (u + 1) * PIECES)
                for q, regions in enumerate(PAIRED):
                    depthwise(u, hf, parity, regions)
                    if q:
                        for gx in PAIRED[q - 1]:
                            add_input(u, hf, gx)
                    elif reached(u, 1):
                        add_input(u - 1, 1 - hf, GRID - 1)

            over_units(dve, body)
            add_input(units - 1, 1, GRID - 1)

            for n in range(16):
                dve.wait_ge(conv3_done, n + 1)
                if n >= 4:
                    dve.wait_ge(h_stored[n % 4], 64 * (n // 4))
                rows = slice(0, 4 * IMG_LEN)
                dve.tensor_tensor(tok[:, n % 4, :], c0_ps[rows, n % 2, 0:D], sb3[rows, 0, :], ALU.mult).then_inc(tok_scaled, 1)
                dve.wait_ge(tok_scaled, n + 1)
                dve.tensor_tensor(tok[:, n % 4, :], tok[:, n % 4, :], sb3[rows, 1, :], ALU.add).then_inc(tok_ready, 1)


EXPERTS = 8
F = 768
ROW = D + 2
SLOT = 128
SLOTS = (2 * TOKENS + EXPERTS * (SLOT - 1)) // SLOT
REGION = TOKENS + SLOT
SPARE = EXPERTS * REGION


def routing_stage(nc, io, slots):
    BT = 8
    NB = TILES // BT
    BE = BT * EXPERTS

    with ExitStack() as ctx:
        def sb(name, shape, dt=F32):
            return ctx.enter_context(nc.sbuf_tensor("rt_sb_" + name, shape, dt))

        def ps(name, shape):
            return ctx.enter_context(nc.psum_tensor("rt_ps_" + name, shape, F32))

        def sem(name):
            return ctx.enter_context(nc.semaphore("rt_" + name))

        h1 = sb("h1", [PAIR, TILES, D])
        ident = sb("ident", [128, 128])
        router_w = sb("router_w", [HALF, 2, EXPERTS])
        earlier = sb("earlier", [PAIR, 2, PAIR])
        token_no = sb("token_no", [PAIR, TILES], I32)
        pad_no = sb("pad_no", [128, 1], I32)
        region_at = sb("region_at", [PAIR, BT, EXPERTS])
        slot_no = sb("slot_no", [1, SLOTS])
        minus_half = sb("minus_half", [PAIR, BT])
        number = sb("number", [PAIR, EXPERTS])
        zeros = sb("zeros", [128, D])
        pad_rows = sb("pad_rows", [128, ROW])
        stats = sb("stats", [PAIR, TILES, 6])
        mv = sb("mv", [PAIR, TILES, 2])
        var_eps = sb("var_eps", [PAIR, TILES])
        rstd = sb("rstd", [PAIR, TILES])
        rows = sb("rows", [PAIR, 2, TILES, ROW])
        xnT = sb("xnT", [HALF, 2, 2, PAIR])
        logits = sb("logits", [PAIR, TILES, EXPERTS])
        top = sb("top", [PAIR, TILES, 8])
        top_at = sb("top_at", [PAIR, TILES, 8], U32)
        top_atf = sb("top_atf", [PAIR, TILES, 8])
        gap = sb("gap", [PAIR, TILES])
        ratio = sb("ratio", [PAIR, TILES])
        one_plus = sb("one_plus", [PAIR, TILES])
        picked = sb("picked", [PAIR, 2, BT, EXPERTS])
        either = sb("either", [PAIR, TILES, EXPERTS])
        before = sb("before", [PAIR, TILES + 1, EXPERTS])
        place = sb("place", [PAIR, BT, EXPERTS])
        own_place = sb("own_place", [PAIR, 2, BT, EXPERTS])
        dest_f = sb("dest_f", [PAIR, 2, BT])
        dest = sb("dest", [PAIR, 2, TILES], U32)
        counts = sb("counts", [1, EXPERTS])
        pad_at_f = sb("pad_at_f", [1, EXPERTS])
        pad_at = sb("pad_at", [1, EXPERTS], I32)
        counts_i = sb("counts_i", [1, EXPERTS], I32)
        blocks_i = sb("blocks_i", [1, EXPERTS], I32)
        ends = sb("ends", [1, EXPERTS])
        passed = sb("passed", [1, SLOTS, EXPERTS])
        passed_end = sb("passed_end", [1, SLOTS, EXPERTS])
        slot_expert = sb("slot_expert", [1, SLOTS])
        slot_begin = sb("slot_begin", [1, SLOTS])
        in_expert = sb("in_expert", [1, SLOTS])
        region_row = sb("region_row", [1, SLOTS])
        slot_row = sb("slot_row", [1, SLOTS])
        table = sb("table", [1, 3, SLOTS])
        turned_ps = ps("turned_ps", [HALF, 2, 512])
        logits_ps = ps("logits_ps", [PAIR, 2, 512])
        place_ps = ps("place_ps", [PAIR, 2, 512])
        count_ps = ps("count_ps", [PAIR, 512])

        const_loaded = sem("const_loaded")
        consts_set = sem("consts_set")
        h1_loaded = [sem("h1_loaded_%d" % b) for b in range(NB)]
        zeros_stored = sem("zeros_stored")
        pads_stored = sem("pads_stored")
        pads_set = sem("pads_set")
        numbers_set = sem("numbers_set")
        stats_done = sem("stats_done")
        var_ready = sem("var_ready")
        eps_added = sem("eps_added")
        rstd_ready = sem("rstd_ready")
        normed = sem("normed")
        doubled = sem("doubled")
        turned = sem("turned")
        xnT_ready = sem("xnT_ready")
        logits_done = sem("logits_done")
        logits_ready = sem("logits_ready")
        gap_ready = sem("gap_ready")
        ratio_ready = sem("ratio_ready")
        step_done = sem("step_done")
        either_ready = sem("either_ready")
        before_ready = sem("before_ready")
        placed = sem("placed")
        place_read = sem("place_read")
        shares_set = sem("shares_set")
        dest_ready = sem("dest_ready")
        counted = sem("counted")
        pad_at_ready = sem("pad_at_ready")
        scattered = sem("scattered")

        block = ctx.enter_context(nc.Block())

        @block.sync
        def _(sp):
            h1_rows = io["out"][0:TOKENS].rearrange("(t p) d -> p t d", p=PAIR)
            for b in range(NB):
                sp.dma_start(h1[:, b * BT:(b + 1) * BT, :], h1_rows[:, b * BT:(b + 1) * BT, :]
                             ).then_inc(h1_loaded[b], 16)
            for dst, name in ((ident, "ident"), (router_w, "router_w"), (earlier, "earlier"), (token_no, "token_no"),
                              (pad_no, "pad_no"), (region_at, "region_at"), (slot_no, "slot_no")):
                sp.dma_start(dst[:], io[name]).then_inc(const_loaded, 16)
            sp.wait_ge(consts_set, 4)
            sp.dma_start(io["out"][TOKENS:TOKENS + SLOT], zeros[:]).then_inc(zeros_stored, 16)
            sp.wait_ge(pads_set, 1)
            sp.dma_start(io["dispatch"][SPARE:SPARE + SLOT], pad_rows[:]).then_inc(pads_stored, 16)
            sp.wait_ge(pad_at_ready, 1)
            for e in range(EXPERTS):
                at = sp.value_load(pad_at[0:1, e:e + 1], min_val=e * REGION, max_val=e * REGION + TOKENS)
                sp.dma_start(io["dispatch"][bass.ds(at, SLOT), :], pad_rows[:]).then_inc(pads_stored, 16)
            sp.wait_ge(zeros_stored, 16)
            sp.wait_ge(pads_stored, 16 * (EXPERTS + 1))

        @block.gpsimd
        def _(pool):
            pool.memset(minus_half[:], -0.5).then_inc(consts_set, 1)
            pool.iota(number[:], pattern=[[1, EXPERTS]], base=0, channel_multiplier=0,
                      allow_small_or_imprecise_dtypes=True).then_inc(consts_set, 1)
            pool.memset(zeros[:], 0.0).then_inc(consts_set, 1)
            pool.memset(pad_rows[:], 0.0).then_inc(consts_set, 1)
            pool.wait_ge(consts_set, 4)

            def rstd_of(b):
                at = slice(b * BT, (b + 1) * BT)
                pool.wait_ge(var_ready, b + 1)
                pool.tensor_scalar(var_eps[:, at], mv[:, at, 1], EPS, None, ALU.add).then_inc(eps_added, 1)
                pool.wait_ge(eps_added, b + 1)
                pool.tensor_tensor(rstd[:, at], var_eps[:, at], minus_half[:], ALU.pow).then_inc(rstd_ready, 1)

            def dispatch(b):
                pool.wait_ge(numbers_set, 1)
                pool.wait_ge(shares_set, b + 1)
                pool.wait_ge(dest_ready, b + 1)
                pool.wait_ge(doubled, (b + 1) * BT)
                for t in range(b * BT, (b + 1) * BT):
                    for k in range(2):
                        pool.indirect_dma_start(io["dispatch"], bass.IndirectOffsetOnAxis(dest[:, k, t:t + 1], 0),
                                                rows[:, k, t, :], None).then_inc(scattered, 16)

            rstd_of(0)
            rstd_of(1)
            for b in range(NB):
                if b + 2 < NB:
                    rstd_of(b + 2)
                dispatch(b)
            pool.wait_ge(scattered, 16 * 2 * TILES)

        @block.tensor
        def _(pe):
            pe.wait_ge(const_loaded, 16 * 7)

            def turn(t):
                pe.wait_ge(normed, t + 1)
                if t >= 2:
                    pe.wait_ge(xnT_ready, t - 1)
                for h in range(2):
                    last = pe.transpose(turned_ps[:, t % 2, h * PAIR:(h + 1) * PAIR],
                                        rows[:, 0, t, h * HALF:(h + 1) * HALF], ident[0:PAIR, 0:PAIR])
                last.then_inc(turned, 1)

            def logits_of(t):
                b, i = divmod(t, BT)
                pe.wait_ge(xnT_ready, t + 1)
                if i == 0 and b >= 2:
                    pe.wait_ge(logits_ready, b - 1)
                for h in range(2):
                    mm = pe.matmul(logits_ps[:, b % 2, i * EXPERTS:(i + 1) * EXPERTS], xnT[:, t % 2, h, :],
                                   router_w[:, h, :], start=(h == 0), stop=(h == 1))
                mm.then_inc(logits_done, 1)

            def count(b):
                at = slice(b * BT, (b + 1) * BT)
                pe.wait_ge(either_ready, b + 1)
                pe.wait_ge(before_ready, (b + 1) * BT)
                if b >= 2:
                    pe.wait_ge(place_read, b - 1)
                pe.matmul(place_ps[:, b % 2, 0:BE], earlier[:, 0, :], either[:, at, :].rearrange("p t e -> p (t e)"),
                          start=True, stop=False)
                pe.matmul(place_ps[:, b % 2, 0:BE], earlier[:, 1, :], before[:, at, :].rearrange("p t e -> p (t e)"),
                          start=False, stop=True).then_inc(placed, 1)

            for b in range(NB):
                for t in range(b * BT, (b + 1) * BT):
                    turn(t)
                    if t >= 1:
                        logits_of(t - 1)
                if b >= 1:
                    count(b - 1)
            logits_of(TILES - 1)
            count(NB - 1)
            pe.wait_ge(before_ready, TILES + 1)
            pe.matmul(count_ps[:, 0:EXPERTS], earlier[:, 1, :], before[:, TILES, :], start=True, stop=True
                      ).then_inc(counted, 1)

        @block.scalar
        def _(act):
            def ratio_of(b):
                at = slice(b * BT, (b + 1) * BT)
                act.wait_ge(gap_ready, b + 1)
                act.activation(ratio[:, at], gap[:, at], ACT.Exp).then_inc(ratio_ready, 1)

            for b in range(NB):
                for t in range(b * BT, (b + 1) * BT):
                    act.wait_ge(turned, t + 1)
                    if t >= 2:
                        act.wait_ge(logits_done, t - 1)
                    act.activation(xnT[:, t % 2], turned_ps[:, t % 2, 0:2 * PAIR].rearrange("p (h n) -> p h n", h=2),
                                   ACT.Copy).then_inc(xnT_ready, 1)
                    act.activation(rows[:, 1, t, 0:D], rows[:, 0, t, 0:D], ACT.Copy).then_inc(doubled, 1)
                if b >= 1:
                    ratio_of(b - 1)
            ratio_of(NB - 1)

        @block.vector
        def _(dve):
            steps = 0

            def chained(instruction):
                nonlocal steps
                steps += 1
                instruction.then_inc(step_done, 1)
                dve.wait_ge(step_done, steps)

            def statistics(b):
                tiles = range(b * BT, (b + 1) * BT)
                dve.wait_ge(h1_loaded[b], 16)
                for t in tiles:
                    s = dve.bn_stats(stats[:, t, :], h1[:, t, :])
                s.then_inc(stats_done, 1)
                dve.wait_ge(stats_done, b + 1)
                for t in tiles:
                    s = dve.bn_aggr(mv[:, t, :], stats[:, t, :])
                s.then_inc(var_ready, 1)

            def normalise(b):
                dve.wait_ge(rstd_ready, b + 1)
                for t in range(b * BT, (b + 1) * BT):
                    dve.tensor_scalar(rows[:, 0, t, 0:D], h1[:, t, :], mv[:, t, 0:1], rstd[:, t:t + 1],
                                      ALU.subtract, ALU.mult).then_inc(normed, 1)

            def route(b):
                tiles = range(b * BT, (b + 1) * BT)
                at = slice(b * BT, (b + 1) * BT)
                dve.wait_ge(logits_done, (b + 1) * BT)
                dve.tensor_copy(logits[:, at, :], logits_ps[:, b % 2, 0:BE].rearrange("p (t e) -> p t e", e=EXPERTS)
                                ).then_inc(logits_ready, 1)
                dve.wait_ge(logits_ready, b + 1)
                for t in tiles:
                    s = dve.max(top[:, t, :], logits[:, t, :])
                chained(s)
                dve.tensor_tensor(gap[:, at], top[:, at, 1], top[:, at, 0], ALU.subtract).then_inc(gap_ready, 1)
                for t in tiles:
                    s = dve.max_index(top_at[:, t, :], top[:, t, :], logits[:, t, :])
                chained(s)
                chained(dve.tensor_copy(top_atf[:, at], top_at[:, at]))
                for k in range(2):
                    s = dve.tensor_tensor(picked[:, k], number[:].unsqueeze(1).to_broadcast([PAIR, BT, EXPERTS]),
                                          top_atf[:, at, k:k + 1].to_broadcast([PAIR, BT, EXPERTS]), ALU.is_equal)
                chained(s)
                dve.tensor_tensor(either[:, at], picked[:, 0], picked[:, 1], ALU.add).then_inc(either_ready, 1)
                dve.wait_ge(either_ready, b + 1)
                for t in tiles:
                    dve.tensor_tensor(before[:, t + 1, :], before[:, t, :], either[:, t, :], ALU.add
                                      ).then_inc(before_ready, 1)
                    dve.wait_ge(before_ready, t + 2)
                dve.wait_ge(ratio_ready, b + 1)
                chained(dve.tensor_scalar(one_plus[:, at], ratio[:, at], 1.0, None, ALU.add))
                chained(dve.reciprocal(rows[:, 0, at, D + 1], one_plus[:, at]))
                dve.tensor_tensor(rows[:, 1, at, D + 1], rows[:, 0, at, D + 1], ratio[:, at], ALU.mult
                                  ).then_inc(shares_set, 1)
                dve.wait_ge(placed, b + 1)
                dve.tensor_tensor(place[:], place_ps[:, b % 2, 0:BE].rearrange("p (t e) -> p t e", e=EXPERTS),
                                  region_at[:], ALU.add).then_inc(place_read, 1)
                dve.wait_ge(place_read, b + 1)
                for k in range(2):
                    s = dve.tensor_tensor(own_place[:, k], picked[:, k], place[:], ALU.mult)
                chained(s)
                for k in range(2):
                    s = dve.tensor_reduce(dest_f[:, k], own_place[:, k], AX_X, ALU.add)
                chained(s)
                dve.tensor_copy(dest[:, :, at], dest_f[:]).then_inc(dest_ready, 1)

            statistics(0)
            statistics(1)
            dve.memset(before[:, 0, :], 0.0).then_inc(before_ready, 1)
            dve.wait_ge(before_ready, 1)
            dve.wait_ge(consts_set, 4)
            dve.wait_ge(const_loaded, 16 * 7)
            dve.tensor_copy(pad_rows[:, D:D + 1].bitcast(I32), pad_no[:]).then_inc(pads_set, 1)
            for k in range(2):
                s = dve.tensor_copy(rows[:, k, :, D].bitcast(I32), token_no[:])
            s.then_inc(numbers_set, 1)
            for b in range(NB):
                normalise(b)
                if b + 2 < NB:
                    statistics(b + 2)
                if b >= 1:
                    route(b - 1)
            route(NB - 1)

            dve.wait_ge(counted, 1)
            chained(dve.tensor_copy(counts[:], count_ps[0:1, 0:EXPERTS]))
            chained(dve.tensor_tensor(pad_at_f[:], counts[:], region_at[0:1, 0, :], ALU.add))
            dve.tensor_copy(pad_at[:], pad_at_f[:]).then_inc(pad_at_ready, 1)
            chained(dve.tensor_scalar(counts[:], counts[:], float(SLOT - 1), None, ALU.add))
            chained(dve.tensor_copy(counts_i[:], counts[:]))
            chained(dve.tensor_scalar(blocks_i[:], counts_i[:], SLOT.bit_length() - 1, None, ALU.logical_shift_right))
            chained(dve.tensor_copy(ends[:], blocks_i[:]))
            for e in range(1, EXPERTS):
                chained(dve.tensor_tensor(ends[:, e:e + 1], ends[:, e:e + 1], ends[:, e - 1:e], ALU.add))
            every = [1, SLOTS, EXPERTS]
            chained(dve.tensor_tensor(passed[:], ends[:].unsqueeze(1).to_broadcast(every),
                                      slot_no[:].unsqueeze(2).to_broadcast(every), ALU.is_le))
            dve.tensor_reduce(slot_expert[:], passed[:], AX_X, ALU.add)
            chained(dve.tensor_tensor(passed_end[:], passed[:], ends[:].unsqueeze(1).to_broadcast(every), ALU.mult))
            dve.tensor_reduce(slot_begin[:], passed_end[:], AX_X, ALU.max)
            chained(dve.tensor_scalar(table[:, 1, :], slot_expert[:], float(EXPERTS - 1), None, ALU.min))
            chained(dve.tensor_tensor(in_expert[:], slot_no[:], slot_begin[:], ALU.subtract))
            dve.tensor_scalar(region_row[:], slot_expert[:], float(REGION), None, ALU.mult)
            chained(dve.tensor_scalar(in_expert[:], in_expert[:], float(SLOT), None, ALU.mult))
            chained(dve.tensor_tensor(slot_row[:], in_expert[:], region_row[:], ALU.add))
            chained(dve.tensor_scalar(table[:, 0, :], slot_row[:], float(SPARE), None, ALU.min))
            dve.memset(table[:, 2, 0:2], 1.0)
            chained(dve.tensor_tensor(table[:, 2, 2:SLOTS], table[:, 1, 2:SLOTS], table[:, 1, 0:SLOTS - 2],
                                      ALU.not_equal))
            chained(dve.tensor_copy(slots[:], table[:]))




def expert_stage(nc, io, slots):
    FB = F // 128
    AHEAD = 8
    LEAD = AHEAD // 2
    ROUNDS = SLOTS // AHEAD
    HB = FB // 2

    with ExitStack() as ctx:
        def sb(name, shape, dt=F32):
            return ctx.enter_context(nc.sbuf_tensor("moe_sb_" + name, shape, dt))

        def ps(name, shape):
            return ctx.enter_context(nc.psum_tensor("moe_ps_" + name, shape, F32))

        def sem(name):
            return ctx.enter_context(nc.semaphore("moe_" + name))

        ident = sb("ident", [128, 128])
        up_w = sb("up_w", [HALF, 2, 2, F])
        up_b = sb("up_b", [128, 2, FB])
        down = sb("down", [128, 2, (FB + 1) * D])
        x = sb("x", [SLOT, AHEAD, ROW])
        xT = sb("xT", [HALF, 2, 2, SLOT])
        hidden = sb("hidden", [128, 2, FB, SLOT])
        biased = sb("biased", [SLOT, 2, D])
        result = sb("result", [SLOT, 2, D])
        turned_ps = ps("turned_ps", [HALF, 2, 512])
        up_ps = ps("up_ps", [128, 4, 512])
        down_ps = ps("down_ps", [SLOT, 2, 512])

        ident_loaded = sem("ident_loaded")
        wait_carrier = sem("wait_carrier")
        rows_loaded = [sem("rows_loaded_%d" % i) for i in range(AHEAD)]
        up_loaded = [sem("up_loaded_even"), sem("up_loaded_odd")]
        down_loaded = [sem("down_loaded_even"), sem("down_loaded_odd")]
        turned = sem("turned")
        xT_ready = sem("xT_ready")
        up_done = sem("up_done")
        hidden_ready = sem("hidden_ready")
        down_done = sem("down_done")
        bias_added = sem("bias_added")
        result_ready = sem("result_ready")
        added = sem("added")

        def over_slots(eng, body):
            for i in range(AHEAD):
                body(i, i, 0)
            with eng.Fori(1, ROUNDS) as k:
                for i in range(AHEAD):
                    body(k * AHEAD + i, i, k)

        def use_of_pair(i, k):
            return k * (AHEAD // 2) + (i // 2 + 1)

        block = ctx.enter_context(nc.Block())

        @block.sync
        def _(sp):
            sp.dma_start(ident[:], io["ident"]).then_inc(ident_loaded, 16)

            def load_rows(s, i):
                row = sp.value_load(slots[0:1, 0, bass.ds(s, 1)], min_val=0, max_val=SPARE)
                if reached(s, AHEAD):
                    sp.wait_ge(added, (s - (AHEAD - 1)) * 16)
                    sp.sem_inc(wait_carrier, 1)
                sp.dma_start(x[:, i, :], io["dispatch"][bass.ds(row, SLOT), :]).then_inc(rows_loaded[i], 16)

            def weights_of(s):
                expert = sp.value_load(slots[0:1, 1, bass.ds(s, 1)], min_val=0, max_val=EXPERTS - 1)
                changed = sp.value_load(slots[0:1, 2, bass.ds(s, 1)], min_val=0, max_val=1)
                return bass.ds(expert, 1), changed

            def load_up(s, par):
                expert, changed = weights_of(s)
                if reached(s, 2):
                    sp.wait_ge(up_done, (s - 1) * 2)
                    sp.sem_inc(wait_carrier, 1)
                    sp.wait_ge(hidden_ready, (s - 1) * FB)
                    sp.sem_inc(wait_carrier, 1)
                sp.dma_start(up_w[:, par].rearrange("p h f -> p (h f)"),
                             io["up_w"][expert].rearrange("e p f -> p (e f)"), cond=changed
                             ).then_inc(up_loaded[par], 16)
                sp.dma_start(up_b[:, par], io["up_b"][expert].rearrange("e p f -> p (e f)"), cond=changed
                             ).then_inc(up_loaded[par], 16)

            def load_down(s, par):
                expert, changed = weights_of(s)
                if reached(s, 2):
                    sp.wait_ge(bias_added, s - 1)
                    sp.sem_inc(wait_carrier, 1)
                sp.dma_start(down[:, par], io["down_w"][expert].rearrange("e p f -> p (e f)"), cond=changed
                             ).then_inc(down_loaded[par], 16)

            def load(s, i):
                if not (isinstance(s, int) and s + 1 >= SLOTS):
                    load_up(s + 1, (i + 1) % 2)
                load_down(s, i % 2)
                if not (isinstance(s, int) and s + LEAD >= SLOTS):
                    load_rows(s + LEAD, (i + LEAD) % AHEAD)

            load_rows(0, 0)
            load_up(0, 0)
            for s in range(1, LEAD):
                load_rows(s, s)
            for i in range(AHEAD):
                load(i, i)
            with sp.Fori(1, ROUNDS - 1) as k:
                for i in range(AHEAD):
                    load(k * AHEAD + i, i)
            for i in range(AHEAD):
                load(SLOTS - AHEAD + i, i)

        @block.gpsimd
        def _(pool):
            def add(s, i, k):
                pool.wait_ge(result_ready, s + 1)
                pool.sem_inc(wait_carrier, 1)
                if reached(s, 1):
                    pool.wait_ge(added, s * 16)
                    pool.sem_inc(wait_carrier, 1)
                pool.indirect_dma_start(io["out"], bass.IndirectOffsetOnAxis(x[:, i, D:D + 1].bitcast(U32), 0),
                                        result[:, i % 2, :], None, compute_op=ALU.add).then_inc(added, 16)

            over_slots(pool, add)
            pool.wait_ge(added, SLOTS * 16)

        @block.tensor
        def _(pe):
            def turn(s, i, k):
                pe.wait_ge(rows_loaded[i], (k + 1) * 16)
                if reached(s, 2):
                    pe.wait_ge(xT_ready, s - 1)
                for h in range(2):
                    last = pe.transpose(turned_ps[:, i % 2, h * SLOT:(h + 1) * SLOT],
                                        x[:, i, h * HALF:(h + 1) * HALF], ident[:])
                last.then_inc(turned, 1)

            def up(s, i, k):
                pe.wait_ge(up_loaded[i % 2], use_of_pair(i, k) * 32)
                pe.wait_ge(xT_ready, s + 1)
                for b in range(2):
                    if reached(s, 2):
                        pe.wait_ge(hidden_ready, (s - 2) * FB + (b + 1) * HB)
                    for m in range(b * HB, (b + 1) * HB):
                        for h in range(2):
                            mm = pe.matmul(up_ps[:, (i % 2) * 2 + b, (m - b * HB) * SLOT:(m - b * HB + 1) * SLOT],
                                           up_w[:, i % 2, h, m * 128:(m + 1) * 128], xT[:, i % 2, h, :],
                                           start=(h == 0), stop=(h == 1))
                    mm.then_inc(up_done, 1)

            def down_of(s, i, k):
                pe.wait_ge(down_loaded[i % 2], use_of_pair(i, k) * 16)
                pe.wait_ge(hidden_ready, (s + 1) * FB)
                if reached(s, 2):
                    pe.wait_ge(bias_added, s - 1)
                for m in range(FB):
                    mm = pe.matmul(down_ps[:, i % 2, 0:D], hidden[:, i % 2, m, :],
                                   down[:, i % 2, m * D:(m + 1) * D], start=(m == 0), stop=(m == FB - 1))
                mm.then_inc(down_done, 1)

            def step(s, i, k):
                up(s, i, k)
                if i + 1 < AHEAD:
                    turn(s + 1, i + 1, k)
                elif not (isinstance(s, int) and s + 1 == SLOTS):
                    turn(s + 1, 0, k + 1)
                if i > 0:
                    down_of(s - 1, i - 1, k)
                elif reached(s, 1):
                    down_of(s - 1, AHEAD - 1, k - 1)

            pe.wait_ge(ident_loaded, 16)
            turn(0, 0, 0)
            for i in range(AHEAD):
                step(i, i, 0)
            with pe.Fori(1, ROUNDS - 1) as k:
                for i in range(AHEAD):
                    step(k * AHEAD + i, i, k)
            for i in range(AHEAD):
                step(SLOTS - AHEAD + i, i, ROUNDS - 1)
            down_of(SLOTS - 1, AHEAD - 1, ROUNDS - 1)

        @block.scalar
        def _(act):
            def gelu(s, i, k):
                act.wait_ge(up_loaded[i % 2], use_of_pair(i, k) * 32)
                if reached(s, 2):
                    act.wait_ge(down_done, s - 1)
                for m in range(FB):
                    if m % HB == 0:
                        act.wait_ge(up_done, s * 2 + (m // HB + 1))
                    act.activation(hidden[:, i % 2, m, :],
                                   up_ps[:, (i % 2) * 2 + m // HB, (m % HB) * SLOT:(m % HB + 1) * SLOT], ACT.Gelu,
                                   bias=up_b[:, i % 2, m:m + 1]).then_inc(hidden_ready, 1)

            over_slots(act, gelu)

        @block.vector
        def _(dve):
            def take_turned(s, i, k):
                dve.wait_ge(turned, s + 1)
                if reached(s, 2):
                    dve.wait_ge(up_done, (s - 1) * 2)
                dve.tensor_copy(xT[:, i % 2], turned_ps[:, i % 2, 0:2 * SLOT].rearrange("p (h n) -> p h n", h=2)
                                ).then_inc(xT_ready, 1)

            def weigh(s, i, k):
                dve.wait_ge(down_loaded[i % 2], use_of_pair(i, k) * 16)
                dve.wait_ge(down_done, s + 1)
                if reached(s, 2):
                    dve.wait_ge(result_ready, s - 1)
                dve.tensor_tensor(biased[:, i % 2], down_ps[:, i % 2, 0:D], down[:, i % 2, FB * D:(FB + 1) * D],
                                  ALU.add).then_inc(bias_added, 1)
                dve.wait_ge(bias_added, s + 1)
                dve.wait_ge(rows_loaded[i], (k + 1) * 16)
                if reached(s, 2):
                    dve.wait_ge(added, (s - 1) * 16)
                dve.tensor_scalar(result[:, i % 2], biased[:, i % 2], x[:, i, D + 1:D + 2], None, ALU.mult
                                  ).then_inc(result_ready, 1)

            def step(s, i, k):
                if i + 1 < AHEAD:
                    take_turned(s + 1, i + 1, k)
                elif not (isinstance(s, int) and s + 1 == SLOTS):
                    take_turned(s + 1, 0, k + 1)
                if i > 0:
                    weigh(s - 1, i - 1, k)
                elif reached(s, 1):
                    weigh(s - 1, AHEAD - 1, k - 1)

            take_turned(0, 0, 0)
            for i in range(AHEAD):
                step(i, i, 0)
            with dve.Fori(1, ROUNDS - 1) as k:
                for i in range(AHEAD):
                    step(k * AHEAD + i, i, k)
            for i in range(AHEAD):
                step(SLOTS - AHEAD + i, i, ROUNDS - 1)
            weigh(SLOTS - 1, AHEAD - 1, ROUNDS - 1)




def build_program(nc, io):
    image_stage(nc, io)
    text_stage(nc, io)
    attention_stage(nc, io)
    with nc.sbuf_tensor("slots", [1, 3, SLOTS], I32) as slots:
        routing_stage(nc, io, slots)
        expert_stage(nc, io, slots)




def _layouts(a):
    import numpy as np
    P = 128
    out = {}
    out["txt_idx"] = a["x_txt"].reshape(-1, P).T
    out["txt_pos"] = np.tile(a["L0_txt_pos_encoding"][0, :TEXT_LEN], (P // TEXT_LEN, 1))
    out["embedding"] = a["L0_txt_embedding"]
    out["ident"] = np.eye(P, dtype=np.float32)
    out["txt_final_g"] = np.broadcast_to(a["L0_txt_final_g"], (P, D))
    out["txt_final_b"] = np.broadcast_to(a["L0_txt_final_b"], (P, D))
    gb = np.stack([a["L0_txt_ln_g"], a["L0_txt_ln_b"]], 1)
    out["txt_ln_gb"] = gb.reshape(LAYERS, 2, 2, HALF).transpose(3, 0, 1, 2)
    out["txt_taps"] = a["L0_txt_conv_w"].reshape(LAYERS, DI_CHUNKS, HALF, 3).transpose(2, 0, 1, 3)
    out["txt_dt_b"] = a["L0_txt_dt_b"].reshape(LAYERS, DI_CHUNKS, HALF).transpose(2, 0, 1)
    out["txt_in_w"] = a["L0_txt_in_w"].reshape(LAYERS, 2 * DI, 2, HALF).transpose(0, 3, 2, 1)
    out["txt_dt_w"] = a["L0_txt_dt_w"].reshape(LAYERS, DI, DI_CHUNKS, HALF).transpose(0, 3, 2, 1)
    ow = a["L0_txt_out_w"].reshape(LAYERS, D, DI_CHUNKS, HALF).transpose(0, 3, 2, 1)
    ls = np.broadcast_to(a["L0_txt_layer_scale"][:, None, None, :], (LAYERS, HALF, 1, D))
    out["txt_out_w"] = np.concatenate([ow, ls], 2)
    def blocks(w):
        w = w.reshape(-1, 3, HEADS // 2, 2, D)
        tail = w[..., 128:].reshape(w.shape[0], 3, HEADS // 2, 1, 128)
        return np.concatenate([w[..., :128], tail], 3).reshape(w.shape[0], -1, 128)
    out["qkv_w"] = blocks(a["L0_attn_W_qkv"]).reshape(2, HALF, -1, 128).transpose(1, 0, 2, 3)
    out["qkv_b"] = blocks(a["L0_attn_b_qkv"][None])[0].T
    out["proj_w"] = a["L0_attn_W_proj"].reshape(2 * HEADS, HALF, D).transpose(1, 0, 2)
    out["proj_b"] = np.broadcast_to(a["L0_attn_b_proj"], (PAIR, D))
    first = np.repeat([1.0, 0.0], SEQ)
    out["mask"] = np.stack([np.stack([first, 1 - first]), np.stack([1 - first, first]) * -1e30], 1).astype(np.float32)
    f = np.float32
    xp = np.pad(a["x"], ((0, 0), (0, 0), (1, 1), (1, 1)))
    out["img_x"] = xp.reshape(8, 8 * C0, -1).transpose(1, 0, 2)
    w0 = np.zeros((3, 8, C0, 3, 8, C1), f)
    for b in range(8):
        w0[:, b, :, :, b, :] = a["L0_tok_w0"].transpose(2, 1, 3, 0)
    out["img_w0"] = w0.reshape(72, 3, 96)
    out["img_sb0"] = np.tile(np.stack([a["L0_tok_s0"], a["L0_tok_b0"]], 1), (8, 1))
    pw = a["L0_tok_wpw"].reshape(GRID, GRID, C1, C1).transpose(0, 3, 1, 2)
    pwd = np.zeros((GRID, 8, C1, GRID, 8, C1), f)
    for b in range(8):
        pwd[:, b, :, :, b, :] = pw
    spw = np.broadcast_to(a["L0_tok_spw"].reshape(GRID, 1, GRID, 1, C1), (GRID, 96, GRID, 8, C1))
    def by_channel(v):
        return np.tile(v.reshape(GRID, GRID, C1, -1).transpose(0, 2, 1, 3), (1, 8, 1, 1)).reshape(GRID, 96, -1)
    out["img_par"] = np.concatenate([pwd.reshape(GRID, 96, -1), spw.reshape(GRID, 96, -1), by_channel(a["L0_tok_wdw"]),
                                     by_channel(a["L0_tok_sdw"]), by_channel(a["L0_tok_bdw"]),
                                     by_channel(a["L0_tok_bpw"])], 2)
    w1 = a["L0_tok_w1"].transpose(1, 2, 3, 0).reshape(2, 96, C2).transpose(1, 0, 2)
    out["img_w1"] = np.pad(w1, ((0, 0), (0, 0), (0, 64 - C2)))
    def padded_pair(s, b):
        return np.tile(np.pad(np.stack([s, b], 1), ((0, 64 - C2), (0, 0))), (2, 1))
    out["img_sb1"] = padded_pair(a["L0_tok_s1"], a["L0_tok_b1"])
    out["img_sb2"] = padded_pair(a["L0_tok_s2"], a["L0_tok_b2"])
    w2 = np.zeros((2, 64, 4, 2, 64), f)
    for k in range(2):
        w2[k, :C2, :, k, :C2] = a["L0_tok_w2"].transpose(1, 2, 3, 0).reshape(C2, 4, C2)
    out["img_w2"] = w2.reshape(128, 4, 128)
    w3 = np.pad(a["L0_tok_w3"].transpose(1, 2, 3, 0).reshape(C2, 4, D), ((0, 64 - C2), (0, 0), (0, 0)))
    out["img_w3"] = np.tile(w3, (2, 1, 1))
    out["img_sb3"] = np.broadcast_to(np.stack([a["L0_tok_s3"], a["L0_tok_b3"]])[None], (128, 2, D))
    out["router_w"] = a["L0_ffn_Wr"].reshape(EXPERTS, 2, HALF).transpose(2, 1, 0)
    out["up_w"] = a["L0_ffn_Wi"].reshape(EXPERTS, F, 2, HALF).transpose(0, 3, 2, 1).reshape(EXPERTS, HALF, 2 * F)
    down_w = a["L0_ffn_Wo"].reshape(EXPERTS, D, F // P, P).transpose(0, 3, 2, 1).reshape(EXPERTS, P, -1)
    down_b = np.broadcast_to(a["L0_ffn_bo"][:, None, :], (EXPERTS, P, D))
    out["up_b"] = a["L0_ffn_bi"].reshape(EXPERTS, F // P, P).transpose(0, 2, 1)
    out["down_w"] = np.concatenate([down_w, down_b], 2)
    out["earlier"] = np.stack([np.triu(np.ones((PAIR, PAIR)), 1), np.ones((PAIR, PAIR))], 1).astype(np.float32)
    out["token_no"] = np.arange(TOKENS, dtype=np.int32).reshape(TILES, PAIR).T
    out["pad_no"] = (TOKENS + np.arange(SLOT, dtype=np.int32))[:, None]
    starts = np.arange(EXPERTS, dtype=np.float32) * REGION
    out["region_at"] = np.broadcast_to(starts, (PAIR, 8, EXPERTS))
    out["slot_no"] = np.arange(SLOTS, dtype=np.float32)[None]
    return {name: np.ascontiguousarray(v) for name, v in out.items()}


def kernel(**inputs):
    import numpy as np
    import concourse.bacc as bacc
    from concourse.bass_utils import run_bass_kernel_spmd

    nc = bacc.Bacc("TRN2", target_bir_lowering=False, num_devices=1)
    arrays = _layouts({name: np.asarray(v) for name, v in inputs.items()})
    io = {name: nc.dram_tensor("in_" + name, v.shape, mybir.dt.from_np(v.dtype), kind="ExternalInput").ap()
          for name, v in arrays.items()}
    io["out"] = nc.dram_tensor("out_dram", (TOKENS + SLOT, D), F32, kind="ExternalOutput").ap()
    io["h"] = nc.dram_tensor("h_dram", (TOKENS, D), F32).ap()
    io["img_taps"] = nc.dram_tensor("img_taps_dram", (2, 96, 3840), F32).ap()
    io["dispatch"] = nc.dram_tensor("dispatch_dram", (SPARE + SLOT, ROW), F32).ap()
    build_program(nc, io)
    r = run_bass_kernel_spmd(nc, [{"in_" + name: v for name, v in arrays.items()}], core_ids=[0])
    return r.results[0]["out_dram"][:TOKENS].reshape(BATCH, SEQ, D)
```

```python
from contextlib import ExitStack

import concourse.bass as bass
from concourse import mybir

F32 = mybir.dt.float32
F32R = mybir.dt.float32r
BF16 = mybir.dt.bfloat16
I32 = mybir.dt.int32
U32 = mybir.dt.uint32
ALU = mybir.AluOpType
ACT = mybir.ActivationFunctionType
AX_X = mybir.AxisListType.X

BATCH = 64
D = 192
HALF = D // 2
TEXT_LEN = 32
IMG_LEN = 25
SEQ = IMG_LEN + TEXT_LEN
TOKENS = BATCH * SEQ
EPS = 1e-5
LN2 = 0.6931471805599453

LAYERS = 4
DI = 288
DI_CHUNKS = DI // HALF


def reached(step, n):
    return not isinstance(step, int) or step >= n


def text_stage(nc, io, wait_carrier):
    T = TEXT_LEN
    seqs_per_tile = 128 // T
    tiles = BATCH * T // 128
    TG = 4
    groups = tiles // TG
    N = 128 * TG
    steps = LAYERS * groups
    IN, C = 2 * DI_CHUNKS, DI_CHUNKS

    with ExitStack() as ctx:
        def sb(name, shape, dt=F32):
            return ctx.enter_context(nc.sbuf_tensor("txt_sb_" + name, shape, dt))

        def ps(name, shape):
            return ctx.enter_context(nc.psum_tensor("txt_ps_" + name, shape, F32))

        def sem(name):
            return ctx.enter_context(nc.semaphore("txt_" + name))

        idx = sb("idx", [128, tiles], I32)
        pos = sb("pos", [128, D])
        x = sb("x", [128, tiles, D])
        ident = sb("ident", [128, 128])
        final_g = sb("final_g", [128, D])
        final_b = sb("final_b", [128, D])
        ln_gb = sb("ln_gb", [HALF, LAYERS, 2, 2])
        taps = sb("taps", [HALF, LAYERS, C, 3])
        dt_b = sb("dt_b", [HALF, LAYERS, C])
        dt_bias = sb("dt_bias", [HALF, LAYERS, C])
        in_w = sb("in_w", [HALF, 2, 2 * DI])
        dt_w = sb("dt_w", [HALF, C, DI])
        out_raw = sb("out_raw", [HALF, C + 1, D])
        half_scale = sb("half_scale", [HALF, D])
        out_w = sb("out_w", [HALF, C, D])
        minus_half = sb("minus_half", [128, TG])
        stats = sb("stats", [128, TG, 6])
        mv = sb("mv", [128, 2, TG, 2])
        var_eps = sb("var_eps", [128, TG])
        rstd = sb("rstd", [128, 2, TG])
        xn = sb("xn", [128, TG, D])
        xnT = sb("xnT", [HALF, 2, N])
        conv = sb("conv", [HALF, C, N])
        conv_sg = sb("conv_sg", [HALF, C, N])
        ssm = sb("ssm", [HALF, 2, C, N])
        x2_sg = sb("x2_sg", [HALF, 2, C, N])
        dt_sg = sb("dt_sg", [HALF, C, N])
        gate = sb("gate", [HALF, C, N])
        xg = sb("xg", [HALF, C, N])
        turn_ps = ps("turn_ps", [HALF, 2, 512])
        ring_ps = ps("ring_ps", [HALF, 4, 512])
        out_ps = ps("out_ps", [128, TG, 256])

        idx_loaded = sem("idx_loaded")
        const_loaded = sem("const_loaded")
        gathered = [sem("gathered_%d" % g) for g in range(groups)]
        embedded = sem("embedded")
        consts_set = sem("consts_set")
        dt_bias_set = sem("dt_bias_set")
        in_w_loaded = sem("in_w_loaded")
        dt_w_loaded = sem("dt_w_loaded")
        out_raw_loaded = sem("out_raw_loaded")
        scale_halved = sem("scale_halved")
        out_w_ready = sem("out_w_ready")
        stats_done = sem("stats_done")
        var_ready = sem("var_ready")
        eps_added = sem("eps_added")
        rstd_ready = sem("rstd_ready")
        normed = sem("normed")
        turned = sem("turned")
        xnT_ready = sem("xnT_ready")
        in_done = sem("in_done")
        conv_tap = sem("conv_tap")
        conv_done = sem("conv_done")
        conv_sg_done = sem("conv_sg_done")
        x2_sg_done = sem("x2_sg_done")
        ssm_ready = sem("ssm_ready")
        dt_done = sem("dt_done")
        dt_sg_done = sem("dt_sg_done")
        gate_done = sem("gate_done")
        xg_ready = sem("xg_ready")
        out_done = sem("out_done")
        added = sem("added")
        scaled = sem("scaled")
        final_ready = sem("final_ready")
        h_stored = sem("h_stored")

        def over_steps(eng, body):
            for g in range(groups):
                body(g, 0, g)
            with eng.Fori(1, LAYERS - 1) as layer:
                for g in range(groups):
                    body(layer * groups + g, layer, g)
            for g in range(groups):
                body((LAYERS - 1) * groups + g, LAYERS - 1, g)

        def next_layer(layer, g):
            return layer + 1 if g == groups - 1 else layer

        block = ctx.enter_context(nc.Block())

        @block.sync
        def _(sp):
            sp.dma_start(idx[:], io["txt_idx"]).then_inc(idx_loaded, 16)
            for dst, name in ((pos, "txt_pos"), (ident, "ident"), (final_g, "txt_final_g"), (final_b, "txt_final_b"),
                              (ln_gb, "txt_ln_gb"), (taps, "txt_taps"), (dt_b, "txt_dt_b")):
                sp.dma_start(dst[:], io[name]).then_inc(const_loaded, 16)

            def load_layer(layer):
                if reached(layer, 1):
                    sp.wait_ge(in_done, layer * (groups * IN))
                    sp.sem_inc(wait_carrier, 1)
                sp.dma_start(in_w[:], io["txt_in_w"][layer]).then_inc(in_w_loaded, 16)
                if reached(layer, 1):
                    sp.wait_ge(out_w_ready, layer)
                    sp.sem_inc(wait_carrier, 1)
                sp.dma_start(out_raw[:], io["txt_out_w"][layer]).then_inc(out_raw_loaded, 16)
                if reached(layer, 1):
                    sp.wait_ge(dt_done, layer * (groups * C))
                    sp.sem_inc(wait_carrier, 1)
                sp.dma_start(dt_w[:], io["txt_dt_w"][layer]).then_inc(dt_w_loaded, 16)

            load_layer(0)
            with sp.Fori(1, LAYERS) as layer:
                load_layer(layer)
            rows = io["h"].rearrange("(n b t) d -> b t n d", b=seqs_per_tile, t=SEQ)
            for g in range(groups):
                sp.wait_ge(final_ready, g + 1)
                for b in range(seqs_per_tile):
                    sp.dma_start(rows[b, IMG_LEN:SEQ, g * TG:(g + 1) * TG, :],
                                 x[b * T:(b + 1) * T, g * TG:(g + 1) * TG, :]).then_inc(h_stored, 16)
            sp.wait_ge(h_stored, 16 * groups * seqs_per_tile)

        @block.gpsimd
        def _(pool):
            def gather(g):
                for t in range(g * TG, (g + 1) * TG):
                    pool.indirect_dma_start(
                        out=x[:, t, :], out_offset=None, in_=io["embedding"],
                        in_offset=bass.IndirectOffsetOnAxis(ap=idx[:, t:t + 1].bitcast(U32), axis=0),
                    ).then_inc(gathered[g], 16)

            pool.wait_ge(idx_loaded, 16)
            gather(0)
            pool.memset(minus_half[:], -0.5).then_inc(consts_set, 1)
            pool.wait_ge(consts_set, 1)
            pool.wait_ge(const_loaded, 16 * 7)
            pool.tensor_scalar(dt_bias[:], dt_b[:], -LN2, None, ALU.add).then_inc(dt_bias_set, 1)

            def inverse_deviation(n, par):
                pool.wait_ge(var_ready, n + 1)
                pool.sem_inc(wait_carrier, 1)
                pool.tensor_scalar(var_eps[:], mv[:, par, :, 1], EPS, None, ALU.add).then_inc(eps_added, 1)
                pool.wait_ge(eps_added, n + 1)
                pool.tensor_tensor(rstd[:, par, :], var_eps[:], minus_half[:], ALU.pow).then_inc(rstd_ready, 1)

            def scale_out_weights(layer):
                pool.wait_ge(out_raw_loaded, (layer + 1) * 16)
                pool.sem_inc(wait_carrier, 1)
                pool.tensor_scalar(half_scale[:], out_raw[:, C, :], 0.5, None, ALU.mult).then_inc(scale_halved, 1)
                pool.wait_ge(scale_halved, layer + 1)
                if reached(layer, 1):
                    pool.wait_ge(out_done, layer * groups)
                for c in range(C):
                    last = pool.tensor_tensor(out_w[:, c, :], out_raw[:, c, :], half_scale[:], ALU.mult)
                last.then_inc(out_w_ready, 1)

            inverse_deviation(0, 0)
            gather(1)
            scale_out_weights(0)
            gather(2)
            gather(3)

            def step(i, layer, g):
                if not (isinstance(i, int) and i == steps - 1):
                    inverse_deviation(i + 1, (g + 1) % 2)
                if g == 1 and reached(layer, 1):
                    scale_out_weights(layer)

            over_steps(pool, step)
            for g in range(groups):
                inverse_deviation(steps + g, g % 2)

        @block.tensor
        def _(pe):
            def turn(i, g):
                pe.wait_ge(normed, i + 1)
                if reached(i, 1):
                    pe.wait_ge(xnT_ready, i * 2)
                for h in range(2):
                    for t in range(TG):
                        last = pe.transpose(turn_ps[:, h, t * 128:(t + 1) * 128],
                                            xn[:, t, h * HALF:(h + 1) * HALF], ident[:])
                    last.then_inc(turned, 1)

            def ring_free(i, k):
                if k == 0:
                    if reached(i, 1):
                        pe.wait_ge(x2_sg_done, i * C)
                elif k < 4:
                    if reached(i, 2):
                        pe.wait_ge(dt_sg_done, (i - 2) * C + k)
                elif k < 7:
                    pe.wait_ge(conv_done, i * C + (k - 3))
                else:
                    pe.wait_ge(x2_sg_done, i * C + (k - 6))

            def in_projection(i, layer, g):
                if g == 0:
                    pe.wait_ge(in_w_loaded, (layer + 1) * 16)
                pe.wait_ge(xnT_ready, (i + 1) * 2)
                for k in range(IN):
                    ring_free(i, k)
                    for h in range(2):
                        mm = pe.matmul(ring_ps[:, (g * (IN + C) + k) % 4, :], in_w[:, h, k * HALF:(k + 1) * HALF],
                                       xnT[:, h, :], start=(h == 0), stop=(h == 1))
                    mm.then_inc(in_done, 1)

            def dt_product(i, g_now, layer, g, free):
                if g == 0:
                    pe.wait_ge(dt_w_loaded, (layer + 1) * 16)
                pe.wait_ge(ssm_ready, (i + 1) * C)
                for m in range(C):
                    free(m)
                    for c in range(C):
                        mm = pe.matmul(ring_ps[:, (g_now * (IN + C) + IN + m) % 4, :], dt_w[:, c, m * HALF:(m + 1) * HALF],
                                       ssm[:, g % 2, c, :], start=(c == 0), stop=(c == C - 1))
                    mm.then_inc(dt_done, 1)

            def out_product(i, layer, g):
                if g == 0:
                    pe.wait_ge(out_w_ready, layer + 1)
                pe.wait_ge(xg_ready, (i + 1) * C)
                if reached(i, 1):
                    pe.wait_ge(added, i)
                for t in range(TG):
                    for c in range(C):
                        mm = pe.matmul(out_ps[:, t, 0:D], xg[:, c, t * 128:(t + 1) * 128], out_w[:, c, :],
                                       start=(c == 0), stop=(c == C - 1))
                mm.then_inc(out_done, 1)

            pe.wait_ge(const_loaded, 16 * 7)
            turn(0, 0)

            def step(i, layer, g):
                in_projection(i, layer, g)
                if reached(i, 2):
                    out_product(i - 2, layer if g >= 2 else layer - 1, (g - 2) % groups)
                if not (isinstance(i, int) and i == steps - 1):
                    turn(i + 1, (g + 1) % groups)
                if reached(i, 1):
                    dt_product(i - 1, g, layer if g >= 1 else layer - 1, (g - 1) % groups,
                               lambda m: ring_free(i, IN + m))

            over_steps(pe, step)
            out_product(steps - 2, LAYERS - 1, groups - 2)
            pe.wait_ge(conv_done, steps * C)
            pe.wait_ge(x2_sg_done, steps * C)
            pe.wait_ge(dt_sg_done, (steps - 1) * C)
            dt_product(steps - 1, 0, LAYERS - 1, groups - 1, lambda m: None)
            out_product(steps - 1, LAYERS - 1, groups - 1)

        @block.scalar
        def _(act):
            def take_turned(i, layer):
                if reached(i, 1):
                    act.wait_ge(in_done, i * IN)
                for h in range(2):
                    act.wait_ge(turned, i * 2 + (h + 1))
                    act.sem_inc(wait_carrier, 1)
                    act.activation(xnT[:, h, :], turn_ps[:, h, :], ACT.Identity, scale=ln_gb[:, layer, 0, h:h + 1],
                                   bias=ln_gb[:, layer, 1, h:h + 1]).then_inc(xnT_ready, 1)

            def gate_sigmoids(i, layer, g, slot_g):
                for m in range(C):
                    act.wait_ge(dt_done, i * C + (m + 1))
                    if m == 0 and reached(i, 1):
                        act.wait_ge(gate_done, i * C)
                    act.sem_inc(wait_carrier, 1)
                    act.activation(dt_sg[:, m, :], ring_ps[:, (slot_g * (IN + C) + IN + m) % 4, :], ACT.Sigmoid,
                                   bias=dt_bias[:, layer, m:m + 1]).then_inc(dt_sg_done, 1)

            act.wait_ge(const_loaded, 16 * 7)
            act.wait_ge(dt_bias_set, 1)
            take_turned(0, 0)

            def step(i, layer, g):
                for c in range(C):
                    act.wait_ge(in_done, i * IN + (C + c + 1))
                    if c == 0 and reached(i, 2):
                        act.wait_ge(xg_ready, (i - 1) * C)
                    act.activation(x2_sg[:, g % 2, c, :], ring_ps[:, (g * (IN + C) + C + c) % 4, :],
                                   ACT.Sigmoid).then_inc(x2_sg_done, 1)
                for c in range(C):
                    act.wait_ge(conv_done, i * C + (c + 1))
                    if c == 0 and reached(i, 1):
                        act.wait_ge(ssm_ready, i * C)
                    act.activation(conv_sg[:, c, :], conv[:, c, :], ACT.Sigmoid).then_inc(conv_sg_done, 1)
                if not (isinstance(i, int) and i == steps - 1):
                    take_turned(i + 1, next_layer(layer, g))
                if reached(i, 1):
                    gate_sigmoids(i - 1, layer if g >= 1 else layer - 1, (g - 1) % groups, g)

            over_steps(act, step)
            gate_sigmoids(steps - 1, LAYERS - 1, groups - 1, 0)

        @block.vector
        def _(dve):
            def statistics(n, g, par):
                for t in range(TG):
                    s = dve.bn_stats(stats[:, t, :], x[:, g * TG + t, :])
                s.then_inc(stats_done, 1)
                dve.wait_ge(stats_done, n + 1)
                dve.sem_inc(wait_carrier, 1)
                for t in range(TG):
                    s = dve.bn_aggr(mv[:, par, t, :], stats[:, t, :])
                s.then_inc(var_ready, 1)

            def normalise(n, g, par):
                dve.wait_ge(rstd_ready, n + 1)
                if reached(n, 1):
                    dve.wait_ge(turned, n * 2)
                for t in range(TG):
                    s = dve.tensor_scalar(xn[:, t, :], x[:, g * TG + t, :], mv[:, par, t, 0:1], rstd[:, par, t:t + 1],
                                          ALU.subtract, ALU.mult)
                s.then_inc(normed, 1)

            def convolve(i, layer, g):
                for c in range(C):
                    seq = ring_ps[:, (g * (IN + C) + c) % 4, :].rearrange("p (s l) -> p s l", l=T)
                    out = conv[:, c, :].rearrange("p (s l) -> p s l", l=T)
                    dve.wait_ge(in_done, i * IN + (c + 1))
                    dve.tensor_scalar(out, seq, taps[:, layer, c, 1:2], None, ALU.mult).then_inc(conv_tap, 1)
                    dve.wait_ge(conv_tap, i * (2 * C) + (2 * c + 1))
                    dve.scalar_tensor_tensor(out[:, :, 1:T], seq[:, :, 0:T - 1], taps[:, layer, c, 0:1], out[:, :, 1:T],
                                             ALU.mult, ALU.add).then_inc(conv_tap, 1)
                    dve.wait_ge(conv_tap, i * (2 * C) + (2 * c + 2))
                    dve.scalar_tensor_tensor(out[:, :, 0:T - 1], seq[:, :, 1:T], taps[:, layer, c, 2:3], out[:, :, 0:T - 1],
                                             ALU.mult, ALU.add).then_inc(conv_done, 1)

            def silu(i, g):
                if reached(i, 2):
                    dve.wait_ge(dt_done, (i - 1) * C)
                for c in range(C):
                    dve.wait_ge(conv_sg_done, i * C + (c + 1))
                    dve.tensor_tensor(ssm[:, g % 2, c, :], conv[:, c, :], conv_sg[:, c, :],
                                      ALU.mult).then_inc(ssm_ready, 1)

            def apply_gate(i, g):
                if reached(i, 1):
                    dve.wait_ge(out_done, i)
                for c in range(C):
                    dve.wait_ge(dt_sg_done, i * C + (c + 1))
                    dve.scalar_tensor_tensor(gate[:, c, :], dt_sg[:, c, :], 1.0, x2_sg[:, g % 2, c, :],
                                             ALU.add, ALU.mult).then_inc(gate_done, 1)
                for c in range(C):
                    dve.wait_ge(gate_done, i * C + (c + 1))
                    dve.tensor_tensor(xg[:, c, :], gate[:, c, :], ssm[:, g % 2, c, :], ALU.mult).then_inc(xg_ready, 1)

            def add_residual(i, g):
                dve.wait_ge(out_done, i + 1)
                dve.tensor_tensor(x[:, g * TG:(g + 1) * TG, :], x[:, g * TG:(g + 1) * TG, :], out_ps[:, :, 0:D],
                                  ALU.add).then_inc(added, 1)

            dve.wait_ge(const_loaded, 16 * 7)
            def embed(g):
                dve.wait_ge(gathered[g], 16 * TG)
                for t in range(g * TG, (g + 1) * TG):
                    dve.tensor_tensor(x[:, t, :], x[:, t, :], pos[:], ALU.add).then_inc(embedded, 1)
                dve.wait_ge(embedded, (g + 1) * TG)

            embed(0)
            statistics(0, 0, 0)
            normalise(0, 0, 0)

            def step(i, layer, g):
                more = not (isinstance(i, int) and i == steps - 1)
                if more:
                    if reached(i, 3):
                        dve.wait_ge(added, i - 2)
                    else:
                        embed(i + 1)
                    statistics(i + 1, (g + 1) % groups, (g + 1) % 2)
                convolve(i, layer, g)
                if more:
                    normalise(i + 1, (g + 1) % groups, (g + 1) % 2)
                if reached(i, 2):
                    add_residual(i - 2, (g - 2) % groups)
                silu(i, g)
                if reached(i, 1):
                    apply_gate(i - 1, (g - 1) % groups)

            def final_norm(g):
                dve.wait_ge(added, steps - groups + 1 + g)
                statistics(steps + g, g, g % 2)
                dve.wait_ge(rstd_ready, steps + g + 1)
                if g == 0:
                    dve.wait_ge(turned, 2 * steps)
                else:
                    dve.wait_ge(final_ready, g)
                for t in range(TG):
                    s = dve.scalar_tensor_tensor(xn[:, t, :], x[:, g * TG + t, :], mv[:, g % 2, t, 0:1], final_g[:],
                                                 ALU.subtract, ALU.mult)
                s.then_inc(scaled, 1)
                dve.wait_ge(scaled, g + 1)
                for t in range(TG):
                    s = dve.scalar_tensor_tensor(x[:, g * TG + t, :], xn[:, t, :], rstd[:, g % 2, t:t + 1], final_b[:],
                                                 ALU.mult, ALU.add)
                s.then_inc(final_ready, 1)

            over_steps(dve, step)
            add_residual(steps - 2, groups - 2)
            final_norm(0)
            apply_gate(steps - 1, groups - 1)
            final_norm(1)
            add_residual(steps - 1, groups - 1)
            final_norm(2)
            final_norm(3)




PAIR = 2 * SEQ
HEADS = 8
TILES = TOKENS // PAIR
SCALING = float(D) ** 0.5


def attention_stage(nc, io, rows, wait_carrier):
    GB = 4
    GT = GB * SEQ
    groups = BATCH // GB
    ROWS = SEQ * HEADS
    PAIRS = ROWS // PAIR
    BLOCKS = 3 * HEADS // 2 * 3
    SLOTS = BLOCKS + 1
    BPS = BLOCKS // GB
    STAGES = 3
    PART = 6
    PARTS = BLOCKS // PART
    BIG, SMALL = 128, D - 128

    with ExitStack() as ctx:
        def sb(name, shape, dt=F32):
            return ctx.enter_context(nc.sbuf_tensor("att_sb_" + name, shape, dt))

        def ps(name, shape):
            return ctx.enter_context(nc.psum_tensor("att_ps_" + name, shape, F32))

        def sem(name):
            return ctx.enter_context(nc.semaphore("att_" + name))

        ident = sb("ident", [128, 128])
        qkv_w_high = sb("qkv_w_high", [HALF, 2, BLOCKS, 128], F32R)
        qkv_w_low = sb("qkv_w_low", [HALF, 2, BLOCKS, 128], F32R)
        qkv_b = sb("qkv_b", [128, BLOCKS])
        proj_w = sb("proj_w", [128, 3 * HEADS // 2, D])
        proj_b = sb("proj_b", [PAIR, D])
        mask_f = sb("mask_f", [2, 2, PAIR])
        mask = sb("mask", [2, 2, PAIR], BF16)
        h_in = sb("h_in", [PAIR, 2, 2, D])
        minus_half = sb("minus_half", [PAIR, 2])
        stats = sb("stats", [PAIR, 2, 6])
        mv = sb("mv", [PAIR, 2, 2])
        var_eps = sb("var_eps", [PAIR, 2])
        rstd = sb("rstd", [PAIR, 2])
        out_stats = sb("out_stats", [PAIR, 6])
        out_mv = sb("out_mv", [PAIR, 2])
        out_var_eps = sb("out_var_eps", [PAIR, 1])
        out_rstd = sb("out_rstd", [PAIR, 1])
        xn = sb("xn", [PAIR, 2, D])
        xnT_high = sb("xnT_high", [HALF, 2, GT], F32R)
        xnT_low = sb("xnT_low", [HALF, 2, GT], F32R)
        big = sb("big", [BIG, 2, 3, GT * HEADS])
        small = sb("small", [2 * SMALL, 3, GT * HEADS])
        h1 = sb("h1", [PAIR, 2, 2, D])
        v_rows = sb("v_rows", [PAIR, PAIRS, D])
        row_max = sb("row_max", [PAIR, PAIRS])
        row_sum = sb("row_sum", [PAIR, PAIRS])
        sum_scaled = sb("sum_scaled", [PAIR, PAIRS])
        inv_sum = sb("inv_sum", [PAIR, PAIRS])
        probs = sb("probs", [PAIR, 2, PAIRS, PAIR])
        probsT = sb("probsT", [PAIR, PAIRS, PAIR])
        outT = sb("outT", [BIG, 2, 2 * ROWS])
        outT_rest = sb("outT_rest", [2 * SMALL, 2, ROWS])
        ring_ps = ps("ring_ps", [128, 2, 512])
        score_ps = ps("score_ps", [PAIR, 512])
        v_ps = ps("v_ps", [PAIR, 2, 256])
        probsT_ps = ps("probsT_ps", [PAIR, 512])
        out_ps = ps("out_ps", [BIG, 2, 512])
        proj_ps = ps("proj_ps", [PAIR, 512])

        const_loaded = sem("const_loaded")
        qkv_w_loaded = [sem("qkv_w_loaded_%d" % i) for i in range(STAGES)]
        qkv_w_high_ready = sem("qkv_w_high_ready")
        qkv_w_ready = sem("qkv_w_ready")
        xnT_low_ready = sem("xnT_low_ready")
        proj_w_loaded = sem("proj_w_loaded")
        h_loaded = [sem("h_loaded_even"), sem("h_loaded_odd")]
        half_set = sem("half_set")
        mask_ready = sem("mask_ready")
        stats_done = sem("stats_done")
        var_ready = sem("var_ready")
        eps_added = sem("eps_added")
        rstd_ready = sem("rstd_ready")
        normed = sem("normed")
        out_stats_done = sem("out_stats_done")
        out_var_ready = sem("out_var_ready")
        out_eps_added = sem("out_eps_added")
        out_rstd_ready = sem("out_rstd_ready")
        out_normed = sem("out_normed")
        h_biased = sem("h_biased")
        ring_done = sem("ring_done")
        ring_read = sem("ring_read")
        scored = sem("scored")
        max_done = sem("max_done")
        shifted = sem("shifted")
        exp_done = sem("exp_done")
        sum_step = sem("sum_step")
        probs_ready = sem("probs_ready")
        probs_turned = sem("probs_turned")
        probsT_ready = sem("probsT_ready")
        v_turned = sem("v_turned")
        v_ready = sem("v_ready")
        out_done = sem("out_done")
        outT_ready = sem("outT_ready")
        proj_done = sem("proj_done")
        h1_ready = sem("h1_ready")
        h1_stored = [sem("h1_stored_even"), sem("h1_stored_odd")]

        def over_groups(eng, body):
            body(0, 0)
            body(1, 1)
            with eng.Fori(1, groups // 2 - 1) as k:
                body(k * 2, 0)
                body(k * 2 + 1, 1)
            body(groups - 2, 0)
            body(groups - 1, 1)

        def exists(group, ahead):
            return not (isinstance(group, int) and group + ahead >= groups)

        block = ctx.enter_context(nc.Block())

        def staged(part):
            size = 2 * PART * 128
            at = (part % STAGES) * size
            return (big[0:HALF, 1].rearrange("p k n -> p (k n)")[:, at:at + size]
                    .rearrange("p (h b f) -> p h b f", h=2, b=PART))

        def small_at(par, kind):
            return small[par * SMALL:(par + 1) * SMALL, kind, :]

        @block.sync
        def _(sp):
            def store(group, par):
                sp.wait_ge(h1_ready, group * 2 + 2)
                sp.sem_inc(wait_carrier, 1)
                sp.dma_start(io["out"][bass.ds(group * GT, GT), :].rearrange("(t p) d -> p t d", p=PAIR), h1[:, par]
                             ).then_inc(h1_stored[par], 16)

            def load(group, par):
                if reached(group, 2):
                    sp.wait_ge(h_biased, group - 1)
                    sp.wait_ge(normed, group - 1)
                    sp.sem_inc(wait_carrier, 1)
                sp.dma_start(h_in[:, par], io["h"][bass.ds(group * GT, GT), :].rearrange("(t p) d -> p t d", p=PAIR)
                             ).then_inc(h_loaded[par], 16)

            load(0, 0)
            load(1, 1)
            for dst, name in ((ident, "ident"), (qkv_b, "qkv_b"), (proj_b, "proj_b"), (mask_f, "mask")):
                sp.dma_start(dst[:], io[name]).then_inc(const_loaded, 16)
            for part in range(PARTS):
                if part >= STAGES:
                    sp.wait_ge(qkv_w_ready, part - STAGES + 1)
                sp.dma_start(staged(part), io["qkv_w"][:, :, part * PART:(part + 1) * PART, :]
                             ).then_inc(qkv_w_loaded[part % STAGES], 16)
            sp.dma_start(proj_w[:], io["proj_w"]).then_inc(proj_w_loaded, 16)
            load(2, 0)
            store(0, 0)
            load(3, 1)
            with sp.Fori(2, groups // 2) as k:
                store(k * 2 - 3, 1)
                load(k * 2, 0)
                store(k * 2 - 2, 0)
                load(k * 2 + 1, 1)
            store(groups - 3, 1)
            store(groups - 2, 0)
            store(groups - 1, 1)
            for par in range(2):
                sp.wait_ge(h1_stored[par], 16 * (groups // 2))

        @block.gpsimd
        def _(pool):
            pool.memset(minus_half[:], -0.5).then_inc(half_set, 1)
            pool.wait_ge(half_set, 1)
            pool.wait_ge(const_loaded, 16 * 4)

            def rstd_of(group):
                pool.wait_ge(var_ready, group + 1)
                pool.sem_inc(wait_carrier, 1)
                pool.tensor_scalar(var_eps[:], mv[:, :, 1], EPS, None, ALU.add).then_inc(eps_added, 1)
                pool.wait_ge(eps_added, group + 1)
                if reached(group, 1):
                    pool.wait_ge(normed, group)
                pool.tensor_tensor(rstd[:], var_eps[:], minus_half[:], ALU.pow).then_inc(rstd_ready, 1)

            def add_bias(group, par, k):
                pool.wait_ge(h_loaded[par], (k + 1) * 16)
                if reached(group, 2):
                    pool.wait_ge(h1_stored[par], k * 16)
                    pool.wait_ge(out_normed, (group - 1) * 2)
                for t in range(2):
                    last = pool.tensor_tensor(h1[:, par, t, :], h_in[:, par, t, :], proj_b[:], ALU.add)
                last.then_inc(h_biased, 1)

            def out_rstd_of(tile):
                pool.wait_ge(out_var_ready, tile + 1)
                if reached(tile, 1):
                    pool.wait_ge(out_normed, tile)
                    pool.sem_inc(wait_carrier, 1)
                pool.tensor_scalar(out_var_eps[:], out_mv[:, 1:2], EPS, None, ALU.add).then_inc(out_eps_added, 1)
                pool.wait_ge(out_eps_added, tile + 1)
                pool.tensor_tensor(out_rstd[:], out_var_eps[:], minus_half[:, 0:1], ALU.pow).then_inc(out_rstd_ready, 1)

            def body(group, next_par, next_k):
                if reached(group, 1):
                    out_rstd_of(group * 2 - 1)
                if exists(group, 2):
                    rstd_of(group + 2)
                if exists(group, 1):
                    add_bias(group + 1, next_par, next_k)
                out_rstd_of(group * 2)

            rstd_of(0)
            rstd_of(1)
            add_bias(0, 0, 0)
            body(0, 1, 0)
            body(1, 0, 1)
            with pool.Fori(1, groups // 2 - 1) as k:
                body(k * 2, 1, k)
                body(k * 2 + 1, 0, k + 1)
            body(groups - 2, 1, groups // 2 - 1)
            body(groups - 1, 0, groups // 2)
            out_rstd_of(TILES - 1)

        @block.tensor
        def _(pe):
            def ring_slot(group, par, s):
                n = group * SLOTS + s
                if not (isinstance(n, int) and n < 2):
                    pe.wait_ge(ring_read, n - 1)
                return ring_ps[:, (par * SLOTS + s) % 2, :]

            def turn(group, par):
                pe.wait_ge(normed, group + 1)
                slot = ring_slot(group, par, 0)
                for h in range(2):
                    for t in range(2):
                        last = pe.transpose(slot[0:HALF, h * GT + t * PAIR:h * GT + (t + 1) * PAIR],
                                            xn[:, t, h * HALF:(h + 1) * HALF], ident[0:PAIR, 0:PAIR])
                last.then_inc(ring_done, 1)

            def project_in(group, par, blocks):
                for blk in blocks:
                    slot = ring_slot(group, par, 1 + blk)
                    if blk == 0:
                        pe.wait_ge(ring_read, group * SLOTS + 1)
                        pe.wait_ge(xnT_low_ready, group + 1)
                    parts = [(w, x, h) for w, x in ((qkv_w_low, xnT_high), (qkv_w_high, xnT_low),
                                                    (qkv_w_high, xnT_high)) for h in range(2)]
                    for n, (w, x, h) in enumerate(parts):
                        mm = pe.matmul(slot[:, 0:GT], w[:, h, blk, :], x[:, h, :], start=(n == 0),
                                       stop=(n == len(parts) - 1))
                    mm.then_inc(ring_done, 1)

            def scores(b, par, j):
                if reached(b, 1):
                    pe.wait_ge(shifted, b)
                for p in range(PAIRS):
                    r = slice(j * ROWS + p * PAIR, j * ROWS + (p + 1) * PAIR)
                    out = score_ps[:, p * PAIR:(p + 1) * PAIR]
                    pe.matmul(out, mask[:, 0, :], mask[:, 1, :], start=True, stop=False)
                    pe.matmul(out, big[:, par, 0, r], big[:, par, 1, r], start=False, stop=False)
                    mm = pe.matmul(out, small_at(par, 0)[:, r], small_at(par, 1)[:, r], start=False, stop=True)
                mm.then_inc(scored, 1)

            def turn_probs(b, j):
                pe.wait_ge(probs_ready, b + 1)
                if reached(b, 1):
                    pe.wait_ge(probsT_ready, b)
                for p in range(PAIRS):
                    last = pe.transpose(probsT_ps[:, p * PAIR:(p + 1) * PAIR], probs[:, j % 2, p, :],
                                        ident[0:PAIR, 0:PAIR])
                last.then_inc(probs_turned, 1)

            def turn_values(b, par, j, rnd):
                if reached(b, 1) or rnd:
                    pe.wait_ge(v_ready, b * 2 + rnd)
                for p in range(2):
                    at = j * ROWS + (2 * rnd + p) * PAIR
                    pe.transpose(v_ps[:, p, 0:BIG], big[:, par, 2, at:at + PAIR], ident[:])
                    half = slice(par * SMALL, (par + 1) * SMALL)
                    last = pe.transpose(v_ps[:, p, BIG:D], small[half, 2, at:at + PAIR], ident[half, half])
                last.then_inc(v_turned, 1)

            def mix_values(b):
                pe.wait_ge(probsT_ready, b + 1)
                pe.wait_ge(v_ready, b * 2 + 2)
                if reached(b, 1):
                    pe.wait_ge(outT_ready, b)
                for h, features in enumerate((slice(0, BIG), slice(BIG, D))):
                    for p in range(PAIRS):
                        mm = pe.matmul(out_ps[0:(BIG, SMALL)[h], h, p * PAIR:(p + 1) * PAIR], v_rows[:, p, features],
                                       probsT[:, p, :], start=True, stop=True)
                mm.then_inc(out_done, 1)

            def project_out(pair, pair_par):
                pe.wait_ge(outT_ready, pair * 2 + 2)
                if reached(pair, 1):
                    pe.wait_ge(h1_ready, pair)
                rows = outT[:, pair_par].rearrange("p (n c) -> p c n", c=HEADS)
                rest = outT_rest[:, pair_par].rearrange("p (n c) -> p c n", c=HEADS // 2)
                operands = [rows[:, c, :] for c in range(HEADS)] + [rest[:, c, :] for c in range(HEADS // 2)]
                for n, x in enumerate(operands):
                    mm = pe.matmul(proj_ps[:, 0:D], x, proj_w[:, n, :], start=(n == 0), stop=(n == len(operands) - 1))
                mm.then_inc(proj_done, 1)

            def body(group, par):
                for j in range(GB):
                    b = group * GB + j
                    last_par = par if j else 1 - par
                    last_j = (j - 1) % GB
                    if j == 0:
                        if exists(group, 1):
                            turn(group + 1, 1 - par)
                        pe.wait_ge(ring_read, (group + 1) * SLOTS)
                    scores(b, par, j)
                    if j % 2 == 1 and reached(b, 3):
                        project_out(group * 2 + (j // 2 - 1), (j // 2 + 1) % 2)
                    if reached(b, 1):
                        turn_probs(b - 1, last_j)
                    for part in range(3):
                        if exists(group, 1):
                            project_in(group + 1, 1 - par, range(j * BPS + 3 * part, j * BPS + 3 * part + 3))
                        if part < 2 and reached(b, 1):
                            turn_values(b - 1, last_par, last_j, part)
                    if reached(b, 1):
                        mix_values(b - 1)

            pe.wait_ge(const_loaded, 16 * 4)
            turn(0, 0)
            pe.wait_ge(mask_ready, 1)
            for part in range(PARTS):
                pe.wait_ge(qkv_w_ready, part + 1)
                project_in(0, 0, range(part * PART, (part + 1) * PART))
            pe.wait_ge(proj_w_loaded, 16)
            over_groups(pe, body)
            turn_probs(BATCH - 1, GB - 1)
            for rnd in range(2):
                turn_values(BATCH - 1, 1, GB - 1, rnd)
            mix_values(BATCH - 1)
            project_out(TILES - 1, 1)

        @block.scalar
        def _(act):
            def take_turned(group, par):
                act.wait_ge(ring_done, group * SLOTS + 1)
                act.activation(xnT_high[:].rearrange("p h n -> p (h n)"), ring_ps[0:HALF, (par * SLOTS) % 2, 0:2 * GT],
                               ACT.Copy).then_inc(ring_read, 1)

            def take_blocks(group, par, blocks):
                for blk in blocks:
                    kind, rest = divmod(blk, BLOCKS // 3)
                    cp, third = divmod(rest, 3)
                    slot = ring_ps[:, (par * SLOTS + 1 + blk) % 2, 0:GT]
                    wide = big[:, par, kind, :].rearrange("p (n c) -> p c n", c=HEADS)
                    narrow = small_at(par, kind).rearrange("p (n c) -> p c n", c=HEADS)
                    act.wait_ge(ring_done, group * SLOTS + (2 + blk))
                    if blk == 0 and reached(group, 2):
                        act.wait_ge(scored, (group - 1) * GB)
                    if blk == 2 * BLOCKS // 3 and reached(group, 2):
                        act.wait_ge(v_turned, (group - 1) * (2 * GB))
                    if third < 2:
                        act.activation(wide[:, 2 * cp + third, :], slot, ACT.Identity,
                                       bias=qkv_b[:, blk:blk + 1]).then_inc(ring_read, 1)
                    else:
                        act.activation(narrow[:, 2 * cp, :], slot[0:SMALL, :], ACT.Identity,
                                       bias=qkv_b[0:SMALL, blk:blk + 1])
                        act.activation(narrow[:, 2 * cp + 1, :], slot[SMALL:128, :], ACT.Identity,
                                       bias=qkv_b[SMALL:128, blk:blk + 1]).then_inc(ring_read, 1)

            def take_mixed(b, pair, j):
                act.wait_ge(out_done, b + 1)
                if j % 2 == 0 and reached(pair, 2):
                    act.wait_ge(proj_done, pair - 1)
                pair_par, batch = (j // 2) % 2, j % 2
                act.activation(outT[:, pair_par, batch * ROWS:(batch + 1) * ROWS], out_ps[:, 0, 0:ROWS], ACT.Copy)
                half = ROWS // 2
                for odd in range(2):
                    last = act.activation(outT_rest[odd * SMALL:(odd + 1) * SMALL, pair_par, batch * half:(batch + 1) * half],
                                          out_ps[0:SMALL, 1, odd:ROWS:2], ACT.Copy)
                last.then_inc(outT_ready, 1)

            def body(group, par):
                for j in range(GB):
                    b = group * GB + j
                    if j == 0 and exists(group, 1):
                        take_turned(group + 1, 1 - par)
                    first = 1 - j % 2
                    if exists(group, 1):
                        take_blocks(group + 1, 1 - par, range(j * BPS, j * BPS + first))
                    act.wait_ge(shifted, b + 1)
                    act.activation(probs[:, j % 2], probs[:, j % 2], ACT.Exp).then_inc(exp_done, 1)
                    if exists(group, 1):
                        take_blocks(group + 1, 1 - par, range(j * BPS + first, (j + 1) * BPS))
                    if reached(b, 1):
                        take_mixed(b - 1, group * 2 + ((j + 1) // 2 - 1), (j - 1) % GB)

            act.wait_ge(const_loaded, 16 * 4)
            take_turned(0, 0)
            for part in range(PARTS):
                act.wait_ge(qkv_w_loaded[part % STAGES], (part // STAGES + 1) * 16)
                act.activation(qkv_w_high[:, :, part * PART:(part + 1) * PART, :], staged(part), ACT.Copy
                               ).then_inc(qkv_w_high_ready, 1)
            take_blocks(0, 0, range(BLOCKS))
            over_groups(act, body)
            take_mixed(BATCH - 1, TILES - 1, GB - 1)

        @block.vector
        def _(dve):
            def statistics(group, par, count):
                dve.wait_ge(h_loaded[par], count * 16)
                for t in range(2):
                    s = dve.bn_stats(stats[:, t, :], h_in[:, par, t, :])
                s.then_inc(stats_done, 1)
                dve.wait_ge(stats_done, group + 1)
                if reached(group, 1):
                    dve.wait_ge(rstd_ready, group)
                dve.sem_inc(wait_carrier, 1)
                for t in range(2):
                    s = dve.bn_aggr(mv[:, t, :], stats[:, t, :])
                s.then_inc(var_ready, 1)

            def normalise(group, par):
                dve.wait_ge(rstd_ready, group + 1)
                if reached(group, 1):
                    dve.wait_ge(ring_done, (group - 1) * SLOTS + 1)
                for t in range(2):
                    s = dve.tensor_scalar(xn[:, t, :], h_in[:, par, t, :], mv[:, t, 0:1], rstd[:, t:t + 1],
                                          ALU.subtract, ALU.mult)
                s.then_inc(normed, 1)

            def take_turned(group, par):
                dve.wait_ge(ring_read, group * SLOTS + 1)
                dve.sem_inc(wait_carrier, 1)
                dve.tensor_tensor(xnT_low[:].rearrange("p h n -> p (h n)"), ring_ps[0:HALF, (par * SLOTS) % 2, 0:2 * GT],
                                  xnT_high[:].rearrange("p h n -> p (h n)"), ALU.subtract).then_inc(xnT_low_ready, 1)

            def add_residual(pair, par, t):
                dve.wait_ge(proj_done, pair + 1)
                dve.tensor_tensor(h1[:, par, t, :], h1[:, par, t, :], proj_ps[:, 0:D], ALU.add).then_inc(h1_ready, 1)

            def out_statistics(tile, par, t):
                dve.wait_ge(h1_ready, tile + 1)
                dve.sem_inc(wait_carrier, 1)
                dve.bn_stats(out_stats[:], h1[:, par, t, :]).then_inc(out_stats_done, 1)
                dve.wait_ge(out_stats_done, tile + 1)
                if reached(tile, 1):
                    dve.wait_ge(out_eps_added, tile)
                dve.sem_inc(wait_carrier, 1)
                dve.bn_aggr(out_mv[:], out_stats[:]).then_inc(out_var_ready, 1)

            def out_normalise(tile, par, t):
                dve.wait_ge(out_rstd_ready, tile + 1)
                dve.sem_inc(wait_carrier, 1)
                dve.tensor_scalar(rows[:, bass.ds(tile, 1), 0:D].rearrange("p t d -> p (t d)"), h1[:, par, t, :],
                                  out_mv[:, 0:1], out_rstd[:, 0:1], ALU.subtract, ALU.mult).then_inc(out_normed, 1)

            def wide(small_tile):
                return small_tile[:].unsqueeze(2).to_broadcast([PAIR, PAIRS, PAIR])

            def take_turned_probs(b):
                dve.wait_ge(probs_turned, b + 1)
                if reached(b, 1):
                    dve.wait_ge(out_done, b)
                dve.tensor_copy(probsT[:], probsT_ps[:, 0:ROWS].rearrange("q (p k) -> q p k", k=PAIR)
                                ).then_inc(probsT_ready, 1)

            def take_values(b, rnd):
                dve.wait_ge(v_turned, b * 2 + rnd + 1)
                dve.tensor_copy(v_rows[:, 2 * rnd:2 * rnd + 2, :], v_ps[:, :, 0:D]).then_inc(v_ready, 1)

            def body(group, par, k):
                for j in range(GB):
                    b = group * GB + j
                    if j == 0 and exists(group, 1):
                        take_turned(group + 1, 1 - par)
                    p = probs[:, j % 2]
                    score = score_ps[:, 0:ROWS].rearrange("q (p k) -> q p k", k=PAIR)
                    dve.wait_ge(scored, b + 1)
                    dve.tensor_reduce(row_max[:], score, AX_X, ALU.max).then_inc(max_done, 1)
                    dve.wait_ge(max_done, b + 1)
                    if reached(b, 2):
                        dve.wait_ge(probs_turned, b - 1)
                    dve.tensor_tensor(p, score, wide(row_max), ALU.subtract).then_inc(shifted, 1)
                    if j % 2 == 1 and reached(b, 3):
                        if j == 1:
                            dve.wait_ge(h_biased, group)
                            add_residual(group * 2 - 1, 1 - par, 1)
                        else:
                            dve.wait_ge(h_biased, group + 1)
                            add_residual(group * 2, par, 0)
                    if reached(b, 1):
                        take_turned_probs(b - 1)
                    tile_of = (group * 2 - 1, 1 - par, 1) if j == 1 else (group * 2, par, 0)
                    if j % 2 == 1 and reached(b, 3):
                        out_statistics(*tile_of)
                    dve.wait_ge(exp_done, b + 1)
                    dve.tensor_reduce(row_sum[:], p, AX_X, ALU.add).then_inc(sum_step, 1)
                    dve.wait_ge(sum_step, b * 3 + 1)
                    dve.tensor_scalar(sum_scaled[:], row_sum[:], SCALING, None, ALU.mult).then_inc(sum_step, 1)
                    dve.wait_ge(sum_step, b * 3 + 2)
                    dve.reciprocal(inv_sum[:], sum_scaled[:]).then_inc(sum_step, 1)
                    dve.wait_ge(sum_step, b * 3 + 3)
                    dve.tensor_tensor(p, p, wide(inv_sum), ALU.mult).then_inc(probs_ready, 1)
                    if reached(b, 1):
                        take_values(b - 1, 0)
                        take_values(b - 1, 1)
                    if j % 2 == 1 and reached(b, 3):
                        out_normalise(*tile_of)
                    if j == 2 and exists(group, 2):
                        statistics(group + 2, par, k + 2)
                    if j == 3 and exists(group, 2):
                        normalise(group + 2, par)

            dve.wait_ge(const_loaded, 16 * 4)
            dve.tensor_copy(mask[:], mask_f[:]).then_inc(mask_ready, 1)
            statistics(0, 0, 1)
            normalise(0, 0)
            statistics(1, 1, 1)
            take_turned(0, 0)
            for part in range(PARTS):
                dve.wait_ge(qkv_w_high_ready, part + 1)
                high = qkv_w_high[:, :, part * PART:(part + 1) * PART, :]
                dve.tensor_tensor(qkv_w_low[:, :, part * PART:(part + 1) * PART, :], staged(part), high, ALU.subtract
                                  ).then_inc(qkv_w_ready, 1)
            normalise(1, 1)
            body(0, 0, 0)
            body(1, 1, 0)
            with dve.Fori(1, groups // 2 - 1) as k:
                body(k * 2, 0, k)
                body(k * 2 + 1, 1, k)
            body(groups - 2, 0, groups // 2 - 1)
            body(groups - 1, 1, groups // 2 - 1)
            take_turned_probs(BATCH - 1)
            take_values(BATCH - 1, 0)
            take_values(BATCH - 1, 1)
            dve.wait_ge(h_biased, groups)
            add_residual(TILES - 1, 1, 1)
            out_statistics(TILES - 1, 1, 1)
            out_normalise(TILES - 1, 1, 1)


IMG = 84
GRID = 7
REG = IMG // GRID
C0, C1, C2 = 3, 12, 48


def image_stage(nc, io, wait_carrier):
    B8, G4 = 8, 4
    CH = B8 * C1
    XW = IMG + 2
    XP = REG * XW
    PITCH = REG + 1
    GP = PITCH * PITCH
    LEAD = PITCH + 1
    RP = LEAD + G4 * GP + PITCH + 1
    WROWS = G4 * PITCH - 1
    RPX = REG * REG
    PIECES = 2 * G4
    PROWS = REG // 2
    OY, OX = REG // 4, 20
    TAPS = 16
    RUN = G4 * OY * OX
    ON_PE = GRID - 1
    ON_DVE = GRID - 1
    THIRDS = [(0, 1), (2, 3), (4, 5)]
    DVE_ADDS = 4
    units = 2 * GRID
    LAST = [(0, 0), (0, 1), (1, 0), (1, 1)]
    P_PW, P_SC = 0, GRID * CH
    P_DW = 2 * GRID * CH
    P_SDW = P_DW + 9 * GRID
    P_BDW, P_BPW, P_LEN = P_SDW + GRID, P_SDW + 2 * GRID, P_SDW + 3 * GRID

    with ExitStack() as ctx:
        def sb(name, shape, dt=F32):
            return ctx.enter_context(nc.sbuf_tensor("img_sb_" + name, shape, dt))

        def ps(name, shape):
            return ctx.enter_context(nc.psum_tensor("img_ps_" + name, shape, F32))

        def sem(name):
            return ctx.enter_context(nc.semaphore("img_" + name))

        ident = sb("ident", [128, 128])
        w0 = sb("w0", [B8 * C0 * 3, 3, CH])
        sb0 = sb("sb0", [CH, 2])
        w1 = sb("w1", [CH, 2, 64])
        sb1 = sb("sb1", [128, 2])
        w2 = sb("w2", [128, 4, 128])
        sb2 = sb("sb2", [128, 2])
        w3 = sb("w3", [128, 4, D])
        sb3 = sb("sb3", [128, 2, D])
        x = sb("x", [128, 2, G4, XP])
        y0_all = sb("y0", [128, 2, GRID, RP])
        y0 = y0_all[0:CH]
        par = sb("par", [CH, 2, P_LEN])
        diag = sb("diag", [CH, 2, 9, CH])
        acc = sb("acc", [CH, 2, G4 * GP])
        y1 = sb("y1", [CH, 2, G4 * RPX])
        y1_pe = sb("y1_pe", [CH, G4 * RPX])
        y2 = sb("y2", [CH, 2, G4 * RPX])
        taps = sb("taps", [128, TAPS * RUN])
        cols = sb("cols", [CH, 2, B8, RUN])
        z1 = sb("z1", [128, 4, 2 * G4, GRID * OY * OX])
        scaled = sb("scaled", [4 * IMG_LEN, 4, D])
        tok = y0_all[0:4 * IMG_LEN, 0].rearrange("p r n -> p (r n)")[:, 0:16 * D].rearrange("p (n d) -> p n d", d=D)
        c0_ps = ps("c0_ps", [128, 2, 512])
        pw_ps = ps("pw_ps", [128, 2, G4, 256])
        c1_ps = ps("c1_ps", [128, 2, 512])
        z2 = x[:, 0].rearrange("p g n -> p (g n)")[:, 0:4 * 32 * IMG_LEN].rearrange("p (t n) -> p t n", t=4)

        const_loaded = sem("const_loaded")
        x_loaded = [sem("x_loaded_half0"), sem("x_loaded_half1")]
        par_loaded = [sem("par_loaded_even"), sem("par_loaded_odd")]
        pads_set = sem("pads_set")
        pw_scaled = sem("pw_scaled")
        conv0_done = sem("conv0_done")
        y0_ready = sem("y0_ready")
        dw_tap = sem("dw_tap")
        dw_done = sem("dw_done")
        diag_ready = sem("diag_ready")
        pe_dw_done = sem("pe_dw_done")
        y1_ready = sem("y1_ready")
        y1_pe_ready = sem("y1_pe_ready")
        pw_done = sem("pw_done")
        y2_ready = sem("y2_ready")
        taps_ready = sem("taps_ready")
        taps_stored = sem("taps_stored")
        cols_loaded = sem("cols_loaded")
        conv1_done = sem("conv1_done")
        z1_ready = sem("z1_ready")
        conv2_done = sem("conv2_done")
        z2_ready = sem("z2_ready")
        conv3_done = sem("conv3_done")
        tok_scaled = sem("tok_scaled")
        tok_ready = sem("tok_ready")
        h_stored = sem("h_stored")

        def over_units(eng, body):
            for hf in range(2):
                body(0, 0, 0, hf)
            with eng.Fori(0, 2) as k:
                for hf in range(2):
                    body(k * 2 + 1, k, 1, hf)
                for hf in range(2):
                    body(k * 2 + 2, k + 1, 0, hf)
            for s in (GRID - 2, GRID - 1):
                for hf in range(2):
                    body(s, s // 2, s % 2, hf)

        def is_last(s):
            return isinstance(s, int) and s == GRID - 1

        def has_next(s, hf):
            return not (is_last(s) and hf == 1)

        def window(half, gx, ky, kx):
            at = LEAD + (ky - 1) * PITCH + (kx - 1)
            return y0[:, half, gx, at:at + WROWS * PITCH].rearrange("p (r c) -> p r c", c=PITCH)[:, :, 0:REG]

        def pixels(tile):
            return tile.rearrange("p (g r c) -> p g r c", r=PITCH, c=PITCH)[:, :, 0:REG, 0:REG]

        def packed(rp, q):
            return pw_ps[0:CH, rp, 2 * q:2 * q + 2, :].rearrange("p g n -> p (g n)")[:, 0:2 * RPX]

        def last_ps(n):
            return pw_ps[0:4 * IMG_LEN, n % 4 // 2, n % 2 * 2, 0:D]

        block = ctx.enter_context(nc.Block())

        @block.sync
        def _(sp):
            def load_x(s, half):
                for dy in range(3):
                    src = io["img_x"][:, half * G4:(half + 1) * G4, bass.ds((s * REG + dy) * XW, XP)]
                    sp.dma_start(x[dy * B8 * C0:(dy + 1) * B8 * C0, half], src).then_inc(x_loaded[half], 16)

            def load_par(s, parity):
                sp.dma_start(par[:, parity], io["img_par"][s]).then_inc(par_loaded[parity], 16)

            def regroup(u, half):
                sp.wait_ge(taps_ready, (u + 1) * GRID)
                sp.dma_start(io["img_taps"][half], taps[0:CH, :]).then_inc(taps_stored, 16)
                sp.wait_ge(taps_stored, (u + 1) * 16)
                sp.sem_inc(wait_carrier, 1)
                if reached(u, 1):
                    sp.wait_ge(conv1_done, u)
                src = io["img_taps"][half].rearrange("(b k c) (t n) -> k c t b n", k=2, c=C1 // 2, n=RUN)
                for k in range(2):
                    sp.dma_start(cols[:, k], src[k].rearrange("c t b n -> (c t) b n")).then_inc(cols_loaded, 16)

            load_x(0, 0)
            consts = ((ident, "ident"), (w0, "img_w0"), (sb0, "img_sb0"), (w1, "img_w1"), (sb1, "img_sb1"), (w2, "img_w2"),
                      (sb2, "img_sb2"), (w3, "img_w3"), (sb3, "img_sb3"))
            for dst, name in consts:
                sp.dma_start(dst[:], io[name]).then_inc(const_loaded, 16)
            load_par(0, 0)
            load_x(0, 1)

            def body(s, sc, parity, hf):
                u = s * 2 + hf
                if not is_last(s):
                    sp.wait_ge(conv0_done, (u + 1) * PIECES)
                    sp.sem_inc(wait_carrier, 1)
                    load_x(s + 1, hf)
                    if hf == 0:
                        if reached(s, 1):
                            sp.wait_ge(taps_ready, u * GRID)
                            sp.sem_inc(wait_carrier, 1)
                        load_par(s + 1, 1 - parity)
                if reached(u, 1):
                    regroup(u - 1, 1 - hf)

            over_units(sp, body)
            regroup(units - 1, 1)

            rows = io["h"].rearrange("(a g b t) d -> a g t b d", a=2, g=G4, t=SEQ)
            for n, (a, h) in enumerate(LAST):
                sp.wait_ge(tok_ready, (n + 1) * 4)
                for g in range(G4):
                    sp.dma_start(rows[a, g, 0:IMG_LEN, h * 4:(h + 1) * 4, :],
                                 tok[g * IMG_LEN:(g + 1) * IMG_LEN, n * 4:(n + 1) * 4, :]).then_inc(h_stored, 16)
            sp.wait_ge(h_stored, 16 * G4 * len(LAST))

        @block.gpsimd
        def _(pool):
            def scale_pointwise(s, sc, parity, hf):
                if hf == 0:
                    pool.wait_ge(par_loaded[parity], (sc + 1) * 16)
                    pool.tensor_tensor(par[:, parity, P_PW:P_PW + GRID * CH], par[:, parity, P_PW:P_PW + GRID * CH],
                                       par[:, parity, P_SC:P_SC + GRID * CH], ALU.mult).then_inc(pw_scaled, 1)

            over_units(pool, scale_pointwise)

        @block.tensor
        def _(pe):
            def conv0(u, half, x_count, pieces):
                for piece in pieces:
                    g, part = divmod(piece, 2)
                    if piece == 0:
                        pe.wait_ge(x_loaded[half], x_count)
                    if piece >= 2 or reached(u, 1):
                        pe.wait_ge(y0_ready, u * PIECES + (piece - 1))
                    rows = x[0:B8 * C0 * 3, half, g, :].rearrange("p (r c) -> p r c", c=XW)[:, part * PROWS:(part + 1) * PROWS, :]
                    out = c0_ps[0:CH, piece % 2, 0:PROWS * IMG]
                    for dx in range(3):
                        mm = pe.matmul(out, w0[:, dx, :], rows[:, :, dx:dx + IMG], start=(dx == 0), stop=(dx == 2))
                    mm.then_inc(conv0_done, 1)

            def pointwise(u, s, hf, parity, gx):
                r, rp = u * GRID + gx, (hf + gx) % 2
                if hf == 0 and gx == 0:
                    pe.wait_ge(pw_scaled, s + 1)
                if gx == ON_PE:
                    pe.wait_ge(y1_pe_ready, u + 1)
                    src = y1_pe[:]
                else:
                    pe.wait_ge(y1_ready, u * ON_DVE + (gx + 1))
                    src = y1[:, gx % 2, :]
                if 2 <= gx < 2 + DVE_ADDS:
                    pe.wait_ge(y2_ready, u * DVE_ADDS + (gx - 1))
                elif reached(r, 2):
                    pe.wait_ge(taps_ready, r - 1)
                for q in range(2):
                    w = par[:, parity, P_PW + gx * CH:P_PW + (gx + 1) * CH]
                    pixels_q = src[:, 2 * q * RPX:(2 * q + 2) * RPX]
                    if gx < DVE_ADDS:
                        mm = pe.matmul(pw_ps[0:CH, rp, 2 * q:2 * q + 2, 0:RPX], w,
                                       pixels_q.rearrange("p (g n) -> p g n", n=RPX), start=True, stop=True)
                    else:
                        out = packed(rp, q)
                        at = LEAD + 2 * q * GP
                        pe.matmul(out, w, pixels_q, start=True, stop=False)
                        mm = pe.matmul(out, ident[0:CH, 0:CH], pixels(y0[:, hf, gx, at:at + 2 * GP]),
                                       start=False, stop=True)
                mm.then_inc(pw_done, 1)

            def depthwise(u, s, hf, parity):
                if hf == 0:
                    pe.wait_ge(diag_ready, (s + 1) * 9)
                pe.wait_ge(y0_ready, (u + 1) * PIECES)
                if reached(u, 2):
                    pe.wait_ge(z1_ready, u - 1)
                for q in range(2):
                    for t in range(9):
                        at = LEAD + 2 * q * GP + (t // 3 - 1) * PITCH + (t % 3 - 1)
                        mm = pe.matmul(c1_ps[0:CH, q, 0:2 * RPX], diag[:, parity, t, :],
                                       pixels(y0[:, hf, ON_PE, at:at + 2 * GP]), start=(t == 0), stop=(t == 8))
                mm.then_inc(pe_dw_done, 1)

            def conv1(u):
                pe.wait_ge(cols_loaded, (u + 1) * 32)
                if not (isinstance(u, int) and u == units - 1):
                    pe.wait_ge(y1_pe_ready, u + 2)
                if reached(u, 1):
                    pe.wait_ge(z1_ready, u)
                for m in range(4):
                    for k in range(2):
                        mm = pe.matmul(c1_ps[64 * (m // 2):64 * (m // 2) + 64, m % 2, 0:2 * RUN], w1[:, k, :],
                                       cols[:, k, 2 * m:2 * m + 2, :], start=(k == 0), stop=(k == 1))
                mm.then_inc(conv1_done, 1)

            pe.wait_ge(const_loaded, 16 * 9)
            conv0(0, 0, 48, range(PIECES))

            def body(s, sc, parity, hf):
                u = s * 2 + hf
                def ahead(*pieces):
                    if has_next(s, hf):
                        conv0(u + 1, 1 - hf, (s + (1 + hf)) * 48, pieces)

                ahead(0)
                if reached(u, 1):
                    pointwise(u - 1, s if hf else s - 1, 1 - hf, parity if hf else 1 - parity, ON_PE)
                depthwise(u, s, hf, parity)
                for gx in THIRDS[0]:
                    pointwise(u, s, hf, parity, gx)
                ahead(1, 2, 3, 4, 5)
                for gx in THIRDS[1]:
                    pointwise(u, s, hf, parity, gx)
                ahead(6, 7)
                if reached(u, 1):
                    conv1(u - 1)
                for gx in THIRDS[2]:
                    pointwise(u, s, hf, parity, gx)

            over_units(pe, body)
            pointwise(units - 1, GRID - 1, 1, (GRID - 1) % 2, ON_PE)

            z = z1[:].rearrange("p b g (y x) -> p (b g) y x", x=OX)

            def conv2(a):
                pe.wait_ge(z1_ready, units - 1 + a)
                if a == 0:
                    pe.wait_ge(y0_ready, units * PIECES)
                for i in range(4):
                    if i >= 2 or a:
                        pe.wait_ge(z2_ready, 4 * a + i - 1)
                    at = 8 * i + 4 * a
                    for t in range(4):
                        mm = pe.matmul(c0_ps[:, i % 2, 0:400], w2[:, t, :],
                                       z[:, at:at + 4, t // 2:t // 2 + 19:2, t % 2:t % 2 + 19:2],
                                       start=(t == 0), stop=(t == 3))
                    mm.then_inc(conv2_done, 1)

            def conv3(a):
                if a == 0:
                    pe.wait_ge(taps_ready, units * GRID)
                for n in range(8 * a, 8 * a + 8):
                    h, i = n % 8 // 4, n % 4
                    if h == 0:
                        pe.wait_ge(z2_ready, 4 * a + i + 1)
                    if n >= 4:
                        pe.wait_ge(tok_scaled, n - 3)
                    at = (8 * i + 4 * a) * IMG_LEN
                    for t in range(4):
                        mm = pe.matmul(last_ps(n), z2[64 * h:64 * h + 64, t, at:at + 4 * IMG_LEN],
                                       w3[64 * h:64 * h + 64, t, :], start=(t == 0), stop=(t == 3))
                    mm.then_inc(conv3_done, 1)

            conv2(0)
            conv3(0)
            conv1(units - 1)
            conv2(1)
            conv3(1)

        @block.scalar
        def _(act):
            def take_conv0(u, half, pieces):
                for piece in pieces:
                    g, part = divmod(piece, 2)
                    act.wait_ge(conv0_done, u * PIECES + (piece + 1))
                    if piece == 0 and reached(u, 2):
                        act.wait_ge(y2_ready, (u - 1) * DVE_ADDS)
                        act.wait_ge(pw_done, (u - 1) * GRID)
                    at = LEAD + g * GP + part * PROWS * PITCH
                    dst = y0[:, half, :, at:at + PROWS * PITCH].rearrange("p r (y c) -> p y r c", c=PITCH)[:, :, :, 0:REG]
                    src = c0_ps[0:CH, piece % 2, 0:PROWS * IMG].rearrange("p (y r c) -> p y r c", r=GRID, c=REG)
                    act.activation(dst, src, ACT.Gelu, scale=sb0[:, 0:1], bias=sb0[:, 1:2]).then_inc(y0_ready, 1)

            def make_diagonals(s, parity):
                if reached(s, 2):
                    act.wait_ge(pe_dw_done, (s - 1) * 2)
                    act.sem_inc(wait_carrier, 1)
                for t in range(9):
                    at = P_DW + ON_PE * 9 + t
                    act.activation(diag[:, parity, t, :], ident[0:CH, 0:CH], ACT.Identity,
                                   scale=par[:, parity, at:at + 1]).then_inc(diag_ready, 1)

            def take_depthwise(u, hf, parity, gx):
                if gx == ON_PE:
                    act.wait_ge(pe_dw_done, u + 1)
                    if reached(u, 1):
                        act.wait_ge(pw_done, u * GRID)
                    src = c1_ps[0:CH, :, 0:2 * RPX]
                    dst = y1_pe[:].rearrange("p (q n) -> p q n", q=2)
                else:
                    act.wait_ge(dw_done, u * ON_DVE + (gx + 1))
                    if gx >= 2:
                        act.wait_ge(pw_done, u * GRID + (gx - 1))
                    elif reached(u, 1):
                        act.wait_ge(pw_done, u * GRID + (gx - 2))
                    src = pixels(acc[:, gx % 2, :])
                    dst = y1[:, gx % 2, :].rearrange("p (g y c) -> p g y c", y=REG, c=REG)
                act.activation(dst, src, ACT.Gelu,
                               scale=par[:, parity, P_SDW + gx:P_SDW + gx + 1],
                               bias=par[:, parity, P_BDW + gx:P_BDW + gx + 1]
                               ).then_inc(y1_pe_ready if gx == ON_PE else y1_ready, 1)

            def take_region(u, hf, parity, gx):
                r, rp = u * GRID + gx, (hf + gx) % 2
                n = min(OY, OX - gx * OY)
                if gx < DVE_ADDS:
                    act.wait_ge(y2_ready, u * DVE_ADDS + (gx + 1))
                    sources = [y2[:, gx % 2, :]]
                else:
                    act.wait_ge(pw_done, r + 1)
                    sources = [packed(rp, 0), packed(rp, 1)]
                if gx == 0 and reached(u, 1):
                    act.wait_ge(taps_stored, u * 16)
                dst = taps[0:CH, :].rearrange("p (d e a x) -> p d a x e", d=4, e=4, x=OX)
                rows = G4 * OY // len(sources)
                for i, source in enumerate(sources):
                    src = source.rearrange("p (a d b e) -> p d a b e", d=4, b=OY, e=4)
                    for dy in range(4):
                        last = act.activation(dst[:, dy, i * rows:(i + 1) * rows, gx * OY:gx * OY + n, :],
                                              src[:, dy, :, 0:n, :], ACT.Gelu,
                                              bias=par[:, parity, P_BPW + gx:P_BPW + gx + 1])
                last.then_inc(taps_ready, 1)

            def take_conv1(u, s, hf):
                act.wait_ge(conv1_done, u + 1)
                act.sem_inc(wait_carrier, 1)
                for m in range(2):
                    last = act.activation(z1[:, 2 * m:2 * m + 2, hf * G4:(hf + 1) * G4, bass.ds(s * (OY * OX), OY * OX)],
                                          c1_ps[:, m, 0:2 * RUN].rearrange("p (b g n) -> p b g n", b=2, g=G4), ACT.Gelu,
                                          scale=sb1[:, 0:1], bias=sb1[:, 1:2])
                last.then_inc(z1_ready, 1)

            act.wait_ge(const_loaded, 16 * 9)
            act.wait_ge(pads_set, 1)
            take_conv0(0, 0, range(PIECES))

            def body(s, sc, parity, hf):
                u = s * 2 + hf
                if hf == 0:
                    act.wait_ge(par_loaded[parity], (sc + 1) * 16)
                    make_diagonals(s, parity)
                before = (u - 1, 1 - hf, parity if hf else 1 - parity)

                def ahead(*pieces):
                    if has_next(s, hf):
                        take_conv0(u + 1, 1 - hf, pieces)

                ahead(0)
                if reached(u, 1):
                    take_region(*before, ON_PE)
                for gx in THIRDS[0]:
                    take_depthwise(u, hf, parity, gx)
                take_depthwise(u, hf, parity, ON_PE)
                ahead(1, 2, 3)
                for gx in THIRDS[1]:
                    take_depthwise(u, hf, parity, gx)
                ahead(4, 5)
                for gx in THIRDS[0]:
                    take_region(u, hf, parity, gx)
                ahead(6, 7)
                for gx in THIRDS[2]:
                    take_depthwise(u, hf, parity, gx)
                if reached(u, 1):
                    take_conv1(u - 1, s if hf else s - 1, 1 - hf)
                for gx in THIRDS[1] + THIRDS[2]:
                    take_region(u, hf, parity, gx)

            over_units(act, body)
            take_region(units - 1, 1, (GRID - 1) % 2, ON_PE)

            def take_conv2(a):
                if a == 0:
                    act.wait_ge(conv0_done, units * PIECES)
                for i in range(4):
                    act.wait_ge(conv2_done, 4 * a + i + 1)
                    src = c0_ps[:, i % 2, 0:400].rearrange("p (a d x e) -> p d a x e", d=2, x=5, e=2)
                    at = (8 * i + 4 * a) * IMG_LEN
                    dst = z2[:, :, at:at + 4 * IMG_LEN].rearrange("p (d e) (a x) -> p d a x e", d=2, x=5)
                    for dy in range(2):
                        last = act.activation(dst[:, dy], src[:, dy], ACT.Gelu, scale=sb2[:, 0:1], bias=sb2[:, 1:2])
                    last.then_inc(z2_ready, 1)

            take_conv2(0)
            take_conv1(units - 1, GRID - 1, 1)
            take_conv2(1)

        @block.vector
        def _(dve):
            dve.memset(y0[:], 0.0).then_inc(pads_set, 1)

            def depthwise(u, hf, parity, regions):
                n = len(regions)
                first = u * (8 * ON_DVE) + 8 * regions[0]
                for k, (ky, kx) in enumerate([(1, 1)] + [(i // 3, i % 3) for i in range(9) if i != 4]):
                    for a, gx in enumerate(regions):
                        out = acc[:, gx % 2, 0:WROWS * PITCH].rearrange("p (r c) -> p r c", c=PITCH)[:, :, 0:REG]
                        at = P_DW + gx * 9 + ky * 3 + kx
                        w = par[:, parity, at:at + 1]
                        if k == 0:
                            if gx >= 2 or reached(u, 1):
                                dve.wait_ge(y1_ready, u * ON_DVE + (gx - 1))
                            s = dve.tensor_scalar(out, window(hf, gx, ky, kx), w, None, ALU.mult)
                        else:
                            dve.wait_ge(dw_tap, first + (n * (k - 1) + a + 1))
                            s = dve.scalar_tensor_tensor(out, window(hf, gx, ky, kx), w, out, ALU.mult, ALU.add)
                        s.then_inc(dw_tap if k < 8 else dw_done, 1)

            def add_input(u, hf, gx):
                r, rp = u * GRID + gx, (hf + gx) % 2
                dve.wait_ge(pw_done, r + 1)
                if gx >= 2:
                    dve.wait_ge(taps_ready, r - 1)
                elif reached(u, 1):
                    dve.wait_ge(taps_ready, (u - 1) * GRID + (gx + 3))
                dve.tensor_tensor(y2[:, gx % 2, :].rearrange("p (g y c) -> p g y c", y=REG, c=REG),
                                  pw_ps[0:CH, rp, :, 0:RPX].rearrange("p g (y c) -> p g y c", c=REG),
                                  pixels(y0[:, hf, gx, LEAD:LEAD + G4 * GP]), ALU.add).then_inc(y2_ready, 1)

            def body(s, sc, parity, hf):
                u = s * 2 + hf
                if hf == 0:
                    dve.wait_ge(par_loaded[parity], (sc + 1) * 16)
                dve.wait_ge(y0_ready, (u + 1) * PIECES)
                depthwise(u, hf, parity, THIRDS[0])
                depthwise(u, hf, parity, THIRDS[1])
                for gx in THIRDS[0]:
                    add_input(u, hf, gx)
                depthwise(u, hf, parity, THIRDS[2])
                for gx in THIRDS[1]:
                    add_input(u, hf, gx)

            over_units(dve, body)

            for n in range(16):
                dve.wait_ge(conv3_done, n + 1)
                if n >= 4:
                    dve.wait_ge(tok_ready, n - 3)
                rows = slice(0, 4 * IMG_LEN)
                dve.tensor_tensor(scaled[:, n % 4, :], last_ps(n), sb3[rows, 0, :], ALU.mult).then_inc(tok_scaled, 1)
                dve.wait_ge(tok_scaled, n + 1)
                dve.tensor_tensor(tok[:, n, :], scaled[:, n % 4, :], sb3[rows, 1, :], ALU.add).then_inc(tok_ready, 1)




EXPERTS = 8
F = 768
ROUTE_TILES = 4
ROW = D + 2
SLOT = 128
SLOTS = (2 * TOKENS + EXPERTS * (SLOT - 1)) // SLOT
REGION = TOKENS + SLOT
SPARE = EXPERTS * REGION


def routing_stage(nc, io, best, slots):
    BT = ROUTE_TILES
    NB = TILES // BT
    BE = BT * EXPERTS

    with ExitStack() as ctx:
        def sb(name, shape, dt=F32):
            return ctx.enter_context(nc.sbuf_tensor("rt_sb_" + name, shape, dt))

        def ps(name, shape):
            return ctx.enter_context(nc.psum_tensor("rt_ps_" + name, shape, F32))

        def sem(name):
            return ctx.enter_context(nc.semaphore("rt_" + name))

        ident = sb("ident", [128, 128])
        router_w = sb("router_w", [HALF, 2, EXPERTS])
        earlier = sb("earlier", [PAIR, 2, PAIR])
        token_no = sb("token_no", [PAIR, TILES], I32)
        pad_no = sb("pad_no", [128, 1], I32)
        region_at = sb("region_at", [PAIR, BT, EXPERTS])
        slot_no = sb("slot_no", [1, SLOTS])
        number = sb("number", [PAIR, EXPERTS])
        zeros = sb("zeros", [128, D])
        pad_rows = sb("pad_rows", [128, ROW])
        second = sb("second", [PAIR, TILES, ROW])
        rows = (best, second)
        xnT = sb("xnT", [HALF, 2, 2, PAIR])
        logits = sb("logits", [PAIR, TILES, EXPERTS])
        top = sb("top", [PAIR, TILES, 8])
        top_at = sb("top_at", [PAIR, TILES, 8], U32)
        top_atf = sb("top_atf", [PAIR, TILES, 8])
        gap = sb("gap", [PAIR, TILES])
        ratio = sb("ratio", [PAIR, TILES])
        one_plus = sb("one_plus", [PAIR, TILES])
        picked = sb("picked", [PAIR, 2, BT, EXPERTS])
        either = sb("either", [PAIR, TILES, EXPERTS])
        before = sb("before", [PAIR, TILES + 1, EXPERTS])
        place = sb("place", [PAIR, BT, EXPERTS])
        own_place = sb("own_place", [PAIR, 2, BT, EXPERTS])
        dest_f = sb("dest_f", [PAIR, 2, BT])
        dest = sb("dest", [PAIR, 2, TILES], U32)
        counts = sb("counts", [1, EXPERTS])
        pad_at_f = sb("pad_at_f", [1, EXPERTS])
        pad_at = sb("pad_at", [1, EXPERTS], I32)
        counts_i = sb("counts_i", [1, EXPERTS], I32)
        blocks_i = sb("blocks_i", [1, EXPERTS], I32)
        ends = sb("ends", [1, EXPERTS])
        passed = sb("passed", [1, SLOTS, EXPERTS])
        passed_end = sb("passed_end", [1, SLOTS, EXPERTS])
        slot_expert = sb("slot_expert", [1, SLOTS])
        slot_begin = sb("slot_begin", [1, SLOTS])
        in_expert = sb("in_expert", [1, SLOTS])
        region_row = sb("region_row", [1, SLOTS])
        slot_row = sb("slot_row", [1, SLOTS])
        table = sb("table", [1, 3, SLOTS])
        turned_ps = ps("turned_ps", [HALF, 2, 512])
        logits_ps = ps("logits_ps", [PAIR, 2, 512])
        place_ps = ps("place_ps", [PAIR, 2, 512])
        count_ps = ps("count_ps", [PAIR, 512])

        const_loaded = sem("const_loaded")
        consts_set = sem("consts_set")
        zeros_stored = sem("zeros_stored")
        pads_stored = sem("pads_stored")
        pads_set = sem("pads_set")
        numbers_set = sem("numbers_set")
        doubled = sem("doubled")
        turned = sem("turned")
        xnT_ready = sem("xnT_ready")
        logits_done = sem("logits_done")
        logits_ready = sem("logits_ready")
        gap_ready = sem("gap_ready")
        ratio_ready = sem("ratio_ready")
        step_done = sem("step_done")
        either_ready = sem("either_ready")
        before_ready = sem("before_ready")
        placed = sem("placed")
        place_read = sem("place_read")
        shares_set = sem("shares_set")
        dest_ready = sem("dest_ready")
        counted = sem("counted")
        pad_at_ready = sem("pad_at_ready")
        scattered = sem("scattered")

        block = ctx.enter_context(nc.Block())

        @block.sync
        def _(sp):
            for dst, name in ((ident, "ident"), (router_w, "router_w"), (earlier, "earlier"), (token_no, "token_no"),
                              (pad_no, "pad_no"), (region_at, "region_at"), (slot_no, "slot_no")):
                sp.dma_start(dst[:], io[name]).then_inc(const_loaded, 16)
            sp.wait_ge(consts_set, 3)
            sp.dma_start(io["out"][TOKENS:TOKENS + SLOT], zeros[:]).then_inc(zeros_stored, 16)
            sp.wait_ge(pads_set, 1)
            sp.dma_start(io["dispatch"][SPARE:SPARE + SLOT], pad_rows[:]).then_inc(pads_stored, 16)
            sp.wait_ge(pad_at_ready, 1)
            for e in range(EXPERTS):
                at = sp.value_load(pad_at[0:1, e:e + 1], min_val=e * REGION, max_val=e * REGION + TOKENS)
                sp.dma_start(io["dispatch"][bass.ds(at, SLOT), :], pad_rows[:]).then_inc(pads_stored, 16)
            sp.wait_ge(zeros_stored, 16)
            sp.wait_ge(pads_stored, 16 * (EXPERTS + 1))

        @block.gpsimd
        def _(pool):
            pool.iota(number[:], pattern=[[1, EXPERTS]], base=0, channel_multiplier=0,
                      allow_small_or_imprecise_dtypes=True).then_inc(consts_set, 1)
            pool.memset(zeros[:], 0.0).then_inc(consts_set, 1)
            pool.memset(pad_rows[:], 0.0).then_inc(consts_set, 1)
            pool.wait_ge(consts_set, 3)

            def dispatch(b):
                pool.wait_ge(numbers_set, 1)
                pool.wait_ge(shares_set, b + 1)
                pool.wait_ge(dest_ready, b + 1)
                pool.wait_ge(doubled, (b + 1) * BT)
                for t in range(b * BT, (b + 1) * BT):
                    for k in range(2):
                        pool.indirect_dma_start(io["dispatch"], bass.IndirectOffsetOnAxis(dest[:, k, t:t + 1], 0),
                                                rows[k][:, t, :], None).then_inc(scattered, 16)

            for b in range(NB):
                dispatch(b)
            pool.wait_ge(scattered, 16 * 2 * TILES)

        @block.tensor
        def _(pe):
            pe.wait_ge(const_loaded, 16 * 7)

            def turn(t):
                if t >= 2:
                    pe.wait_ge(xnT_ready, t - 1)
                for h in range(2):
                    last = pe.transpose(turned_ps[:, t % 2, h * PAIR:(h + 1) * PAIR],
                                        best[:, t, h * HALF:(h + 1) * HALF], ident[0:PAIR, 0:PAIR])
                last.then_inc(turned, 1)

            def logits_of(t):
                b, i = divmod(t, BT)
                pe.wait_ge(xnT_ready, t + 1)
                if i == 0 and b >= 2:
                    pe.wait_ge(logits_ready, b - 1)
                for h in range(2):
                    mm = pe.matmul(logits_ps[:, b % 2, i * EXPERTS:(i + 1) * EXPERTS], xnT[:, t % 2, h, :],
                                   router_w[:, h, :], start=(h == 0), stop=(h == 1))
                mm.then_inc(logits_done, 1)

            def count(b):
                at = slice(b * BT, (b + 1) * BT)
                pe.wait_ge(either_ready, b + 1)
                pe.wait_ge(before_ready, (b + 1) * BT)
                if b >= 2:
                    pe.wait_ge(place_read, b - 1)
                pe.matmul(place_ps[:, b % 2, 0:BE], earlier[:, 0, :], either[:, at, :].rearrange("p t e -> p (t e)"),
                          start=True, stop=False)
                pe.matmul(place_ps[:, b % 2, 0:BE], earlier[:, 1, :], before[:, at, :].rearrange("p t e -> p (t e)"),
                          start=False, stop=True).then_inc(placed, 1)

            for b in range(NB):
                for t in range(b * BT, (b + 1) * BT):
                    turn(t)
                    if t > b * BT:
                        logits_of(t - 1)
                logits_of((b + 1) * BT - 1)
                count(b)
            pe.wait_ge(before_ready, TILES + 1)
            pe.matmul(count_ps[:, 0:EXPERTS], earlier[:, 1, :], before[:, TILES, :], start=True, stop=True
                      ).then_inc(counted, 1)

        @block.scalar
        def _(act):
            def ratio_of(b):
                at = slice(b * BT, (b + 1) * BT)
                act.wait_ge(gap_ready, b + 1)
                act.activation(ratio[:, at], gap[:, at], ACT.Exp).then_inc(ratio_ready, 1)

            for b in range(NB):
                for t in range(b * BT, (b + 1) * BT):
                    act.wait_ge(turned, t + 1)
                    if t >= 2:
                        act.wait_ge(logits_done, t - 1)
                    act.activation(xnT[:, t % 2], turned_ps[:, t % 2, 0:2 * PAIR].rearrange("p (h n) -> p h n", h=2),
                                   ACT.Copy).then_inc(xnT_ready, 1)
                    act.activation(second[:, t, 0:D], best[:, t, 0:D], ACT.Copy).then_inc(doubled, 1)
                ratio_of(b)

        @block.vector
        def _(dve):
            steps = 0

            def chained(instruction):
                nonlocal steps
                steps += 1
                instruction.then_inc(step_done, 1)
                dve.wait_ge(step_done, steps)

            def route(b):
                tiles = range(b * BT, (b + 1) * BT)
                at = slice(b * BT, (b + 1) * BT)
                dve.wait_ge(logits_done, (b + 1) * BT)
                dve.tensor_copy(logits[:, at, :], logits_ps[:, b % 2, 0:BE].rearrange("p (t e) -> p t e", e=EXPERTS)
                                ).then_inc(logits_ready, 1)
                dve.wait_ge(logits_ready, b + 1)
                for t in tiles:
                    s = dve.max(top[:, t, :], logits[:, t, :])
                chained(s)
                dve.tensor_tensor(gap[:, at], top[:, at, 1], top[:, at, 0], ALU.subtract).then_inc(gap_ready, 1)
                for t in tiles:
                    s = dve.max_index(top_at[:, t, :], top[:, t, :], logits[:, t, :])
                chained(s)
                chained(dve.tensor_copy(top_atf[:, at], top_at[:, at]))
                for k in range(2):
                    s = dve.tensor_tensor(picked[:, k], number[:].unsqueeze(1).to_broadcast([PAIR, BT, EXPERTS]),
                                          top_atf[:, at, k:k + 1].to_broadcast([PAIR, BT, EXPERTS]), ALU.is_equal)
                chained(s)
                dve.tensor_tensor(either[:, at], picked[:, 0], picked[:, 1], ALU.add).then_inc(either_ready, 1)
                dve.wait_ge(either_ready, b + 1)
                for t in tiles:
                    dve.tensor_tensor(before[:, t + 1, :], before[:, t, :], either[:, t, :], ALU.add
                                      ).then_inc(before_ready, 1)
                    dve.wait_ge(before_ready, t + 2)
                dve.wait_ge(ratio_ready, b + 1)
                chained(dve.tensor_scalar(one_plus[:, at], ratio[:, at], 1.0, None, ALU.add))
                chained(dve.reciprocal(best[:, at, D + 1], one_plus[:, at]))
                dve.tensor_tensor(second[:, at, D + 1], best[:, at, D + 1], ratio[:, at], ALU.mult
                                  ).then_inc(shares_set, 1)
                dve.wait_ge(placed, b + 1)
                dve.tensor_tensor(place[:], place_ps[:, b % 2, 0:BE].rearrange("p (t e) -> p t e", e=EXPERTS),
                                  region_at[:], ALU.add).then_inc(place_read, 1)
                dve.wait_ge(place_read, b + 1)
                for k in range(2):
                    s = dve.tensor_tensor(own_place[:, k], picked[:, k], place[:], ALU.mult)
                chained(s)
                for k in range(2):
                    s = dve.tensor_reduce(dest_f[:, k], own_place[:, k], AX_X, ALU.add)
                chained(s)
                dve.tensor_copy(dest[:, :, at], dest_f[:]).then_inc(dest_ready, 1)

            dve.memset(before[:, 0, :], 0.0).then_inc(before_ready, 1)
            dve.wait_ge(before_ready, 1)
            dve.wait_ge(consts_set, 3)
            dve.wait_ge(const_loaded, 16 * 7)
            dve.tensor_copy(pad_rows[:, D:D + 1].bitcast(I32), pad_no[:]).then_inc(pads_set, 1)
            for k in range(2):
                s = dve.tensor_copy(rows[k][:, :, D].bitcast(I32), token_no[:])
            s.then_inc(numbers_set, 1)
            for b in range(NB):
                route(b)

            dve.wait_ge(counted, 1)
            chained(dve.tensor_copy(counts[:], count_ps[0:1, 0:EXPERTS]))
            chained(dve.tensor_tensor(pad_at_f[:], counts[:], region_at[0:1, 0, :], ALU.add))
            dve.tensor_copy(pad_at[:], pad_at_f[:]).then_inc(pad_at_ready, 1)
            chained(dve.tensor_scalar(counts[:], counts[:], float(SLOT - 1), None, ALU.add))
            chained(dve.tensor_copy(counts_i[:], counts[:]))
            chained(dve.tensor_scalar(blocks_i[:], counts_i[:], SLOT.bit_length() - 1, None, ALU.logical_shift_right))
            chained(dve.tensor_copy(ends[:], blocks_i[:]))
            for e in range(1, EXPERTS):
                chained(dve.tensor_tensor(ends[:, e:e + 1], ends[:, e:e + 1], ends[:, e - 1:e], ALU.add))
            every = [1, SLOTS, EXPERTS]
            chained(dve.tensor_tensor(passed[:], ends[:].unsqueeze(1).to_broadcast(every),
                                      slot_no[:].unsqueeze(2).to_broadcast(every), ALU.is_le))
            dve.tensor_reduce(slot_expert[:], passed[:], AX_X, ALU.add)
            chained(dve.tensor_tensor(passed_end[:], passed[:], ends[:].unsqueeze(1).to_broadcast(every), ALU.mult))
            dve.tensor_reduce(slot_begin[:], passed_end[:], AX_X, ALU.max)
            chained(dve.tensor_scalar(table[:, 1, :], slot_expert[:], float(EXPERTS - 1), None, ALU.min))
            chained(dve.tensor_tensor(in_expert[:], slot_no[:], slot_begin[:], ALU.subtract))
            dve.tensor_scalar(region_row[:], slot_expert[:], float(REGION), None, ALU.mult)
            chained(dve.tensor_scalar(in_expert[:], in_expert[:], float(SLOT), None, ALU.mult))
            chained(dve.tensor_tensor(slot_row[:], in_expert[:], region_row[:], ALU.add))
            chained(dve.tensor_scalar(table[:, 0, :], slot_row[:], float(SPARE), None, ALU.min))
            dve.memset(table[:, 2, 0:2], 1.0)
            chained(dve.tensor_tensor(table[:, 2, 2:SLOTS], table[:, 1, 2:SLOTS], table[:, 1, 0:SLOTS - 2],
                                      ALU.not_equal))
            chained(dve.tensor_copy(slots[:], table[:]))




def expert_stage(nc, io, slots, wait_carrier):
    FB = F // 128
    AHEAD = 8
    LEAD = AHEAD // 2
    ROUNDS = SLOTS // AHEAD
    HB = FB // 2

    with ExitStack() as ctx:
        def sb(name, shape, dt=F32):
            return ctx.enter_context(nc.sbuf_tensor("moe_sb_" + name, shape, dt))

        def ps(name, shape):
            return ctx.enter_context(nc.psum_tensor("moe_ps_" + name, shape, F32))

        def sem(name):
            return ctx.enter_context(nc.semaphore("moe_" + name))

        ident = sb("ident", [128, 128])
        up_w = sb("up_w", [HALF, 2, 2, F])
        up_b = sb("up_b", [128, 2, FB])
        down = sb("down", [128, 2, (FB + 1) * D])
        x = sb("x", [SLOT, AHEAD, ROW])
        xT = sb("xT", [HALF, 2, 2, SLOT])
        hidden = sb("hidden", [128, 2, FB, SLOT])
        biased = sb("biased", [SLOT, 2, D])
        result = sb("result", [SLOT, 2, D])
        turned_ps = ps("turned_ps", [HALF, 2, 512])
        up_ps = ps("up_ps", [128, 4, 512])
        down_ps = ps("down_ps", [SLOT, 2, 512])

        ident_loaded = sem("ident_loaded")
        rows_loaded = [sem("rows_loaded_%d" % i) for i in range(AHEAD)]
        up_loaded = [sem("up_loaded_even"), sem("up_loaded_odd")]
        down_loaded = [sem("down_loaded_even"), sem("down_loaded_odd")]
        turned = sem("turned")
        xT_ready = sem("xT_ready")
        up_done = sem("up_done")
        hidden_ready = sem("hidden_ready")
        down_done = sem("down_done")
        bias_added = sem("bias_added")
        result_ready = sem("result_ready")
        added = sem("added")

        def over_slots(eng, body):
            for i in range(AHEAD):
                body(i, i, 0)
            with eng.Fori(1, ROUNDS) as k:
                for i in range(AHEAD):
                    body(k * AHEAD + i, i, k)

        def use_of_pair(i, k):
            return k * (AHEAD // 2) + (i // 2 + 1)

        block = ctx.enter_context(nc.Block())

        @block.sync
        def _(sp):
            sp.dma_start(ident[:], io["ident"]).then_inc(ident_loaded, 16)

            def load_rows(s, i):
                row = sp.value_load(slots[0:1, 0, bass.ds(s, 1)], min_val=0, max_val=SPARE)
                if reached(s, AHEAD):
                    sp.wait_ge(added, (s - (AHEAD - 1)) * 16)
                    sp.sem_inc(wait_carrier, 1)
                sp.dma_start(x[:, i, :], io["dispatch"][bass.ds(row, SLOT), :]).then_inc(rows_loaded[i], 16)

            def weights_of(s):
                expert = sp.value_load(slots[0:1, 1, bass.ds(s, 1)], min_val=0, max_val=EXPERTS - 1)
                changed = sp.value_load(slots[0:1, 2, bass.ds(s, 1)], min_val=0, max_val=1)
                return bass.ds(expert, 1), changed

            def load_up(s, par):
                expert, changed = weights_of(s)
                if reached(s, 2):
                    sp.wait_ge(up_done, (s - 1) * 2)
                    sp.sem_inc(wait_carrier, 1)
                    sp.wait_ge(hidden_ready, (s - 1) * FB)
                    sp.sem_inc(wait_carrier, 1)
                sp.dma_start(up_w[:, par].rearrange("p h f -> p (h f)"),
                             io["up_w"][expert].rearrange("e p f -> p (e f)"), cond=changed
                             ).then_inc(up_loaded[par], 16)
                sp.dma_start(up_b[:, par], io["up_b"][expert].rearrange("e p f -> p (e f)"), cond=changed
                             ).then_inc(up_loaded[par], 16)

            def load_down(s, par):
                expert, changed = weights_of(s)
                if reached(s, 2):
                    sp.wait_ge(bias_added, s - 1)
                    sp.sem_inc(wait_carrier, 1)
                sp.dma_start(down[:, par], io["down_w"][expert].rearrange("e p f -> p (e f)"), cond=changed
                             ).then_inc(down_loaded[par], 16)

            def load(s, i):
                if not (isinstance(s, int) and s + 1 >= SLOTS):
                    load_up(s + 1, (i + 1) % 2)
                load_down(s, i % 2)
                if not (isinstance(s, int) and s + LEAD >= SLOTS):
                    load_rows(s + LEAD, (i + LEAD) % AHEAD)

            load_rows(0, 0)
            load_up(0, 0)
            for s in range(1, LEAD):
                load_rows(s, s)
            for i in range(AHEAD):
                load(i, i)
            with sp.Fori(1, ROUNDS - 1) as k:
                for i in range(AHEAD):
                    load(k * AHEAD + i, i)
            for i in range(AHEAD):
                load(SLOTS - AHEAD + i, i)

        @block.gpsimd
        def _(pool):
            def add(s, i, k):
                pool.wait_ge(result_ready, s + 1)
                pool.sem_inc(wait_carrier, 1)
                if reached(s, 1):
                    pool.wait_ge(added, s * 16)
                    pool.sem_inc(wait_carrier, 1)
                pool.indirect_dma_start(io["out"], bass.IndirectOffsetOnAxis(x[:, i, D:D + 1].bitcast(U32), 0),
                                        result[:, i % 2, :], None, compute_op=ALU.add).then_inc(added, 16)

            over_slots(pool, add)
            pool.wait_ge(added, SLOTS * 16)

        @block.tensor
        def _(pe):
            def turn(s, i, k):
                pe.wait_ge(rows_loaded[i], (k + 1) * 16)
                if reached(s, 2):
                    pe.wait_ge(xT_ready, s - 1)
                for h in range(2):
                    last = pe.transpose(turned_ps[:, i % 2, h * SLOT:(h + 1) * SLOT],
                                        x[:, i, h * HALF:(h + 1) * HALF], ident[:])
                last.then_inc(turned, 1)

            def up(s, i, k):
                pe.wait_ge(up_loaded[i % 2], use_of_pair(i, k) * 32)
                pe.wait_ge(xT_ready, s + 1)
                for b in range(2):
                    if reached(s, 2):
                        pe.wait_ge(hidden_ready, (s - 2) * FB + (b + 1) * HB)
                    for m in range(b * HB, (b + 1) * HB):
                        for h in range(2):
                            mm = pe.matmul(up_ps[:, (i % 2) * 2 + b, (m - b * HB) * SLOT:(m - b * HB + 1) * SLOT],
                                           up_w[:, i % 2, h, m * 128:(m + 1) * 128], xT[:, i % 2, h, :],
                                           start=(h == 0), stop=(h == 1))
                    mm.then_inc(up_done, 1)

            def down_of(s, i, k):
                pe.wait_ge(down_loaded[i % 2], use_of_pair(i, k) * 16)
                pe.wait_ge(hidden_ready, (s + 1) * FB)
                if reached(s, 2):
                    pe.wait_ge(bias_added, s - 1)
                for m in range(FB):
                    mm = pe.matmul(down_ps[:, i % 2, 0:D], hidden[:, i % 2, m, :],
                                   down[:, i % 2, m * D:(m + 1) * D], start=(m == 0), stop=(m == FB - 1))
                mm.then_inc(down_done, 1)

            def step(s, i, k):
                up(s, i, k)
                if i + 1 < AHEAD:
                    turn(s + 1, i + 1, k)
                elif not (isinstance(s, int) and s + 1 == SLOTS):
                    turn(s + 1, 0, k + 1)
                if i > 0:
                    down_of(s - 1, i - 1, k)
                elif reached(s, 1):
                    down_of(s - 1, AHEAD - 1, k - 1)

            pe.wait_ge(ident_loaded, 16)
            turn(0, 0, 0)
            for i in range(AHEAD):
                step(i, i, 0)
            with pe.Fori(1, ROUNDS - 1) as k:
                for i in range(AHEAD):
                    step(k * AHEAD + i, i, k)
            for i in range(AHEAD):
                step(SLOTS - AHEAD + i, i, ROUNDS - 1)
            down_of(SLOTS - 1, AHEAD - 1, ROUNDS - 1)

        @block.scalar
        def _(act):
            def gelu(s, i, k):
                act.wait_ge(up_loaded[i % 2], use_of_pair(i, k) * 32)
                if reached(s, 2):
                    act.wait_ge(down_done, s - 1)
                for m in range(FB):
                    if m % HB == 0:
                        act.wait_ge(up_done, s * 2 + (m // HB + 1))
                    act.activation(hidden[:, i % 2, m, :],
                                   up_ps[:, (i % 2) * 2 + m // HB, (m % HB) * SLOT:(m % HB + 1) * SLOT], ACT.Gelu,
                                   bias=up_b[:, i % 2, m:m + 1]).then_inc(hidden_ready, 1)

            over_slots(act, gelu)

        @block.vector
        def _(dve):
            def take_turned(s, i, k):
                dve.wait_ge(turned, s + 1)
                if reached(s, 2):
                    dve.wait_ge(up_done, (s - 1) * 2)
                dve.tensor_copy(xT[:, i % 2], turned_ps[:, i % 2, 0:2 * SLOT].rearrange("p (h n) -> p h n", h=2)
                                ).then_inc(xT_ready, 1)

            def weigh(s, i, k):
                dve.wait_ge(down_loaded[i % 2], use_of_pair(i, k) * 16)
                dve.wait_ge(down_done, s + 1)
                if reached(s, 2):
                    dve.wait_ge(result_ready, s - 1)
                dve.tensor_tensor(biased[:, i % 2], down_ps[:, i % 2, 0:D], down[:, i % 2, FB * D:(FB + 1) * D],
                                  ALU.add).then_inc(bias_added, 1)
                dve.wait_ge(bias_added, s + 1)
                dve.wait_ge(rows_loaded[i], (k + 1) * 16)
                if reached(s, 2):
                    dve.wait_ge(added, (s - 1) * 16)
                dve.tensor_scalar(result[:, i % 2], biased[:, i % 2], x[:, i, D + 1:D + 2], None, ALU.mult
                                  ).then_inc(result_ready, 1)

            def step(s, i, k):
                if i + 1 < AHEAD:
                    take_turned(s + 1, i + 1, k)
                elif not (isinstance(s, int) and s + 1 == SLOTS):
                    take_turned(s + 1, 0, k + 1)
                if i > 0:
                    weigh(s - 1, i - 1, k)
                elif reached(s, 1):
                    weigh(s - 1, AHEAD - 1, k - 1)

            take_turned(0, 0, 0)
            for i in range(AHEAD):
                step(i, i, 0)
            with dve.Fori(1, ROUNDS - 1) as k:
                for i in range(AHEAD):
                    step(k * AHEAD + i, i, k)
            for i in range(AHEAD):
                step(SLOTS - AHEAD + i, i, ROUNDS - 1)
            weigh(SLOTS - 1, AHEAD - 1, ROUNDS - 1)




def build_program(nc, io):
    with nc.semaphore("wait_carrier") as wait_carrier:
        image_stage(nc, io, wait_carrier)
        text_stage(nc, io, wait_carrier)
        with nc.sbuf_tensor("slots", [1, 3, SLOTS], I32) as slots:
            with nc.sbuf_tensor("rows", [PAIR, TILES, ROW], F32) as rows:
                attention_stage(nc, io, rows, wait_carrier)
                routing_stage(nc, io, rows, slots)
            expert_stage(nc, io, slots, wait_carrier)




def _layouts(a):
    import numpy as np
    P = 128
    out = {}
    out["txt_idx"] = a["x_txt"].reshape(-1, P).T
    out["txt_pos"] = np.tile(a["L0_txt_pos_encoding"][0, :TEXT_LEN], (P // TEXT_LEN, 1))
    out["embedding"] = a["L0_txt_embedding"]
    out["ident"] = np.eye(P, dtype=np.float32)
    out["txt_final_g"] = np.broadcast_to(a["L0_txt_final_g"], (P, D))
    out["txt_final_b"] = np.broadcast_to(a["L0_txt_final_b"], (P, D))
    gb = np.stack([a["L0_txt_ln_g"], a["L0_txt_ln_b"]], 1)
    out["txt_ln_gb"] = gb.reshape(LAYERS, 2, 2, HALF).transpose(3, 0, 1, 2)
    out["txt_taps"] = a["L0_txt_conv_w"].reshape(LAYERS, DI_CHUNKS, HALF, 3).transpose(2, 0, 1, 3)
    out["txt_dt_b"] = a["L0_txt_dt_b"].reshape(LAYERS, DI_CHUNKS, HALF).transpose(2, 0, 1)
    out["txt_in_w"] = a["L0_txt_in_w"].reshape(LAYERS, 2 * DI, 2, HALF).transpose(0, 3, 2, 1)
    out["txt_dt_w"] = a["L0_txt_dt_w"].reshape(LAYERS, DI, DI_CHUNKS, HALF).transpose(0, 3, 2, 1)
    ow = a["L0_txt_out_w"].reshape(LAYERS, D, DI_CHUNKS, HALF).transpose(0, 3, 2, 1)
    ls = np.broadcast_to(a["L0_txt_layer_scale"][:, None, None, :], (LAYERS, HALF, 1, D))
    out["txt_out_w"] = np.concatenate([ow, ls], 2)
    def blocks(w):
        w = w.reshape(-1, 3, HEADS // 2, 2, D)
        tail = w[..., 128:].reshape(w.shape[0], 3, HEADS // 2, 1, 128)
        return np.concatenate([w[..., :128], tail], 3).reshape(w.shape[0], -1, 128)
    out["qkv_w"] = blocks(a["L0_attn_W_qkv"]).reshape(2, HALF, -1, 128).transpose(1, 0, 2, 3)
    out["qkv_b"] = blocks(a["L0_attn_b_qkv"][None])[0].T
    pw = a["L0_attn_W_proj"].reshape(HEADS, D, D)
    out["proj_w"] = np.concatenate([pw[:, :128], pw[:, 128:].reshape(HEADS // 2, 128, D)]).transpose(1, 0, 2)
    out["proj_b"] = np.broadcast_to(a["L0_attn_b_proj"], (PAIR, D))
    first = np.repeat([1.0, 0.0], SEQ)
    out["mask"] = np.stack([np.stack([first, 1 - first]), np.stack([1 - first, first]) * -1e30], 1).astype(np.float32)
    f = np.float32
    xp = np.pad(a["x"], ((0, 0), (0, 0), (1, 1), (1, 1)))
    out["img_x"] = xp.reshape(8, 8 * C0, -1).transpose(1, 0, 2)
    w0 = np.zeros((3, 8, C0, 3, 8, C1), f)
    for b in range(8):
        w0[:, b, :, :, b, :] = a["L0_tok_w0"].transpose(2, 1, 3, 0)
    out["img_w0"] = w0.reshape(72, 3, 96)
    out["img_sb0"] = np.tile(np.stack([a["L0_tok_s0"], a["L0_tok_b0"]], 1), (8, 1))
    pw = a["L0_tok_wpw"].reshape(GRID, GRID, C1, C1).transpose(0, 3, 1, 2)
    pwd = np.zeros((GRID, 8, C1, GRID, 8, C1), f)
    for b in range(8):
        pwd[:, b, :, :, b, :] = pw
    spw = np.broadcast_to(a["L0_tok_spw"].reshape(GRID, 1, GRID, 1, C1), (GRID, 96, GRID, 8, C1))
    def by_channel(v):
        return np.tile(v.reshape(GRID, GRID, C1, -1).transpose(0, 2, 1, 3), (1, 8, 1, 1)).reshape(GRID, 96, -1)
    out["img_par"] = np.concatenate([pwd.reshape(GRID, 96, -1), spw.reshape(GRID, 96, -1), by_channel(a["L0_tok_wdw"]),
                                     by_channel(a["L0_tok_sdw"]), by_channel(a["L0_tok_bdw"]),
                                     by_channel(a["L0_tok_bpw"])], 2)
    w1 = a["L0_tok_w1"].transpose(1, 2, 3, 0).reshape(2, 96, C2).transpose(1, 0, 2)
    out["img_w1"] = np.pad(w1, ((0, 0), (0, 0), (0, 64 - C2)))
    def padded_pair(s, b):
        return np.tile(np.pad(np.stack([s, b], 1), ((0, 64 - C2), (0, 0))), (2, 1))
    out["img_sb1"] = padded_pair(a["L0_tok_s1"], a["L0_tok_b1"])
    out["img_sb2"] = padded_pair(a["L0_tok_s2"], a["L0_tok_b2"])
    w2 = np.zeros((2, 64, 4, 2, 64), f)
    for k in range(2):
        w2[k, :C2, :, k, :C2] = a["L0_tok_w2"].transpose(1, 2, 3, 0).reshape(C2, 4, C2)
    out["img_w2"] = w2.reshape(128, 4, 128)
    w3 = np.pad(a["L0_tok_w3"].transpose(1, 2, 3, 0).reshape(C2, 4, D), ((0, 64 - C2), (0, 0), (0, 0)))
    out["img_w3"] = np.tile(w3, (2, 1, 1))
    out["img_sb3"] = np.broadcast_to(np.stack([a["L0_tok_s3"], a["L0_tok_b3"]])[None], (128, 2, D))
    out["router_w"] = a["L0_ffn_Wr"].reshape(EXPERTS, 2, HALF).transpose(2, 1, 0)
    out["up_w"] = a["L0_ffn_Wi"].reshape(EXPERTS, F, 2, HALF).transpose(0, 3, 2, 1).reshape(EXPERTS, HALF, 2 * F)
    down_w = a["L0_ffn_Wo"].reshape(EXPERTS, D, F // P, P).transpose(0, 3, 2, 1).reshape(EXPERTS, P, -1)
    down_b = np.broadcast_to(a["L0_ffn_bo"][:, None, :], (EXPERTS, P, D))
    out["up_b"] = a["L0_ffn_bi"].reshape(EXPERTS, F // P, P).transpose(0, 2, 1)
    out["down_w"] = np.concatenate([down_w, down_b], 2)
    out["earlier"] = np.stack([np.triu(np.ones((PAIR, PAIR)), 1), np.ones((PAIR, PAIR))], 1).astype(np.float32)
    out["token_no"] = np.arange(TOKENS, dtype=np.int32).reshape(TILES, PAIR).T
    out["pad_no"] = (TOKENS + np.arange(SLOT, dtype=np.int32))[:, None]
    starts = np.arange(EXPERTS, dtype=np.float32) * REGION
    out["region_at"] = np.broadcast_to(starts, (PAIR, ROUTE_TILES, EXPERTS))
    out["slot_no"] = np.arange(SLOTS, dtype=np.float32)[None]
    return {name: np.ascontiguousarray(v) for name, v in out.items()}


def kernel(**inputs):
    import numpy as np
    import concourse.bacc as bacc
    from concourse.bass_utils import run_bass_kernel_spmd

    nc = bacc.Bacc("TRN2", target_bir_lowering=False, num_devices=1)
    arrays = _layouts({name: np.asarray(v) for name, v in inputs.items()})
    io = {name: nc.dram_tensor("in_" + name, v.shape, mybir.dt.from_np(v.dtype), kind="ExternalInput").ap()
          for name, v in arrays.items()}
    io["out"] = nc.dram_tensor("out_dram", (TOKENS + SLOT, D), F32, kind="ExternalOutput").ap()
    io["h"] = nc.dram_tensor("h_dram", (TOKENS, D), F32).ap()
    io["img_taps"] = nc.dram_tensor("img_taps_dram", (2, 96, 3840), F32).ap()
    io["dispatch"] = nc.dram_tensor("dispatch_dram", (SPARE + SLOT, ROW), F32).ap()
    build_program(nc, io)
    r = run_bass_kernel_spmd(nc, [{"in_" + name: v for name, v in arrays.items()}], core_ids=[0])
    return r.results[0]["out_dram"][:TOKENS].reshape(BATCH, SEQ, D)
```
